# Optimizing a Trainium2 kernel written in Bass

```python
import numpy as np
import jax
import jax.numpy as jnp

def _softmax(x, axis=-1):
    return jax.nn.softmax(x, axis=axis)

def _gelu(x):
    return jax.nn.gelu(x, approximate=True)

def _silu(x):
    return jax.nn.silu(x)

def _sigmoid(x):
    return jax.nn.sigmoid(x)

def _layernorm(x, axis=-1, eps=1e-05):
    m = jnp.mean(x, axis=axis, keepdims=True)
    v = jnp.var(x, axis=axis, keepdims=True)
    return (x - m) / jnp.sqrt(v + eps)

def _scatter_add(tgt, idx, src, axis=0):
    return tgt.at[idx].add(src)

def _segment_sum(src, seg, n):
    return jax.ops.segment_sum(src, seg, n)
kernel_name = 'mk_decoder_preln_d2_seqx_r8_2bd516'

def setup_inputs(seed: int=0):
    np.random.seed(seed)
    _w = jnp.asarray

    def _rec_inputs():
        import jax
        import jax.numpy as jnp
        _rk = jax.random.key(seed)
        x = 7.22e-05 + 1 * jax.random.normal(jax.random.fold_in(_rk, 1), (16, 128, 128), jnp.float32)
        _lenS = 128 - jax.random.randint(jax.random.fold_in(_rk, 7), (16,), 0, max(1, 128 // 4) + 1, jnp.int32)
        _lenS2 = 128 - jax.random.randint(jax.random.fold_in(_rk, 8), (16,), 0, max(1, 128 // 4) + 1, jnp.int32)
        _ctx_1024P = jax.random.normal(jax.random.fold_in(_rk, 11), (16, 16, 128), jnp.float32)
        _ctx_1024c = jax.random.dirichlet(jax.random.fold_in(_rk, 511), 0.3 * jnp.ones((16,), jnp.float32), (16, 128))
        _ctx_1024t = jnp.einsum('bsk,bkd->bsd', _ctx_1024c, _ctx_1024P)
        _ctx_1024t = _ctx_1024t * jax.lax.rsqrt(jnp.mean(jnp.square(_ctx_1024t)) + 1e-12) * 0.953939
        ctx_1024 = 4.13588e-05 + 0.999923 * (_ctx_1024t + 0.3 * jax.random.normal(jax.random.fold_in(_rk, 611), (16, 128, 128), jnp.float32))
        _validS = jnp.arange(128)[None, :] < _lenS[:, None]
        _validS2 = jnp.arange(128)[None, :] < _lenS2[:, None]
        _causal = jnp.tril(jnp.ones((128, 128), dtype=bool))
        mask_Bx1xS2_if1 = jnp.where(jnp.ones((16, 1, 128), dtype=bool), 1, 0).astype(jnp.int32)
        mask_Bx1xSxS2_if1 = jnp.where(jnp.ones((16, 1, 128, 128), dtype=bool), 1, 0).astype(jnp.int32)
        return (x, ctx_1024, mask_Bx1xS2_if1, mask_Bx1xSxS2_if1)
    x, ctx_1024, mask_Bx1xS2_if1, mask_Bx1xSxS2_if1 = _rec_inputs()

    def _L0_attn_setup():
        import jax, jax.numpy as jnp
        import numpy as np
        D = 128
        FF = 512
        EPS = 1e-06

        def _linear(x, w, b):
            return jnp.einsum('bld,fd->blf', x, w) + b

        def _rmsnorm(x, g):
            xf = x.astype(jnp.float32)
            out = xf * jax.lax.rsqrt(jnp.mean(xf * xf, axis=-1, keepdims=True) + EPS)
            return out.astype(x.dtype) * g

        def _silu(x):
            return x * jax.nn.sigmoid(x)
        key = jax.random.key(seed)
        ks = jax.random.split(key, 20)
        sd = 1.0 / np.sqrt(D)
        sf = 1.0 / np.sqrt(FF)
        inp = {'x': jax.random.normal(ks[0], (4, 512, D), jnp.float32), 'w_ln_z': jax.random.uniform(ks[1], (D, D), jnp.float32, -sd, sd), 'b_ln_z': jax.random.uniform(ks[2], (D,), jnp.float32, -sd, sd), 'w_dt': jax.random.uniform(ks[3], (D, D), jnp.float32, -sd, sd), 'b_dt': jax.random.uniform(ks[4], (D,), jnp.float32, -sd, sd), 'w_y': jax.random.uniform(ks[5], (D, D), jnp.float32, -sd, sd), 'b_y': jax.random.uniform(ks[6], (D,), jnp.float32, -sd, sd), 'w_yact': jax.random.uniform(ks[7], (D, D), jnp.float32, -sd, sd), 'b_yact': jax.random.uniform(ks[8], (D,), jnp.float32, -sd, sd), 'h0': jax.random.normal(ks[9], (D,), jnp.float32), 'w_fc': jax.random.uniform(ks[10], (FF, D), jnp.float32, -sd, sd), 'b_fc': jax.random.uniform(ks[11], (FF,), jnp.float32, -sd, sd), 'w_fcact': jax.random.uniform(ks[12], (FF, D), jnp.float32, -sd, sd), 'b_fcact': jax.random.uniform(ks[13], (FF,), jnp.float32, -sd, sd), 'w_out': jax.random.uniform(ks[14], (D, FF), jnp.float32, -sf, sf), 'b_out': jax.random.uniform(ks[15], (D,), jnp.float32, -sf, sf), 'g_sio': jnp.ones((D,), jnp.float32), 'g_ffn': jnp.ones((D,), jnp.float32)}
        return inp
    _L0_attn_all = _L0_attn_setup()
    _L0_attn_in = {k: v for k, v in _L0_attn_all.items() if k in ('w_ln_z', 'b_ln_z', 'w_dt', 'b_dt', 'w_y', 'b_y', 'w_yact', 'b_yact', 'h0', 'w_fc', 'b_fc', 'w_fcact', 'b_fcact', 'w_out', 'b_out', 'g_sio', 'g_ffn')}
    del _L0_attn_all

    def _L0_xattn_setup():
        import jax, jax.numpy as jnp
        import numpy as np
        HEADS = 16
        D_MODEL = 128
        D_K = D_MODEL // HEADS
        ROPE_BASE = 10000.0

        def _rope_cache(seq_len, dim):
            theta = 1.0 / ROPE_BASE ** (jnp.arange(0, dim, 2, dtype=jnp.float32) / dim)
            idx_theta = jnp.arange(seq_len, dtype=jnp.float32)[:, None] * theta[None, :]
            return (jnp.cos(idx_theta), jnp.sin(idx_theta))

        def _apply_rope(x, cos, sin):
            b, s, h, d = x.shape
            xs = x.reshape(b, s, h, d // 2, 2)
            x0, x1 = (xs[..., 0], xs[..., 1])
            c = cos[None, :, None, :]
            sn = sin[None, :, None, :]
            out = jnp.stack([x0 * c - x1 * sn, x1 * c + x0 * sn], axis=-1)
            return out.reshape(b, s, h, d)
        key = jax.random.key(seed)
        ks = jax.random.split(key, 12)
        b, s = (4, 256)
        scale = 1.0 / np.sqrt(D_MODEL)
        inp = {'q': jax.random.normal(ks[0], (b, s, D_MODEL), jnp.float32), 'k': jax.random.normal(ks[1], (b, s, D_MODEL), jnp.float32), 'v': jax.random.normal(ks[2], (b, s, D_MODEL), jnp.float32), 'mask': jnp.ones((b, 1, s), jnp.int32), 'Wq': jax.random.normal(ks[3], (D_MODEL, D_MODEL), jnp.float32) * scale, 'bq': jnp.zeros((D_MODEL,), jnp.float32), 'Wk': jax.random.normal(ks[4], (D_MODEL, D_MODEL), jnp.float32) * scale, 'bk': jnp.zeros((D_MODEL,), jnp.float32), 'Wv': jax.random.normal(ks[5], (D_MODEL, D_MODEL), jnp.float32) * scale, 'bv': jnp.zeros((D_MODEL,), jnp.float32), 'Wo': jax.random.normal(ks[6], (D_MODEL, D_MODEL), jnp.float32) * scale, 'bo': jnp.zeros((D_MODEL,), jnp.float32)}
        return inp
    _L0_xattn_all = _L0_xattn_setup()
    _L0_xattn_in = {k: v for k, v in _L0_xattn_all.items() if k in ('Wq', 'bq', 'Wk', 'bk', 'Wv', 'bv', 'Wo', 'bo')}
    del _L0_xattn_all

    def _L0_ffn_setup():
        import jax, jax.numpy as jnp
        import numpy as np
        B, S, H = (2, 256, 128)
        E_ROUTED = 8
        TOP_K = 2
        I = 256
        key = jax.random.key(seed)
        ks = jax.random.split(key, 9)
        s = 0.02
        return {'x': jax.random.normal(ks[0], (B, S, H), dtype=jnp.float32), 'shared_gate': jax.random.normal(ks[1], (I, H), dtype=jnp.float32) * s, 'shared_up': jax.random.normal(ks[2], (I, H), dtype=jnp.float32) * s, 'shared_down': jax.random.normal(ks[3], (H, I), dtype=jnp.float32) * s, 'gate_w': jax.random.normal(ks[4], (E_ROUTED, H, I), dtype=jnp.float32) * s, 'up_w': jax.random.normal(ks[5], (E_ROUTED, H, I), dtype=jnp.float32) * s, 'down_w': jax.random.normal(ks[6], (E_ROUTED, I, H), dtype=jnp.float32) * s, 'router_w': jax.random.normal(ks[7], (E_ROUTED, H), dtype=jnp.float32) * s, 'routing_bias': jnp.zeros((E_ROUTED,), dtype=jnp.float32)}
    _L0_ffn_all = _L0_ffn_setup()
    _L0_ffn_in = {k: v for k, v in _L0_ffn_all.items() if k in ('shared_gate', 'shared_up', 'shared_down', 'gate_w', 'up_w', 'down_w', 'router_w', 'routing_bias')}
    del _L0_ffn_all

    def _L1_attn_setup():
        import jax, jax.numpy as jnp
        import numpy as np
        import math
        N_HEADS = 16
        FACTOR = 5
        key = jax.random.key(seed)
        ks = jax.random.split(key, 9)
        B, T, D = (2, 256, 128)
        s = D ** (-0.5)
        return {'x': jax.random.normal(ks[0], (B, T, D), dtype=jnp.float32), 'Wq': jax.random.normal(ks[1], (D, D), dtype=jnp.float32) * s, 'bq': jnp.zeros((D,), dtype=jnp.float32), 'Wk': jax.random.normal(ks[2], (D, D), dtype=jnp.float32) * s, 'bk': jnp.zeros((D,), dtype=jnp.float32), 'Wv': jax.random.normal(ks[3], (D, D), dtype=jnp.float32) * s, 'bv': jnp.zeros((D,), dtype=jnp.float32), 'Wo': jax.random.normal(ks[4], (D, D), dtype=jnp.float32) * s, 'bo': jnp.zeros((D,), dtype=jnp.float32)}
    _L1_attn_all = _L1_attn_setup()
    _L1_attn_in = {k: v for k, v in _L1_attn_all.items() if k in ('Wq', 'bq', 'Wk', 'bk', 'Wv', 'bv', 'Wo', 'bo')}
    del _L1_attn_all

    def _L1_xattn_setup():
        import jax, jax.numpy as jnp
        import numpy as np
        EMBED = 128
        HEADS = 16
        HEAD_DIM = EMBED // HEADS
        key = jax.random.key(seed)
        ks = jax.random.split(key, 8)
        N, S = (4, 256)
        scale = 1.0 / np.sqrt(EMBED)
        return {'values': jax.random.normal(ks[0], (N, S, EMBED), jnp.float32), 'keys': jax.random.normal(ks[1], (N, S, EMBED), jnp.float32), 'query': jax.random.normal(ks[2], (N, S, EMBED), jnp.float32), 'mask': jnp.ones((N, 1, S, S), jnp.int32), 'Wv': jax.random.normal(ks[3], (EMBED, EMBED), jnp.float32) * scale, 'Wk': jax.random.normal(ks[4], (EMBED, EMBED), jnp.float32) * scale, 'Wq': jax.random.normal(ks[5], (EMBED, EMBED), jnp.float32) * scale, 'Wo': jax.random.normal(ks[6], (EMBED, EMBED), jnp.float32) * scale, 'bo': jnp.zeros((EMBED,), jnp.float32)}
    _L1_xattn_all = _L1_xattn_setup()
    _L1_xattn_in = {k: v for k, v in _L1_xattn_all.items() if k in ('Wv', 'Wk', 'Wq', 'Wo', 'bo')}
    del _L1_xattn_all

    def _L1_ffn_setup():
        import jax, jax.numpy as jnp
        import numpy as np
        B, S, D, E, F = (4, 256, 128, 8, 512)
        MIN_CAPACITY = 4

        def _make_waff():
            g = D // E
            scale = E / D
            w = np.zeros((E, D), np.float32)
            for i in range(E):
                w[i, i * g:(i + 1) * g] = scale
            return jnp.asarray(w)
        key = jax.random.key(seed)
        ks = jax.random.split(key, 6)
        inputs = jax.random.normal(ks[0], (B, S, D), dtype=jnp.float32)
        W1 = jax.random.normal(ks[1], (E, D, F), dtype=jnp.float32) * (1.0 / np.sqrt(D))
        b1 = jnp.zeros((E, F), dtype=jnp.float32)
        W2 = jax.random.normal(ks[2], (E, F, D), dtype=jnp.float32) * (1.0 / np.sqrt(F))
        b2 = jnp.zeros((E, D), dtype=jnp.float32)
        return {'inputs': inputs, 'waff': _make_waff(), 'W1': W1, 'b1': b1, 'W2': W2, 'b2': b2, 'affinity_threshold': jnp.float32(0.5)}
    _L1_ffn_all = _L1_ffn_setup()
    _L1_ffn_in = {k: v for k, v in _L1_ffn_all.items() if k in ('waff', 'W1', 'b1', 'W2', 'b2', 'affinity_threshold')}
    del _L1_ffn_all
    return {'x': x, 'ctx_1024': ctx_1024, 'mask_Bx1xS2_if1': mask_Bx1xS2_if1, 'mask_Bx1xSxS2_if1': mask_Bx1xSxS2_if1, 'L0_attn_w_ln_z': _L0_attn_in['w_ln_z'], 'L0_attn_b_ln_z': _L0_attn_in['b_ln_z'], 'L0_attn_w_dt': _L0_attn_in['w_dt'], 'L0_attn_b_dt': _L0_attn_in['b_dt'], 'L0_attn_w_y': _L0_attn_in['w_y'], 'L0_attn_b_y': _L0_attn_in['b_y'], 'L0_attn_w_yact': _L0_attn_in['w_yact'], 'L0_attn_b_yact': _L0_attn_in['b_yact'], 'L0_attn_h0': _L0_attn_in['h0'], 'L0_attn_w_fc': _L0_attn_in['w_fc'], 'L0_attn_b_fc': _L0_attn_in['b_fc'], 'L0_attn_w_fcact': _L0_attn_in['w_fcact'], 'L0_attn_b_fcact': _L0_attn_in['b_fcact'], 'L0_attn_w_out': _L0_attn_in['w_out'], 'L0_attn_b_out': _L0_attn_in['b_out'], 'L0_attn_g_sio': _L0_attn_in['g_sio'], 'L0_attn_g_ffn': _L0_attn_in['g_ffn'], 'L0_xattn_Wq': _L0_xattn_in['Wq'], 'L0_xattn_bq': _L0_xattn_in['bq'], 'L0_xattn_Wk': _L0_xattn_in['Wk'], 'L0_xattn_bk': _L0_xattn_in['bk'], 'L0_xattn_Wv': _L0_xattn_in['Wv'], 'L0_xattn_bv': _L0_xattn_in['bv'], 'L0_xattn_Wo': _L0_xattn_in['Wo'], 'L0_xattn_bo': _L0_xattn_in['bo'], 'L0_ffn_shared_gate': _L0_ffn_in['shared_gate'], 'L0_ffn_shared_up': _L0_ffn_in['shared_up'], 'L0_ffn_shared_down': _L0_ffn_in['shared_down'], 'L0_ffn_gate_w': _L0_ffn_in['gate_w'], 'L0_ffn_up_w': _L0_ffn_in['up_w'], 'L0_ffn_down_w': _L0_ffn_in['down_w'], 'L0_ffn_router_w': _L0_ffn_in['router_w'], 'L0_ffn_routing_bias': _L0_ffn_in['routing_bias'], 'L1_attn_Wq': _L1_attn_in['Wq'], 'L1_attn_bq': _L1_attn_in['bq'], 'L1_attn_Wk': _L1_attn_in['Wk'], 'L1_attn_bk': _L1_attn_in['bk'], 'L1_attn_Wv': _L1_attn_in['Wv'], 'L1_attn_bv': _L1_attn_in['bv'], 'L1_attn_Wo': _L1_attn_in['Wo'], 'L1_attn_bo': _L1_attn_in['bo'], 'L1_xattn_Wv': _L1_xattn_in['Wv'], 'L1_xattn_Wk': _L1_xattn_in['Wk'], 'L1_xattn_Wq': _L1_xattn_in['Wq'], 'L1_xattn_Wo': _L1_xattn_in['Wo'], 'L1_xattn_bo': _L1_xattn_in['bo'], 'L1_ffn_waff': _L1_ffn_in['waff'], 'L1_ffn_W1': _L1_ffn_in['W1'], 'L1_ffn_b1': _L1_ffn_in['b1'], 'L1_ffn_W2': _L1_ffn_in['W2'], 'L1_ffn_b2': _L1_ffn_in['b2'], 'L1_ffn_affinity_threshold': _L1_ffn_in['affinity_threshold']}

def reference(x, ctx_1024, mask_Bx1xS2_if1, mask_Bx1xSxS2_if1, L0_attn_w_ln_z, L0_attn_b_ln_z, L0_attn_w_dt, L0_attn_b_dt, L0_attn_w_y, L0_attn_b_y, L0_attn_w_yact, L0_attn_b_yact, L0_attn_h0, L0_attn_w_fc, L0_attn_b_fc, L0_attn_w_fcact, L0_attn_b_fcact, L0_attn_w_out, L0_attn_b_out, L0_attn_g_sio, L0_attn_g_ffn, L0_xattn_Wq, L0_xattn_bq, L0_xattn_Wk, L0_xattn_bk, L0_xattn_Wv, L0_xattn_bv, L0_xattn_Wo, L0_xattn_bo, L0_ffn_shared_gate, L0_ffn_shared_up, L0_ffn_shared_down, L0_ffn_gate_w, L0_ffn_up_w, L0_ffn_down_w, L0_ffn_router_w, L0_ffn_routing_bias, L1_attn_Wq, L1_attn_bq, L1_attn_Wk, L1_attn_bk, L1_attn_Wv, L1_attn_bv, L1_attn_Wo, L1_attn_bo, L1_xattn_Wv, L1_xattn_Wk, L1_xattn_Wq, L1_xattn_Wo, L1_xattn_bo, L1_ffn_waff, L1_ffn_W1, L1_ffn_b1, L1_ffn_W2, L1_ffn_b2, L1_ffn_affinity_threshold):
    import jax
    import jax.numpy as jnp

    def _L0_attn_ref(x, w_ln_z, b_ln_z, w_dt, b_dt, w_y, b_y, w_yact, b_yact, h0, w_fc, b_fc, w_fcact, b_fcact, w_out, b_out, g_sio, g_ffn):
        import jax, jax.numpy as jnp
        import numpy as np
        D = 128
        FF = 512
        EPS = 1e-06

        def _linear(x, w, b):
            return jnp.einsum('bld,fd->blf', x, w) + b

        def _rmsnorm(x, g):
            xf = x.astype(jnp.float32)
            out = xf * jax.lax.rsqrt(jnp.mean(xf * xf, axis=-1, keepdims=True) + EPS)
            return out.astype(x.dtype) * g

        def _silu(x):
            return x * jax.nn.sigmoid(x)
        xn = _rmsnorm(x, g_sio)
        ln_z = -jax.nn.softplus(-_linear(xn, w_ln_z, b_ln_z))
        dt = _linear(xn, w_dt, b_dt)
        ln_da = -jax.nn.softplus(-dt)
        ln_o_da = -jax.nn.softplus(dt)
        ln_o_da_cumsum = jnp.cumsum(ln_o_da, axis=1)
        lcse = jax.lax.cumlogsumexp(ln_z + ln_da - ln_o_da_cumsum, axis=1)
        h_inner = jnp.exp(lcse + ln_o_da_cumsum)
        h_cross = jnp.exp(ln_o_da_cumsum) * h0[None, None, :]
        h = h_inner + h_cross
        y = _linear(h, w_y, b_y) * _silu(_linear(xn, w_yact, b_yact))
        x = x + y
        xn2 = _rmsnorm(x, g_ffn)
        hid = _linear(xn2, w_fc, b_fc) * _silu(_linear(xn2, w_fcact, b_fcact))
        return x + _linear(hid, w_out, b_out)

    def _L0_xattn_ref(q, k, v, mask, Wq, bq, Wk, bk, Wv, bv, Wo, bo):
        import jax, jax.numpy as jnp
        import numpy as np
        HEADS = 16
        D_MODEL = 128
        D_K = D_MODEL // HEADS
        ROPE_BASE = 10000.0

        def _rope_cache(seq_len, dim):
            theta = 1.0 / ROPE_BASE ** (jnp.arange(0, dim, 2, dtype=jnp.float32) / dim)
            idx_theta = jnp.arange(seq_len, dtype=jnp.float32)[:, None] * theta[None, :]
            return (jnp.cos(idx_theta), jnp.sin(idx_theta))

        def _apply_rope(x, cos, sin):
            b, s, h, d = x.shape
            xs = x.reshape(b, s, h, d // 2, 2)
            x0, x1 = (xs[..., 0], xs[..., 1])
            c = cos[None, :, None, :]
            sn = sin[None, :, None, :]
            out = jnp.stack([x0 * c - x1 * sn, x1 * c + x0 * sn], axis=-1)
            return out.reshape(b, s, h, d)
        b, s, _ = q.shape
        qh = (q @ Wq + bq).reshape(b, s, HEADS, D_K)
        kh = (k @ Wk + bk).reshape(b, s, HEADS, D_K)
        vh = (v @ Wv + bv).reshape(b, s, HEADS, D_K)
        cos, sin = _rope_cache(s, D_K)
        qh = _apply_rope(qh, cos, sin)
        kh = _apply_rope(kh, cos, sin)
        qh = qh.transpose(0, 2, 1, 3)
        kh = kh.transpose(0, 2, 1, 3)
        vh = vh.transpose(0, 2, 1, 3)
        scores = jnp.einsum('bhqd,bhkd->bhqk', qh, kh) / jnp.sqrt(jnp.float32(D_K))
        m = mask[:, None, :, :]
        scores = jnp.where(m == 0, jnp.float32(-1000000000.0), scores)
        attn = jax.nn.softmax(scores, axis=-1)
        out = jnp.einsum('bhqk,bhkd->bhqd', attn, vh)
        concat = out.transpose(0, 2, 1, 3).reshape(b, s, D_MODEL)
        return concat @ Wo + bo

    def _L0_ffn_ref(x, shared_gate, shared_up, shared_down, gate_w, up_w, down_w, router_w, routing_bias):
        import jax, jax.numpy as jnp
        import numpy as np
        B, S, H = (2, 256, 128)
        E_ROUTED = 8
        TOP_K = 2
        I = 256
        b, s, h = x.shape
        shared = jnp.einsum('bsi,hi->bsh', jax.nn.silu(jnp.einsum('bsh,ih->bsi', x, shared_gate)) * jnp.einsum('bsh,ih->bsi', x, shared_up), shared_down)
        logits = jnp.einsum('bsh,eh->bse', x, router_w) + routing_bias
        probs = jax.nn.sigmoid(logits)
        scores, indices = jax.lax.top_k(probs, TOP_K)
        scores = scores / jnp.sum(scores, axis=-1, keepdims=True)
        t = b * s
        xf = x.reshape(t, h)
        idx = indices.reshape(t, TOP_K)
        sc = scores.reshape(t, TOP_K)
        w = jnp.zeros((t, E_ROUTED), dtype=x.dtype)
        w = w.at[jnp.arange(t)[:, None], idx].add(sc)
        g = jax.nn.silu(jnp.einsum('th,ehi->tei', xf, gate_w))
        u = jnp.einsum('th,ehi->tei', xf, up_w)
        combined = jnp.einsum('tei,eih,te->th', g * u, down_w, w)
        return shared + combined.reshape(b, s, h)

    def _L1_attn_ref(x, Wq, bq, Wk, bk, Wv, bv, Wo, bo):
        import jax, jax.numpy as jnp
        import numpy as np
        import math
        N_HEADS = 16
        FACTOR = 5
        B, T, D = x.shape
        H = N_HEADS
        Hd = D // H
        scale = Hd ** (-0.5)

        def proj(W, b):
            return (x @ W + b).reshape(B, T, H, Hd).transpose(0, 2, 1, 3)
        q = proj(Wq, bq)
        k = proj(Wk, bk)
        v = proj(Wv, bv)
        q_norm = jnp.sum(jnp.abs(q), axis=-1)
        u = min(int(FACTOR * math.log(T)), T)
        _, index = jax.lax.top_k(q_norm, u)
        scores = jnp.einsum('bhqd,bhkd->bhqk', q, k) * scale
        causal = jnp.tril(jnp.ones((T, T), dtype=bool))
        scores = jnp.where(causal, scores, -jnp.inf)
        sel_scores = jnp.take_along_axis(scores, index[..., None], axis=2)
        sel_attn = jax.nn.softmax(sel_scores, axis=-1)
        sel_out = jnp.einsum('bhut,bhtd->bhud', sel_attn, v)
        attn_output = jnp.zeros_like(q)
        bI = jnp.arange(B)[:, None, None]
        hI = jnp.arange(H)[None, :, None]
        attn_output = attn_output.at[bI, hI, index].set(sel_out)
        out = attn_output.transpose(0, 2, 1, 3).reshape(B, T, D)
        return out @ Wo + bo

    def _L1_xattn_ref(values, keys, query, mask, Wv, Wk, Wq, Wo, bo):
        import jax, jax.numpy as jnp
        import numpy as np
        EMBED = 128
        HEADS = 16
        HEAD_DIM = EMBED // HEADS
        N, Q = (query.shape[0], query.shape[1])
        K = keys.shape[1]
        v = (values @ Wv.T).reshape(N, K, HEADS, HEAD_DIM)
        k = (keys @ Wk.T).reshape(N, K, HEADS, HEAD_DIM)
        q = (query @ Wq.T).reshape(N, Q, HEADS, HEAD_DIM)
        att = jnp.einsum('nqhd,nkhd->nhqk', q, k)
        att = jnp.where(mask == 0, jnp.float32(-1e+20), att)
        att = jax.nn.softmax(att / np.sqrt(HEAD_DIM), axis=3)
        out = jnp.einsum('nhqk,nkhd->nqhd', att, v).reshape(N, Q, EMBED)
        return out @ Wo.T + bo

    def _L1_ffn_ref(inputs, waff, W1, b1, W2, b2, affinity_threshold):
        import jax, jax.numpy as jnp
        import numpy as np
        B, S, D, E, F = (4, 256, 128, 8, 512)
        MIN_CAPACITY = 4

        def _make_waff():
            g = D // E
            scale = E / D
            w = np.zeros((E, D), np.float32)
            for i in range(E):
                w[i, i * g:(i + 1) * g] = scale
            return jnp.asarray(w)
        num = jnp.einsum('bsd,ed->bse', inputs, waff)
        x_norm = jnp.linalg.norm(inputs, axis=-1, keepdims=True)
        w_norm = jnp.linalg.norm(waff, axis=-1)
        aff = num / (x_norm * w_norm[None, None, :] + 1e-09)
        router_probs = jax.nn.softmax(aff, axis=-1)
        cap = jnp.floor(S * jax.nn.sigmoid(aff.mean() - affinity_threshold)).astype(jnp.int32)
        cap = jnp.minimum(jnp.maximum(cap, MIN_CAPACITY), S)
        tcr = jax.nn.one_hot(jnp.argmax(router_probs, axis=-1), E, dtype=inputs.dtype)
        order = jnp.argsort(-aff, axis=1)
        ranks = jnp.argsort(order, axis=1)
        ecr = (ranks < cap).astype(inputs.dtype)
        dispatch = tcr * ecr
        masks = jnp.moveaxis(dispatch, -1, 0)

        def body(acc, expert):
            W1e, b1e, W2e, b2e, me = expert
            xi = inputs * me[..., None]
            h = jax.nn.gelu(xi @ W1e + b1e, approximate=False)
            return (acc + (h @ W2e + b2e), None)
        out, _ = jax.lax.scan(body, jnp.zeros_like(inputs), (W1, b1, W2, b2, masks))
        return out
    x = x + _L0_attn_ref(_layernorm(x, axis=-1), L0_attn_w_ln_z, L0_attn_b_ln_z, L0_attn_w_dt, L0_attn_b_dt, L0_attn_w_y, L0_attn_b_y, L0_attn_w_yact, L0_attn_b_yact, L0_attn_h0, L0_attn_w_fc, L0_attn_b_fc, L0_attn_w_fcact, L0_attn_b_fcact, L0_attn_w_out, L0_attn_b_out, L0_attn_g_sio, L0_attn_g_ffn)
    x = x + _L0_xattn_ref(_layernorm(x, axis=-1), ctx_1024, ctx_1024, mask_Bx1xS2_if1, L0_xattn_Wq, L0_xattn_bq, L0_xattn_Wk, L0_xattn_bk, L0_xattn_Wv, L0_xattn_bv, L0_xattn_Wo, L0_xattn_bo)
    x = x + _L0_ffn_ref(_layernorm(x, axis=-1), L0_ffn_shared_gate, L0_ffn_shared_up, L0_ffn_shared_down, L0_ffn_gate_w, L0_ffn_up_w, L0_ffn_down_w, L0_ffn_router_w, L0_ffn_routing_bias)
    x = x + _L1_attn_ref(_layernorm(x, axis=-1), L1_attn_Wq, L1_attn_bq, L1_attn_Wk, L1_attn_bk, L1_attn_Wv, L1_attn_bv, L1_attn_Wo, L1_attn_bo)
    x = x + _L1_xattn_ref(ctx_1024, ctx_1024, _layernorm(x, axis=-1), mask_Bx1xSxS2_if1, L1_xattn_Wv, L1_xattn_Wk, L1_xattn_Wq, L1_xattn_Wo, L1_xattn_bo)
    x = x + _L1_ffn_ref(_layernorm(x, axis=-1), L1_ffn_waff, L1_ffn_W1, L1_ffn_b1, L1_ffn_W2, L1_ffn_b2, L1_ffn_affinity_threshold)
    return x

_drawn_inputs = setup_inputs


def setup_inputs(seed=0):
    import zlib

    import numpy as np

    out = dict(_drawn_inputs(seed))
    spreads = {'L0_attn_g_sio': (1.0, 0.2),
     'L0_attn_g_ffn': (1.0, 0.2),
     'L0_xattn_bq': (0.0, 0.1),
     'L0_xattn_bk': (0.0, 0.1),
     'L0_xattn_bv': (0.0, 0.1),
     'L0_xattn_bo': (0.0, 0.1),
     'L0_ffn_routing_bias': (0.0, 0.489),
     'L1_attn_bq': (0.0, 0.1),
     'L1_attn_bk': (0.0, 0.8),
     'L1_attn_bv': (0.0, 0.1),
     'L1_attn_bo': (0.0, 0.1),
     'L1_xattn_bo': (0.0, 0.1),
     'L1_ffn_b1': (0.0, 0.1),
     'L1_ffn_b2': (0.0, 0.1)}
    factors = {'L0_attn_b_ln_z': 3.795,
     'L0_attn_w_dt': 2.76,
     'L0_attn_b_dt': 8.0,
     'L0_attn_h0': 6.243,
     'L0_ffn_router_w': 3.009}
    for name, (base, spread) in spreads.items():
        noise = np.random.default_rng([zlib.crc32(name.encode()), seed]).standard_normal(out[name].shape)
        drawn = base * np.exp(spread * noise) if base else spread * noise
        out[name] = jnp.asarray(drawn.astype(out[name].dtype))
    for name, factor in factors.items():
        out[name] = (out[name] * factor).astype(out[name].dtype)
    return out
```

```python
import concourse.bass as bass
from concourse import mybir
from contextlib import ExitStack, contextmanager

B, S, D, H = 16, 128, 128, 16
DH = D // H
NBLK = 4
GB = B // NBLK
BT = GB * S
NPAIR = NBLK // 2
NSTEP = 8
SB = B // NSTEP
ST = SB * S
FF0, I0, E0, TOPK = 512, 256, 8, 2
FF1, E1 = 512, 8
CAP_S, MIN_CAP = 256, 4
NTOP = 24
NPART = 3
ROW_M = NPART * NPART * DH
ROW_MASK = ROW_M + 2
NEG = -1.0e30
SCALE = float(DH) ** -0.5
LN_EPS, RMS_EPS = 1e-5, 1e-6
VC = DH + 1

STAGES = ["ctx", "sio", "ffn", "qp0", "ac0", "po0", "moe0", "qp1", "ac1", "po1", "qp2", "ac2", "po2",
          "aff", "route", "moe1"]

COLS = ["b_z", "b_dt", "b_y", "b_ya", "h0", "g_sio", "g_ffn", "b_out", "bq0", "bq0s", "bk0", "bk0s", "bo0",
        "bq1", "bk1", "bo1", "bo2"] + [f"b_fc{c}" for c in range(4)] + [f"b_fa{c}" for c in range(4)]


class Handoff:

    def __init__(self, sem, name, depth, uses):
        self.filled, self.freed, self.depth = sem(name + "_filled"), sem(name + "_freed"), depth
        self.base, n = {}, 0
        for s in STAGES:
            self.base[s] = n
            n += uses.get(s, 0)

    def at(self, stage, k):
        return self.base[stage] + k + 1

    def freed_at(self, stage, k):
        return self.base[stage] + k + 1 + self.depth

    def slot(self, stage, k):
        return (self.base[stage] + k) % self.depth


class Chain:

    def __init__(self, eng, sem, settled=None):
        self.eng, self.sem, self.base, self.k, self.settled = eng, sem, 0, 0, settled

    def settle(self):
        self.eng.sem_inc(self.settled, 1)

    def release(self, ins, filled, value, *freed):
        ins.then_inc(filled, 1)
        self.eng.wait_ge(filled, value)
        for r in freed:
            self.eng.sem_inc(r, 1)

    def __call__(self, ins, settle=False):
        ins.then_inc(self.sem, 1)
        self.k += 1
        self.eng.wait_ge(self.sem, self.base + self.k)
        if settle:
            self.settle()

    @contextmanager
    def loop(self, count, per):
        start = self.base + self.k
        with self.eng.Fori(0, count) as i:
            self.base, self.k = i * per + start, 0
            yield i
            assert self.k == per, (self.k, per)
        self.base, self.k = start + count * per, 0


def program(nc, t):
    f32, bf16, i32 = mybir.dt.float32, mybir.dt.bfloat16, mybir.dt.int32
    ALU, ACT, AX = mybir.AluOpType, mybir.ActivationFunctionType, mybir.AxisListType

    with ExitStack() as ctx:
        def sb(name, shape, dt=f32):
            return ctx.enter_context(nc.sbuf_tensor(name, shape, dt))

        def sem(name):
            return ctx.enter_context(nc.semaphore(name))

        q_scr = nc.dram_tensor("q_scr", (3, NSTEP, NPART, D, ST), bf16, kind="Internal").ap()
        k_scr = nc.dram_tensor("k_scr", (3, NSTEP, NPART, D, ST), bf16, kind="Internal").ap()
        keymask_scr = nc.dram_tensor("keymask_scr", (B, S), bf16, kind="Internal").ap()
        disp_scr = nc.dram_tensor("disp_scr", (E1 * B, S), bf16, kind="Internal").ap()

        x_tok = sb("x_tok", [128, B, D])
        y_tok = sb("y_tok", [128, B, D])
        w = {n: sb("w_" + n, list(t[n].shape)) for n in
             ("wz", "wdt", "wya", "wy", "wfc", "wfa", "wout", "wq0", "wq0s", "wk0", "wk0s", "wv0", "wo0",
              "wq1", "wk1", "wv1", "wo1", "wq2", "wk2", "wv2", "wo2", "gate", "up", "down", "router", "waff",
              "w1", "w2", "b1c", "b2r", "cols", "cos", "sin")}
        bv0 = sb("bv0", [128, D]); bv1 = sb("bv1", [128, D]); rbias = sb("rbias", [128, E0]); thr = sb("thr", [128, 1])
        col = {n: w["cols"][:, i:i + 1] for i, n in enumerate(COLS)}
        negbdt = sb("negbdt", [128, 1])

        ident = sb("ident", [128, 128]); identb = sb("identb", [128, 128], bf16)
        causal = sb("causal", [128, 128], bf16)
        fullmask = sb("fullmask", [128, B, S], bf16)
        earlier = sb("earlier", [128, S])
        lower_e = sb("lower_e", [128, E0, E0])
        batch_rows = sb("batch_rows", [128, B])
        head_cols = sb("head_cols", [128, 15 * H])
        rev = sb("rev", [128, E1])
        ones = sb("ones", [128, 128])
        halves = sb("halves", [128, 2, 4 * B])
        eps_tile = sb("eps_tile", [128, GB]); inv_d = sb("inv_d", [128, GB])
        keymask = sb("keymask", [B, S], bf16)

        bn = sb("bn", [128, GB, 6]); mv_b = sb("mv_b", [128, GB, 2]); mv = sb("mv", [128, B, 2]); rstd = sb("rstd", [128, B])
        rr = sb("rr", [128, B]); r2 = sb("r2", [128, B]); ssq = sb("ssq", [128, B])
        ps_a = sb("ps_a", [128, GB]); ps_b = sb("ps_b", [128, GB])
        xn_tm = sb("xn_tm", [128, 2, GB, D]); nT = sb("nT", [128, 2, BT])
        wa = sb("wa", [128, 2, 2 * BT]); wb = sb("wb", [128, 2, 2 * BT])
        f = sb("f", [128, 6, BT])
        parts = sb("parts", [128, 2, NPART, BT], bf16)
        oT = sb("oT", [128, 2, BT])
        stack = sb("stack", [128, 4, H * ST], bf16)
        qflat = [stack[:, 0, :], stack[:, 1, :], wb[:, :, :].rearrange("p a n -> p (a n)").bitcast(bf16)]
        kflat = [stack[:, 2, :], stack[:, 3, :], f[:, 0:4, :].rearrange("p a n -> p (a n)").bitcast(bf16)]
        qst = [x.rearrange("p (h t) -> p h t", h=H) for x in qflat]
        kst = [x.rearrange("p (h t) -> p h t", h=H) for x in kflat]
        v0x = sb("v0x", [128, B, H, VC]); v2x = sb("v2x", [128, B, H, VC])
        vx = [v0x, v0x, v2x]
        attnT = y_tok
        negm = sb("negm", [128, H, SB]); mp = sb("mp", [128, 2, H, SB], bf16); mT = sb("mT", [64, S], bf16)
        rec = sb("rec", [128, H]); o_tok = sb("o_tok", [128, 2, H, DH])
        qn = sb("qn", [128, S]); top8 = sb("top8", [128, 8]); selT = sb("selT", [128, B, H])
        sel = sb("sel", [128, S])
        rl = sb("rl", [128, GB, E0]); pr = sb("pr", [128, GB, E0]); rk = sb("rk", [128, GB, E0])
        cmp1 = sb("cmp1", [128, GB * E0, E0]); cmp2 = sb("cmp2", [128, GB * E0, E0])
        junk = [c.rearrange("p a b -> p (a b)")[:, k * D:(k + 1) * D] for c in (cmp1[:, :, :], cmp2[:, :, :]) for k in (0, 1)]
        wsum = sb("wsum", [128, GB]); wr = sb("wr", [128, 2, GB, E0])
        num = sb("num", [128, B, E1]); aff = sb("aff", [128, B, E1]); oh = sb("oh", [128, B, E1])
        a1 = sb("a1", [128, B, E1]); wn = sb("wn", [128, E1]); own = sb("own", [128, B]); mx = sb("mx", [128, B])
        xnorm = sb("xnorm", [128, B]); asum = sb("asum", [128, 1]); capv = sb("capv", [128, 1])
        negthr = sb("negthr", [128, 1]); rank = sb("rank", [128, B])
        affT = sel; ohT = sb("ohT", [128, S]); dT = sb("dT", [128, S], bf16)
        b2s = qn
        mask_i = wa[:, :, :].rearrange("p a n -> p (a n)").bitcast(i32).rearrange("p (b s) -> p b s", b=B)
        km_i = wb[0:B, 0, 0:S].bitcast(i32)
        aff_rows = wa[:, :, :].rearrange("p a n -> p (a n)").rearrange("p (b s) -> p b s", b=B)
        v_batch = [f[:, 4, j * 256:j * 256 + (H - 1) * VC + 32] for j in range(2)]
        o_wide = f[:, 5, :]

        ps = ctx.enter_context(nc.psum_tensor("ps", [128, 8, 512], f32))
        T, U = ps[:, 0, :], ps[:, 1, :]
        A = [ps[:, 2, :], ps[:, 3, :]]
        Bk = [ps[:, 4:6, :], ps[:, 6:8, :]]
        BF = [b.rearrange("p a n -> p (a n)") for b in Bk]

        hT = Handoff(sem, "bankT", 1, dict(ctx=4, sio=8, ffn=8, qp0=4, ac0=40, po0=4, moe0=4, qp1=8, ac1=40,
                                            po1=4, qp2=4, ac2=40, po2=4, aff=4, route=3))
        hU = Handoff(sem, "bankU", 1, dict(ctx=4, sio=4, ac0=16, moe0=4, qp1=2, ac1=16, ac2=16, aff=4, route=3))
        hA = Handoff(sem, "bankA", 2, dict(ctx=8, sio=4, ffn=4, ac0=64, moe0=36, qp1=4, ac1=64, ac2=64, moe1=4))
        hB = Handoff(sem, "bankB", 2, dict(ctx=4, sio=4, ffn=16, qp0=4, ac0=32, po0=4, moe0=72, qp1=4, ac1=32,
                                           po1=4, qp2=4, ac2=32, po2=4, route=2, moe1=64))
        hXN = Handoff(sem, "xn_tm", 2, dict(ctx=4, sio=4, ffn=4, qp0=4, moe0=4, qp1=4, qp2=4, aff=4))
        hNT = Handoff(sem, "nT", 2, dict(ctx=4, sio=4, ffn=4, qp0=4, moe0=4, qp1=4, qp2=4, aff=4, moe1=32))
        hWA = Handoff(sem, "wa", 2, dict(sio=4, ffn=16, ac0=32, moe0=36, ac1=32, ac2=32, moe1=32))
        hWB = Handoff(sem, "wb", 2, dict(sio=4, ffn=16, moe0=36, moe1=32))
        hOT = Handoff(sem, "oT", 2, dict(sio=4, ffn=4, po0=4, po1=4, po2=4))
        hP = Handoff(sem, "parts", 2, dict(ctx=8, qp0=4, qp1=8, qp2=4))
        hO = Handoff(sem, "o_tok", 2, dict(ac0=16, ac1=16, ac2=16))
        hFV = Handoff(sem, "to_split", 2, dict(ctx=8, qp0=4, qp1=8, qp2=4))
        hF45 = Handoff(sem, "f45", 2, dict(sio=4, qp1=4))
        hVB = Handoff(sem, "v_batch", 2, dict(ac0=16, ac1=16, ac2=16))
        hOW = Handoff(sem, "o_wide", 1, dict(ac0=16, ac1=16, ac2=16))
        rings = (hVB, hOW, hT, hU, hA, hB, hXN, hNT, hWA, hWB, hOT, hP, hO, hFV, hF45)

        consts_ready = sem("consts_ready"); x_loaded = sem("x_loaded"); w_loaded = sem("w_loaded")
        masks_loaded = sem("masks_loaded"); ctx_loaded = [sem("ctx_loaded0"), sem("ctx_loaded1")]; stack_init = sem("stack_init")
        const_rows = sem("const_rows"); keymask_ready = sem("keymask_ready"); masks_ready = sem("masks_ready")
        dve_chain = sem("dve_chain"); pool_chain = sem("pool_chain"); act_chain = sem("act_chain")
        pool_settled = sem("pool_settled"); dve_settled = sem("dve_settled"); pe_settled = sem("pe_settled")
        stats_done = sem("stats_done"); rstd_done = sem("rstd_done")
        x1_done = sem("x1_done"); ssq_done = sem("ssq_done"); r2_done = sem("r2_done")
        scratch_written = sem("scratch_written"); stack_loaded = [sem("stack_loaded%d" % k) for k in range(3)]; slot2_filled = sem("slot2_filled")
        stack_freed = sem("stack_freed"); m_ready = sem("m_ready"); mp_ready = sem("mp_ready"); m_stored = sem("m_stored")
        attnT_done = sem("attnT_done"); v0_ready = sem("v0_ready"); v2_ready = sem("v2_ready")
        h_ready = sem("h_ready")
        absq_ready = sem("absq_ready"); sel_ready = sem("sel_ready"); selT_ready = sem("selT_ready")
        logits_ready = sem("logits_ready"); probs_ready = sem("probs_ready")
        scaled_ready = sem("scaled_ready"); scaled_used = sem("scaled_used")
        sq_done = sem("sq_done"); num_ready = sem("num_ready"); route_pe = sem("route_pe")
        waff_sq = sem("waff_sq"); wn_ready = sem("wn_ready"); wn_raw = sem("wn_raw"); xnorm_ready = sem("xnorm_ready")
        asum_ready = sem("asum_ready"); cap_ready = sem("cap_ready"); aff_ready = sem("aff_ready")
        affT_ready = sem("affT_ready"); affrows_ready = sem("affrows_ready"); disp_ready = sem("disp_ready")
        dT_ready = sem("dT_ready"); disp_stored = sem("disp_stored"); disp_loaded = sem("disp_loaded")
        x_done = sem("x_done"); out_stored = sem("out_stored")

        def blk(tile, b, n=GB):
            return tile[:, bass.ts(b, n), :]

        STAT = {s: 4 * k for k, s in enumerate(["sio", "qp0", "moe0", "qp1", "qp2", "aff"])}
        W_LOADS = 16 * (len(w) + 4)
        block = ctx.enter_context(nc.Block())

        @block.sync
        def _(sp):
            for b in range(NBLK):
                sp.dma_start(x_tok[:, b * GB:(b + 1) * GB, :],
                             t["x"][b * GB:(b + 1) * GB].rearrange("b t d -> t b d")).then_inc(x_loaded, 16)
            with sp.Fori(0, NPAIR) as i:
                for p in range(2):
                    sp.wait_ge(hXN.freed, hXN.at("ctx", i * 2 + p))
                    sp.dma_start(xn_tm[:, p], t["ctx"][bass.ts(i * 2 + p, GB)].rearrange("b t d -> t b d"))\
                      .then_inc(ctx_loaded[p], 16)
                    sp.wait_ge(ctx_loaded[p], i * 16 + 16)
                    sp.sem_inc(hXN.filled, 1)
            sp.wait_ge(stack_init, 2)
            for s in (0, 1):
                sp.dma_start(qst[s][ROW_MASK:ROW_MASK + 1], kst[s][ROW_MASK:ROW_MASK + 1]).then_inc(const_rows, 16)
            sp.wait_ge(keymask_ready, 1)
            sp.dma_start(keymask_scr, keymask[:, :]).then_inc(const_rows, 16)
            sp.wait_ge(const_rows, 48)

            def scratch_stage(stage, tensors, written):
                per = len(tensors)
                with sp.Fori(0, NPAIR) as i:
                    for p in range(2):
                        for q, dst in enumerate(tensors):
                            k = per * p + q
                            sp.wait_ge(hP.filled, hP.at(stage, i * (2 * per) + k))
                            for half in range(2):
                                sp.dma_start(dst[bass.ds(i * 4 + (2 * p + half), 1)].rearrange("o c p t -> p (o c) t"),
                                             parts[:, hP.slot(stage, k), :, half * ST:(half + 1) * ST])\
                                  .then_inc(scratch_written, 16)
                            sp.wait_ge(scratch_written, i * (64 * per) + (written + 32 * (k + 1)))
                            sp.sem_inc(hP.freed, 1)

            def load_stack(a, n, slot):
                loaded = stack_loaded[slot]
                sp.wait_ge(stack_freed, n + (NSTEP * a + 1))
                sp.dma_start(qflat[slot][ROW_M:ROW_M + 2], qflat[slot][ROW_MASK + 1:ROW_MASK + 3]).then_inc(loaded, 16)
                for i in range(NPART):
                    src = q_scr[a, bass.ds(n, 1), i].rearrange("o (d h) t -> o d (h t)", d=DH)
                    sp.dma_start(qflat[slot][i * 24:i * 24 + 24], src.broadcast_to([NPART, DH, H * ST]))\
                      .then_inc(loaded, 16)
                src = k_scr[a, bass.ds(n, 1)].rearrange("o c (d h) t -> o (c d) (h t)", d=DH)
                sp.dma_start(kflat[slot][0:ROW_M], src.broadcast_to([NPART, NPART * DH, H * ST])).then_inc(loaded, 16)
                if a == 0:
                    src = keymask_scr.rearrange("(n b) s -> n (b s)", b=SB)[bass.ds(n, 1)]
                    sp.dma_start(kst[slot][ROW_MASK:ROW_MASK + 1], src.unsqueeze(1).broadcast_to([1, H, ST]))\
                      .then_inc(loaded, 16)
                else:
                    sp.dma_start(kflat[slot][ROW_MASK:ROW_MASK + 1], qflat[slot][ROW_MASK + 1:ROW_MASK + 2])\
                      .then_inc(loaded, 16)

            def store_m(a, n, slot):
                sp.wait_ge(m_ready, n + (NSTEP * a + 1))
                for k in range(2):
                    sp.dma_start(qflat[slot][ROW_M + k:ROW_M + k + 1], mT[k * H * SB:(k + 1) * H * SB, :])\
                      .then_inc(m_stored, 16)

            def attention_loads(a, written):
                sp.wait_ge(scratch_written, written)
                load_stack(a, 0, 0)
                load_stack(a, 1, 1)
                sp.wait_ge(slot2_filled, 2 * a + 2)
                sp.dma_start(qflat[2][ROW_MASK:ROW_MASK + 1], kflat[2][ROW_MASK + 1:ROW_MASK + 2]).then_inc(const_rows, 16)
                sp.wait_ge(const_rows, 16 * (4 + a))
                store_m(a, 0, 0)
                with sp.Fori(0, NSTEP // 3) as i:
                    for p in range(3):
                        load_stack(a, i * 3 + (p + 2), (p + 2) % 3)
                        store_m(a, i * 3 + (p + 1), (p + 1) % 3)
                store_m(a, NSTEP - 1, (NSTEP - 1) % 3)

            TENSOR = 16 * NSTEP
            scratch_stage("ctx", [k_scr[0], k_scr[2]], 0)
            scratch_stage("qp0", [q_scr[0]], 2 * TENSOR)
            attention_loads(0, 3 * TENSOR)
            scratch_stage("qp1", [q_scr[1], k_scr[1]], 3 * TENSOR)
            attention_loads(1, 5 * TENSOR)
            scratch_stage("qp2", [q_scr[2]], 5 * TENSOR)
            attention_loads(2, 6 * TENSOR)
            sp.wait_ge(dT_ready, 1)
            sp.dma_start(disp_scr, dT[:, :]).then_inc(disp_stored, 16)
            sp.wait_ge(disp_stored, 16)
            for e in range(E1):
                sp.dma_start(stack[:, e // 2, (e % 2) * B * S:(e % 2 + 1) * B * S],
                             disp_scr[e * B:(e + 1) * B, :].rearrange("b s -> (b s)").partition_broadcast(128))\
                  .then_inc(disp_loaded, 16)
            with sp.Fori(0, NBLK) as b:
                sp.wait_ge(x_done, b + 1)
                sp.dma_start(t["out"][bass.ts(b, GB)].rearrange("b t d -> t b d"), blk(x_tok, b)).then_inc(out_stored, 16)
            sp.wait_ge(out_stored, 16 * NBLK)

        @block.gpsimd
        def _(g):
            chain = Chain(g, pool_chain, pool_settled)

            def link(ins):
                chain(ins, settle=True)

            for r in rings:
                g.sem_inc(r.freed, r.depth)
            g.sem_inc(stack_freed, 3)
            g.sem_inc(scaled_used, 2)
            g.memset(halves[:, 0, :], -0.5)
            g.memset(halves[:, 1, :], 0.5)
            g.memset(eps_tile[:, :], LN_EPS)
            g.memset(inv_d[:, :], 1.0 / D)
            g.memset(ones[:, :], 1.0)
            g.memset(v0x[:, :, :, :], 1.0)
            g.memset(v2x[:, :, :, :], 1.0)
            g.memset(head_cols[:, :], 0.0)
            g.memset(batch_rows[:, :], 1.0)
            g.memset(lower_e[:, :, :], 1.0)
            g.memset(earlier[:, :], 1.0)
            g.memset(causal[:, :], 0.0)
            g.memset(ident[:, :], 0.0)
            g.iota(rev[:, :], [[-1, E1]], base=E1, channel_multiplier=0, allow_small_or_imprecise_dtypes=True)
            g.memset(stack[:, 0:2, :], 0.0).then_inc(stack_init, 1)
            g.memset(stack[:, 2:4, :], 1.0).then_inc(stack_init, 1)
            g.wait_ge(stack_init, 2)
            link(g.affine_select(out=ident[:, :], in_=ident[:, :], compare_op=ALU.not_equal, fill=1.0, base=0,
                                 pattern=[[-1, 128]], channel_multiplier=1))
            link(g.tensor_copy(identb[:, :], ident[:, :]))
            link(g.affine_select(out=causal[:, :], in_=causal[:, :], compare_op=ALU.is_ge, fill=NEG, base=0,
                                 pattern=[[-1, 128]], channel_multiplier=1))
            link(g.affine_select(out=earlier[:, :], in_=earlier[:, :], compare_op=ALU.is_gt, fill=0.0, base=0,
                                 pattern=[[-1, 128]], channel_multiplier=1))
            link(g.affine_select(out=lower_e[:, :, :], in_=lower_e[:, :, :], compare_op=ALU.is_gt, fill=0.0, base=0,
                                 pattern=[[1, E0], [-1, E0]], channel_multiplier=0))
            link(g.affine_select(out=batch_rows[:, :], in_=batch_rows[:, :], compare_op=ALU.is_ge, fill=0.0, base=0,
                                 pattern=[[-E1, B]], channel_multiplier=1))
            link(g.affine_select(out=batch_rows[:, :], in_=batch_rows[:, :], compare_op=ALU.is_ge, fill=0.0,
                                 base=E1 - 1, pattern=[[E1, B]], channel_multiplier=-1))
            for d in range(DH):
                link(g.affine_select(out=head_cols[:, 7 * H:8 * H], in_=head_cols[:, 7 * H:8 * H],
                                     compare_op=ALU.not_equal, fill=1.0, base=-H * d, pattern=[[-1, H]],
                                     channel_multiplier=1))
            g.sem_inc(consts_ready, 1)
            g.wait_ge(w_loaded, W_LOADS)
            link(g.tensor_scalar(negbdt[:, :], col["b_dt"], -1.0, None, ALU.mult))
            link(g.tensor_scalar(negthr[:, :], thr[:, :], -1.0, None, ALU.mult))
            g.sem_inc(consts_ready, 1)

            def stats(s):
                with chain.loop(NBLK, 2) as b:
                    g.wait_ge(stats_done, b + (STAT[s] + 1))
                    chain.settle()
                    link(g.tensor_tensor(ps_a[:, :], mv[:, bass.ts(b, GB), 1], eps_tile[:, :], ALU.add))
                    link(g.tensor_tensor(rstd[:, bass.ts(b, GB)], ps_a[:, :], halves[:, 0, 0:GB], ALU.pow))
                    g.sem_inc(rstd_done, 1)

            def split_stage(stage, tensors):
                per = len(tensors)
                with chain.loop(NPAIR, 2 * (3 * per + sum(tensors))) as i:
                    for p in range(2):
                        for q, rope in enumerate(tensors):
                            k = per * p + q
                            g.wait_ge(hFV.filled, hFV.at(stage, i * (2 * per) + k))
                            chain.settle()
                            v, r = f[:, 2 * hFV.slot(stage, k), :], f[:, 2 * hFV.slot(stage, k) + 1, :]
                            if rope:
                                link(g.tensor_tensor(v, v, r, ALU.add))
                            g.wait_ge(hP.freed, hP.at(stage, i * (2 * per) + k))
                            chain.settle()
                            part = parts[:, hP.slot(stage, k)]
                            link(g.tensor_copy(part[:, 0, :], v))
                            link(g.tensor_tensor(r, v, part[:, 0, :], ALU.subtract))
                            link(g.tensor_copy(part[:, 1, :], r))
                            chain.release(g.tensor_tensor(part[:, 2, :], r, part[:, 1, :], ALU.subtract),
                                         hP.filled, hP.at(stage, i * (2 * per) + k), hFV.freed)

            def attention(a):
                stage = "ac%d" % a
                g.memset(qflat[2], 0.0).then_inc(slot2_filled, 1)
                g.memset(kflat[2], 1.0).then_inc(slot2_filled, 1)
                g.wait_ge(hF45.freed, hF45.at(stage, 1))
                link(g.memset(f[:, 4:6, :], 0.0))
                g.wait_ge(v0_ready, NBLK if a == 0 else 2 * NBLK)
                g.wait_ge(v2_ready, NBLK)
                with chain.loop(NSTEP, 0) as n:
                    for j in range(2):
                        k = n * 2 + j
                        g.wait_ge(hVB.freed, hVB.at(stage, k))
                        chain.settle()
                        g.tensor_copy(v_batch[j][:, 0:H * VC],
                                      vx[a][:, bass.ds(k, 1), :, :].rearrange("p o h c -> p (o h c)"))\
                         .then_inc(hVB.filled, 1)

            with chain.loop(NBLK, 7) as b:
                q4 = bass.ts(b, GB)
                g.wait_ge(stats_done, b + 1)
                chain.settle()
                link(g.tensor_tensor(ps_a[:, :], mv[:, q4, 1], eps_tile[:, :], ALU.add))
                link(g.tensor_tensor(rstd[:, q4], ps_a[:, :], halves[:, 0, 0:GB], ALU.pow))
                link(g.tensor_tensor(ps_a[:, :], rstd[:, q4], rstd[:, q4], ALU.mult))
                link(g.tensor_tensor(ps_a[:, :], ps_a[:, :], mv[:, q4, 1], ALU.mult))
                link(g.tensor_scalar(ps_a[:, :], ps_a[:, :], RMS_EPS, None, ALU.add))
                link(g.tensor_tensor(ps_b[:, :], ps_a[:, :], halves[:, 0, 0:GB], ALU.pow))
                link(g.tensor_tensor(rr[:, q4], ps_b[:, :], rstd[:, q4], ALU.mult))
                g.sem_inc(rstd_done, 1)

            split_stage("ctx", [1, 0])

            with chain.loop(NBLK, 4) as b:
                q4 = bass.ts(b, GB)
                g.wait_ge(x1_done, b + 1)
                chain.settle()
                link(g.tensor_tensor(blk(x_tok, b), blk(x_tok, b), blk(y_tok, b), ALU.add))
                g.wait_ge(ssq_done, b * GB + GB)
                chain.settle()
                link(g.tensor_tensor(ps_b[:, :], ssq[:, q4], inv_d[:, :], ALU.mult))
                link(g.tensor_scalar(ps_a[:, :], ps_b[:, :], RMS_EPS, None, ALU.add))
                link(g.tensor_tensor(r2[:, q4], ps_a[:, :], halves[:, 0, 0:GB], ALU.pow))
                g.sem_inc(r2_done, 1)
            stats("qp0")
            split_stage("qp0", [1])
            attention(0)
            stats("moe0")
            with chain.loop(NBLK, E0) as b:
                for e in range(E0):
                    g.wait_ge(scaled_ready, b * E0 + (e + 1))
                    chain.settle()
                    link(g.tensor_tensor(blk(x_tok, b), blk(x_tok, b),
                                         f[:, e % 2, :].rearrange("p (b d) -> p b d", b=GB), ALU.add))
                    g.sem_inc(scaled_used, 1)
            stats("qp1")
            split_stage("qp1", [0, 0])
            attention(1)
            stats("qp2")
            split_stage("qp2", [0])
            attention(2)
            stats("aff")
            g.wait_ge(wn_raw, 1)
            g.tensor_tensor(wn[:, :], wn[:, :], halves[:, 1, 0:E1], ALU.pow).then_inc(wn_ready, 1)
            g.wait_ge(ssq_done, 2 * B)
            g.tensor_tensor(xnorm[:, :], ssq[:, :], halves[:, 1, 0:B], ALU.pow).then_inc(xnorm_ready, 1)

        @block.scalar
        def _(act):
            link = Chain(act, act_chain)
            for n in w:
                act.dma_start(w[n][...], t[n]).then_inc(w_loaded, 16)
            for dst, src in ((bv0, t["bv0"]), (bv1, t["bv1"]), (rbias, t["rbias"]), (thr, t["thr"])):
                act.dma_start(dst[:, :], src.partition_broadcast(128)).then_inc(w_loaded, 16)
            act.dma_start(mask_i, t["maskf"].rearrange("b o q k -> q (b o) k")).then_inc(masks_loaded, 16)
            act.dma_start(km_i, t["maskk"].rearrange("b o k -> (b o) k")).then_inc(masks_loaded, 16)
            act.wait_ge(consts_ready, 2)
            act.wait_ge(w_loaded, W_LOADS)

            def transposed(stage, i, k, p, scale=None, xn_freed=True):
                act.wait_ge(hT.filled, hT.at(stage, k))
                if xn_freed:
                    act.sem_inc(hXN.freed, 1)
                act.wait_ge(hNT.freed, hNT.at(stage, i * 2 + p))
                ins = (act.activation(nT[:, p, :], T, ACT.Copy) if scale is None
                       else act.activation(nT[:, p, :], T, ACT.Identity, scale=scale))
                link.release(ins, hNT.filled, hNT.at(stage, i * 2 + p), hT.freed)

            with link.loop(NPAIR, 0) as i:
                for p in range(2):
                    transposed("ctx", i, i * 2 + p, p)
                for p in range(2):
                    act.wait_ge(hA.filled, hA.at("ctx", i * 4 + 2 * p + 1))
                    link.release(act.activation(v2x[:, bass.ts(i * 2 + p, GB), :, 0:DH],
                                                A[1].rearrange("p (b h d) -> p b h d", b=GB, h=H), ACT.Copy),
                                 v2_ready, i * 2 + (p + 1), hA.freed)
                    act.wait_ge(hU.filled, hU.at("ctx", i * 2 + p))
                    act.sem_inc(hNT.freed, 1)
                    k = i * 4 + (2 * p + 1)
                    act.wait_ge(hFV.filled, hFV.at("ctx", i * 4 + 2 * p))
                    act.wait_ge(hFV.freed, hFV.at("ctx", k))
                    link.release(act.activation(f[:, 2 * hFV.slot("ctx", 1), :], U, ACT.Copy),
                                 hFV.filled, hFV.at("ctx", k), hU.freed)

            with link.loop(NPAIR, 0) as i:
                for p in range(2):
                    transposed("sio", i, i * 4 + p, p, scale=col["g_sio"])
                for p in range(2):
                    n = i * 2 + p
                    act.wait_ge(hB.filled, hB.at("sio", n))
                    act.wait_ge(hWA.freed, hWA.at("sio", n))
                    act.wait_ge(hWB.freed, hWB.at("sio", n))
                    act.activation(wa[:, p, 0:BT], Bk[p][:, 0, :], ACT.Sigmoid, bias=col["b_z"])
                    act.activation(wa[:, p, BT:], Bk[p][:, 1, :], ACT.Sigmoid, bias=col["b_dt"])
                    act.activation(wb[:, p, 0:BT], Bk[p][:, 1, :], ACT.Sigmoid, bias=negbdt[:, :], scale=-1.0)\
                       .then_inc(hB.freed, 1)
                    act.wait_ge(hA.filled, hA.at("sio", n))
                    act.sem_inc(hNT.freed, 1)
                    link.release(act.activation(wb[:, p, BT:], A[p], ACT.Silu, bias=col["b_ya"]),
                                 hWB.filled, hWB.at("sio", n), hWA.filled, hA.freed)
                for p in range(2):
                    act.wait_ge(x1_done, i * 2 + (p + 1))
                    for j in range(GB):
                        tok = bass.ds(i * 8 + (4 * p + j), 1)
                        act.activation(junk[j], y_tok[:, tok, :].rearrange("p o d -> p (o d)"), ACT.Square,
                                       accum_out=ssq[:, tok]).then_inc(ssq_done, 1)
                    act.wait_ge(ssq_done, i * 8 + (4 * p + 4))

            with link.loop(NPAIR, 0) as i:
                for p in range(2):
                    transposed("ffn", i, i * 4 + p, p, scale=col["g_ffn"])
                for p in range(2):
                    for c in range(4):
                        k = 4 * p + c
                        act.wait_ge(hB.filled, hB.at("ffn", i * 8 + k))
                        if c == 3:
                            act.sem_inc(hNT.freed, 1)
                        act.wait_ge(hWA.freed, hWA.at("ffn", i * 8 + k))
                        act.activation(wa[:, k % 2, 0:BT], Bk[k % 2][:, 1, :], ACT.Silu, bias=col["b_fa%d" % c])\
                           .then_inc(hWA.filled, 1)
                    act.wait_ge(hA.filled, hA.at("ffn", i * 2 + p))
                    act.sem_inc(hWB.freed, 1)
                    act.wait_ge(hOT.freed, hOT.at("ffn", i * 2 + p))
                    link.release(act.activation(oT[:, p, :], A[p], ACT.Identity, bias=col["b_out"]),
                                 hOT.filled, hOT.at("ffn", i * 2 + p), hA.freed)

            def query_stage(a):
                stage = "qp%d" % a
                with link.loop(NPAIR, 0) as i:
                    for p in range(2):
                        transposed(stage, i, i * (4 if a == 1 else 2) + p, p)
                    for p in range(2):
                        n = i * 2 + p
                        if a == 0:
                            continue
                        act.wait_ge(hB.filled, hB.at(stage, n))
                        if a == 1:
                            for q, bias in enumerate(("bq1", "bk1")):
                                k = i * 4 + (2 * p + q)
                                act.wait_ge(hFV.freed, hFV.at(stage, k))
                                act.activation(f[:, 2 * hFV.slot(stage, q), :], Bk[p][:, q, :], ACT.Identity,
                                               bias=col[bias]).then_inc(hFV.filled, 1)
                            act.wait_ge(hF45.freed, hF45.at(stage, n))
                            link.release(act.activation(f[:, 4 + p, :], Bk[p][:, 0, :], ACT.Abs, bias=col["bq1"]),
                                         hF45.filled, hF45.at(stage, n), hB.freed)
                        else:
                            act.sem_inc(hNT.freed, 1)
                            act.wait_ge(hFV.freed, hFV.at(stage, n))
                            link.release(act.activation(f[:, 2 * hFV.slot(stage, p), :], Bk[p][:, 0, :], ACT.Copy),
                                         hFV.filled, hFV.at(stage, n), hB.freed)

            def attention(a):
                stage = "ac%d" % a

                def exps(n, u):
                    act.wait_ge(hB.filled, hB.at(stage, n * 4 + u))
                    if u == 3:
                        act.sem_inc(stack_freed, 1)
                    act.wait_ge(hWA.freed, hWA.at(stage, n * 4 + u))
                    link.release(act.activation(wa[:, u % 2, :], BF[u % 2], ACT.Exp, scale=SCALE),
                                 hWA.filled, hWA.at(stage, n * 4 + u), hB.freed)

                def products_out(n, j):
                    k = n * 2 + j
                    act.wait_ge(hU.filled, hU.at(stage, k))
                    act.sem_inc(hWA.freed, 1)
                    act.sem_inc(hVB.freed, 1)
                    act.wait_ge(hOW.freed, hOW.at(stage, k))
                    link.release(act.activation(o_wide, U, ACT.Copy), hOW.filled, hOW.at(stage, k), hU.freed)

                def store_o(n, j, k):
                    act.wait_ge(hT.filled, hT.at(stage, k))
                    act.sem_inc(hO.freed, 1)
                    link.release(act.activation(attnT[:, bass.ds(n * 2 + j, 1), :].rearrange("p o t -> p (o t)"),
                                                T[:, 0:S], ACT.Copy),
                                 attnT_done, n * 2 + (B * a + j + 1), hT.freed)

                def step(n, before):
                    for op, u in STEP:
                        if op == "B":
                            exps(n, u)
                        elif op == "K":
                            products_out(n, u)
                        elif op == "O":
                            store_o(n, u, n * 5 + 2)
                        elif op == "k" and before is not None:
                            products_out(before, u)
                        elif op == "o" and before is not None:
                            store_o(before, u, before * 5 + 5)

                step(0, None)
                with link.loop((NSTEP - 2) // 3, 0) as i:
                    for p in range(3):
                        step(i * 3 + (p + 1), i * 3 + p)
                step(NSTEP - 1, NSTEP - 2)
                products_out(NSTEP - 1, 1)
                store_o(NSTEP - 1, 1, 5 * NSTEP - 1)

            def output_stage(a):
                stage = "po%d" % a
                with link.loop(NPAIR, 0) as i:
                    for p in range(2):
                        n = i * 2 + p
                        act.wait_ge(hB.filled, hB.at(stage, n))
                        act.wait_ge(hOT.freed, hOT.at(stage, n))
                        link.release(act.activation(oT[:, p, :], Bk[p][:, 0, :], ACT.Identity, bias=col["bo%d" % a]),
                                     hOT.filled, hOT.at(stage, n), hB.freed)

            query_stage(0)
            attention(0)
            output_stage(0)

            with link.loop(NPAIR, 0) as i:
                for p in range(2):
                    transposed("moe0", i, i * 2 + p, p)
                for p in range(2):
                    act.wait_ge(logits_ready, i * 2 + (p + 1))
                    act.activation(pr[:, :, :], rl[:, :, :], ACT.Sigmoid).then_inc(probs_ready, 1)
                for p in range(2):
                    for e in range(E0 + 1):
                        k = i * 18 + (9 * p + e)
                        s = (p + e) % 2
                        act.wait_ge(hB.filled, hB.at("moe0", k * 2))
                        act.wait_ge(hWA.freed, hWA.at("moe0", k))
                        link.release(act.activation(wa[:, s, :], BF[0], ACT.Silu),
                                     hWA.filled, hWA.at("moe0", k), hB.freed)

            query_stage(1)
            attention(1)
            output_stage(1)
            query_stage(2)
            attention(2)
            output_stage(2)

            act.activation(a1[:, 0, :], w["waff"][:, :], ACT.Square).then_inc(waff_sq, 1)
            with link.loop(NPAIR, 0) as i:
                for p in range(2):
                    act.wait_ge(hXN.filled, hXN.at("aff", i * 2 + p))
                    act.wait_ge(ssq_done, i * 8 + (B + 4 * p))
                    for j in range(GB):
                        tok = bass.ds(i * 8 + (4 * p + j), 1)
                        act.activation(junk[j], xn_tm[:, p, j, :], ACT.Square,
                                       accum_out=ssq[:, tok]).then_inc(ssq_done, 1)
                    act.wait_ge(ssq_done, i * 8 + (B + 4 * p + 4))
                    act.wait_ge(hT.filled, hT.at("aff", i * 2 + p))
                    act.sem_inc(hXN.freed, 1)
                    act.activation(attnT[:, bass.ts(i * 2 + p, GB), :].rearrange("p b t -> p (b t)"), T, ACT.Copy)
                    act.wait_ge(hNT.freed, hNT.at("aff", i * 2 + p))
                    link.release(act.activation(nT[:, p, :], T, ACT.Copy),
                                 hNT.filled, hNT.at("aff", i * 2 + p), hT.freed)
            act.wait_ge(route_pe, 2)
            act.activation(capv[:, :], U[:, 0:1], ACT.Sigmoid, bias=negthr[:, :], scale=1.0 / (B * S * E1))\
               .then_inc(cap_ready, 1)

            with link.loop(NPAIR, 0) as i:
                for p in range(2):
                    for e in range(E1):
                        k = i * 16 + (8 * p + e)
                        s = e % 2
                        act.wait_ge(hB.filled, hB.at("moe1", k * 2))
                        act.wait_ge(hWA.freed, hWA.at("moe1", k))
                        act.activation(wa[:, s, 0:BT], Bk[0][:, 0, :], ACT.Gelu, bias=w["b1c"][:, e, 0:1])
                        link.release(act.activation(wa[:, s, BT:], Bk[0][:, 1, :], ACT.Gelu, bias=w["b1c"][:, e, 1:2]),
                                     hWA.filled, hWA.at("moe1", k), hB.freed)
                        act.wait_ge(hB.filled, hB.at("moe1", k * 2 + 1))
                        act.sem_inc(hNT.freed, 1)
                        act.wait_ge(hWB.freed, hWB.at("moe1", k))
                        act.activation(wb[:, s, 0:BT], Bk[1][:, 0, :], ACT.Gelu, bias=w["b1c"][:, e, 2:3])
                        link.release(act.activation(wb[:, s, BT:], Bk[1][:, 1, :], ACT.Gelu, bias=w["b1c"][:, e, 3:4]),
                                     hWB.filled, hWB.at("moe1", k), hB.freed)

        @block.vector
        def _(v):
            link = Chain(v, dve_chain, dve_settled)

            def statistics(b):
                link.settle()
                for j in range(GB):
                    last = v.bn_stats(bn[:, j, :], x_tok[:, bass.ds(b * GB + j, 1), :].rearrange("p o d -> p (o d)"))
                link(last, settle=True)
                for j in range(GB):
                    last = v.bn_aggr(mv_b[:, j, :], bn[:, j, :])
                link(last)
                v.tensor_copy(mv[:, bass.ts(b, GB), :], mv_b[:, :, :]).then_inc(stats_done, 1)

            def normalise(stage, i, p, r=rstd, src=x_tok, sub=True):
                v.wait_ge(hXN.freed, hXN.at(stage, i * 2 + p))
                for j in range(GB):
                    tok = bass.ds(i * 8 + (4 * p + j), 1)
                    x_j = src[:, tok, :].rearrange("p o d -> p (o d)")
                    if sub:
                        last = v.tensor_scalar(xn_tm[:, p, j, :], x_j, mv[:, tok, 0], r[:, tok], ALU.subtract, ALU.mult)
                    else:
                        last = v.tensor_scalar(xn_tm[:, p, j, :], x_j, r[:, tok], None, ALU.mult)
                last.then_inc(hXN.filled, 1)

            def ln_wait(stage, i, p):
                v.wait_ge(rstd_done, i * 2 + (STAT[stage] + p + 1))

            v.wait_ge(x_loaded, 16 * NBLK)
            with link.loop(NBLK, 2) as b:
                statistics(b)
            v.wait_ge(w_loaded, W_LOADS)
            v.wait_ge(consts_ready, 2)
            v.wait_ge(masks_loaded, 32)
            v.tensor_scalar(keymask[:, :], km_i, 0.0, NEG, ALU.is_equal, ALU.mult).then_inc(keymask_ready, 1)
            link(v.tensor_scalar(fullmask[:, :, :], mask_i, 0.0, NEG, ALU.is_equal, ALU.mult))
            v.sem_inc(masks_ready, 1)

            def rope(stage, i, p, k, per, b0, b1):
                v.wait_ge(hB.filled, hB.at(stage, i * 2 + p))
                v.wait_ge(hFV.freed, hFV.at(stage, i * (2 * per) + k))
                s = hFV.slot(stage, k)
                for q, (bias, tab) in enumerate(((b0, "cos"), (b1, "sin"))):
                    last = v.scalar_tensor_tensor(
                        out=f[:, 2 * s + q, :].rearrange("p (b t) -> p b t", b=GB),
                        in0=Bk[p][:, q, :].rearrange("p (b t) -> p b t", b=GB), scalar=col[bias],
                        in1=w[tab][:, :].unsqueeze(1).broadcast_to([128, GB, S]), op0=ALU.add, op1=ALU.mult)
                link.release(last, hFV.filled, hFV.at(stage, i * (2 * per) + k), hB.freed)

            def values(stage, i, p, k, bias, ready):
                v.wait_ge(hA.filled, hA.at(stage, k))
                s = 0 if stage == "ctx" else p
                link.release(v.tensor_tensor(v0x[:, bass.ts(i * 2 + p, GB), :, 0:DH],
                                             A[s].rearrange("p (b h d) -> p b h d", b=GB, h=H),
                                             bias[:, :].rearrange("p (h d) -> p h d", h=H).unsqueeze(1)
                                             .broadcast_to([128, GB, H, DH]), ALU.add),
                             v0_ready, ready, hA.freed)

            with link.loop(NPAIR, 0) as i:
                for p in range(2):
                    rope("ctx", i, p, 2 * p, 2, "bk0", "bk0s")
                    values("ctx", i, p, i * 4 + 2 * p, bv0, i * 2 + (p + 1))
                    v.wait_ge(hFV.filled, i * 4 + (2 * p + 2))

            v.wait_ge(hFV.freed, hFV.at("sio", 1))
            with link.loop(NPAIR, 2) as i:
                for p in range(2):
                    ln_wait("sio", i, p)
                    for j in range(GB):
                        tok = bass.ds(i * 8 + (4 * p + j), 1)
                        v.tensor_scalar(y_tok[:, tok, :].rearrange("p o d -> p (o d)"),
                                        x_tok[:, tok, :].rearrange("p o d -> p (o d)"), mv[:, tok, 0], rstd[:, tok],
                                        ALU.subtract, ALU.mult)
                    normalise("sio", i, p, r=rr)
                for p in range(2):
                    n = i * 2 + p
                    v.wait_ge(hWB.filled, hWB.at("sio", n))
                    v.wait_ge(hWA.filled, hWA.at("sio", n))
                    link(v.tensor_tensor(f[:, p, :], wa[:, p, 0:BT], wa[:, p, BT:], ALU.mult))
                    v.wait_ge(hF45.freed, hF45.at("sio", n))
                    for j in range(GB):
                        c = slice(j * S, (j + 1) * S)
                        last = v.tensor_tensor_scan(f[:, 4 + p, c], wb[:, p, c], f[:, p, c], col["h0"],
                                                    ALU.mult, ALU.add)
                    link.release(last, hF45.filled, hF45.at("sio", n), hWA.freed)
                for p in range(2):
                    n = i * 2 + p
                    v.wait_ge(hU.filled, hU.at("sio", n))
                    v.sem_inc(hF45.freed, 1)
                    v.wait_ge(hOT.freed, hOT.at("sio", n))
                    link.release(v.scalar_tensor_tensor(out=oT[:, p, :], in0=U, scalar=col["b_y"], in1=wb[:, p, BT:],
                                                        op0=ALU.add, op1=ALU.mult),
                                 hOT.filled, hOT.at("sio", n), hU.freed, hWB.freed)
                for p in range(2):
                    n = i * 2 + p
                    v.wait_ge(hT.filled, hT.at("sio", i * 4 + (2 + p)))
                    v.sem_inc(hOT.freed, 1)
                    y_b = y_tok[:, bass.ts(n, GB), :].rearrange("p b d -> p (b d)")
                    link.release(v.tensor_tensor(y_b, y_b, T, ALU.add), x1_done, n + 1, hT.freed)

            def add_output(stage, n, k):
                v.wait_ge(hT.filled, hT.at(stage, k))
                v.sem_inc(hOT.freed, 1)
                x_b = x_tok[:, bass.ts(n, GB), :].rearrange("p b d -> p (b d)")
                link.release(v.tensor_tensor(x_b, x_b, T, ALU.add), hT.freed, hT.freed_at(stage, k))
                statistics(n)

            with link.loop(NPAIR, 4) as i:
                for p in range(2):
                    v.wait_ge(r2_done, i * 2 + (p + 1))
                    normalise("ffn", i, p, r=r2, src=y_tok, sub=False)
                for p in range(2):
                    for c in range(4):
                        k = 4 * p + c
                        v.wait_ge(hWA.filled, hWA.at("ffn", i * 8 + k))
                        v.wait_ge(hWB.freed, hWB.at("ffn", i * 8 + k))
                        link.release(v.scalar_tensor_tensor(out=wb[:, k % 2, 0:BT], in0=Bk[k % 2][:, 0, :],
                                                            scalar=col["b_fc%d" % c], in1=wa[:, k % 2, 0:BT],
                                                            op0=ALU.add, op1=ALU.mult),
                                     hWB.filled, hWB.at("ffn", i * 8 + k), hB.freed, hWA.freed)
                for p in range(2):
                    add_output("ffn", i * 2 + p, i * 4 + (2 + p))

            def query_stage(a):
                stage = "qp%d" % a
                with link.loop(NPAIR, 0 if a != 1 else SELECT_LINKS) as i:
                    for p in range(2):
                        ln_wait(stage, i, p)
                        normalise(stage, i, p)
                    for p in range(2):
                        if a == 0:
                            rope(stage, i, p, p, 1, "bq0", "bq0s")
                            v.sem_inc(hNT.freed, 1)
                        if a == 1:
                            values(stage, i, p, i * 2 + p, bv1, i * 2 + (NBLK + p + 1))
                            v.sem_inc(hNT.freed, 1)
                    if a == 1:
                        v.wait_ge(hU.filled, hU.at(stage, i))
                        v.sem_inc(hF45.freed, 2)
                        link(v.tensor_copy(qn[:, :], U[:, 0:S]), settle=True)
                        v.sem_inc(hU.freed, 1)
                        for _ in range(NTOP // 8):
                            link(v.max(top8[:, :], qn[:, :]), settle=True)
                            link(v.match_replace(qn[:, :], top8[:, :], qn[:, :], -1.0), settle=True)
                        link(v.tensor_scalar(sel[:, :], qn[:, :], 0.0, None, ALU.is_lt))
                        v.sem_inc(sel_ready, 1)
                        v.wait_ge(hT.filled, hT.at(stage, i * 4 + 2))
                        link(v.tensor_copy(selT[:, bass.ts(i, 8), :].rearrange("p b h -> p (b h)"), T[:, 0:S]))
                        v.sem_inc(hT.freed, 1)

            def attention(a):
                stage = "ac%d" % a

                def maxima(n, u):
                    j, g4 = u // 4, u % 4
                    v.wait_ge(hA.filled, hA.at(stage, n * 8 + u))
                    v.tensor_reduce(negm[:, g4 * 4:g4 * 4 + 4, j], A[u % 2].rearrange("p (h k) -> p h k", h=4),
                                    AX.X, ALU.max, negate=True).then_inc(hA.freed, 1)

                def m_parts(n):
                    v.wait_ge(hA.freed, hA.freed_at(stage, n * 8 + 7))
                    link(v.tensor_copy(mp[:, 0], negm[:, :, :]))
                    v.tensor_tensor(mp[:, 1], negm[:, :, :], mp[:, 0], ALU.subtract).then_inc(mp_ready, 1)

                def m_store(n, k):
                    v.wait_ge(hT.filled, hT.at(stage, k))
                    link.release(v.tensor_copy(mT[:, :], T.bitcast(bf16)[0:64, 0:S]),
                                 m_ready, n + (NSTEP * a + 1), hT.freed)

                def normalise_heads(n, j, kt):
                    k = n * 2 + j
                    v.wait_ge(hT.filled, hT.at(stage, kt))
                    v.sem_inc(hOW.freed, 1)
                    o = T.rearrange("p (h w) -> p h w", h=H)
                    link(v.reciprocal(rec[:, :].unsqueeze(2), o[:, :, DH:VC]))
                    if a == 1:
                        link(v.tensor_tensor(rec[:, :], rec[:, :],
                                             selT[:, bass.ds(k, 1), :].rearrange("p o h -> p (o h)"), ALU.mult))
                    v.wait_ge(hO.freed, hO.at(stage, k))
                    link.release(v.tensor_tensor(o_tok[:, j], o[:, :, 0:DH],
                                                 rec[:, :].unsqueeze(2).broadcast_to([128, H, DH]), ALU.mult),
                                 hO.filled, hO.at(stage, k), hT.freed)

                def step(n, before, do_a=True):
                    for op, u in STEP:
                        if op == "A" and do_a:
                            maxima(n + 1, u)
                        elif op == "P" and do_a:
                            m_parts(n + 1)
                        elif op == "E" and do_a:
                            m_store(n + 1, n * 5 + 3)
                        elif op == "N":
                            normalise_heads(n, u, n * 5 + 1)
                        elif op == "n" and before is not None:
                            normalise_heads(before, u, before * 5 + 4)

                nl = 2 if a == 1 else 1
                for u in range(8):
                    maxima(0, u)
                m_parts(0)
                m_store(0, 0)
                step(0, None)
                with link.loop((NSTEP - 2) // 3, 3 * (1 + 2 * nl)) as i:
                    for p in range(3):
                        step(i * 3 + (p + 1), i * 3 + p)
                step(NSTEP - 1, NSTEP - 2, do_a=False)
                normalise_heads(NSTEP - 1, 1, 5 * NSTEP - 2)

            def output_stage(a):
                stage = "po%d" % a
                with link.loop(NPAIR, 4) as i:
                    for p in range(2):
                        add_output(stage, i * 2 + p, i * 2 + p)

            SELECT_LINKS = 1 + 2 * (NTOP // 8) + 1 + 1
            query_stage(0)
            attention(0)
            output_stage(0)

            v.wait_ge(hFV.freed, hFV.at("moe0", 1))
            with link.loop(NPAIR, 2 * 10 + 2 + 4) as i:
                for p in range(2):
                    ln_wait("moe0", i, p)
                    normalise("moe0", i, p)
                for p in range(2):
                    n = i * 2 + p
                    v.wait_ge(hU.filled, hU.at("moe0", n))
                    link.release(v.tensor_tensor(rl[:, :, :], U[:, 0:GB * E0].rearrange("p (b e) -> p b e", b=GB),
                                                 rbias[:, :].unsqueeze(1).broadcast_to([128, GB, E0]), ALU.add),
                                 logits_ready, n + 1, hU.freed)
                    v.wait_ge(probs_ready, n + 1)
                    p_j = pr[:, :, :].unsqueeze(2).broadcast_to([128, GB, E0, E0])
                    p_e = pr[:, :, :].unsqueeze(3).broadcast_to([128, GB, E0, E0])
                    c1 = cmp1[:, :, :].rearrange("p (b e) j -> p b e j", b=GB)
                    c2 = cmp2[:, :, :].rearrange("p (b e) j -> p b e j", b=GB)
                    link(v.tensor_tensor(c1, p_j, p_e, ALU.is_gt))
                    link(v.tensor_tensor(c2, p_j, p_e, ALU.is_equal))
                    link(v.tensor_tensor(c2, c2, lower_e[:, :, :].unsqueeze(1).broadcast_to([128, GB, E0, E0]), ALU.mult))
                    link(v.tensor_tensor(c1, c1, c2, ALU.add))
                    rk2 = rk[:, :, :].rearrange("p b e -> p (b e)")
                    link(v.tensor_reduce(rk2, cmp1[:, :, :], AX.X, ALU.add))
                    link(v.tensor_scalar(rk2, rk2, float(TOPK) - 0.5, None, ALU.is_lt))
                    link(v.tensor_tensor(rk[:, :, :], rk[:, :, :], pr[:, :, :], ALU.mult))
                    link(v.tensor_reduce(wsum[:, :], rk[:, :, :], AX.X, ALU.add))
                    link(v.reciprocal(wsum[:, :], wsum[:, :]))
                    link(v.tensor_tensor(wr[:, p], rk[:, :, :], wsum[:, :].unsqueeze(2).broadcast_to([128, GB, E0]),
                                         ALU.mult))
                for p in range(2):
                    n = i * 2 + p
                    x_b = x_tok[:, bass.ts(n, GB), :].rearrange("p b d -> p (b d)")
                    for e in range(E0 + 2):
                        if e < E0 + 1:
                            k, s = i * 18 + (9 * p + e), (p + e) % 2
                            v.wait_ge(hWA.filled, hWA.at("moe0", k))
                            v.wait_ge(hB.filled, hB.at("moe0", k * 2 + 1))
                            if e == E0:
                                v.sem_inc(hNT.freed, 1)
                            v.wait_ge(hWB.freed, hWB.at("moe0", k))
                            link.release(v.tensor_tensor(wb[:, s, :], wa[:, s, :], BF[1], ALU.mult),
                                         hWB.filled, hWB.at("moe0", k), hB.freed, hWA.freed)
                        if e > 0:
                            k, s = i * 18 + (9 * p + e - 1), (p + e - 1) % 2
                            v.wait_ge(hA.filled, hA.at("moe0", k))
                            v.sem_inc(hWB.freed, 1)
                            if e == 1:
                                link(v.tensor_tensor(x_b, x_b, A[s], ALU.add))
                                v.sem_inc(hA.freed, 1)
                            else:
                                m = e - 2
                                v.wait_ge(scaled_used, n * E0 + (m + 1))
                                link.release(v.tensor_tensor(f[:, m % 2, :].rearrange("p (b d) -> p b d", b=GB),
                                                             A[s].rearrange("p (b d) -> p b d", b=GB),
                                                             wr[:, p, :, m:m + 1].broadcast_to([128, GB, D]), ALU.mult),
                                             scaled_ready, n * E0 + (m + 1), hA.freed)
                    v.wait_ge(scaled_used, n * E0 + (E0 + 2))
                    statistics(n)

            query_stage(1)
            attention(1)
            output_stage(1)
            query_stage(2)
            attention(2)
            output_stage(2)

            v.wait_ge(hFV.freed, hFV.at("aff", 1))
            v.wait_ge(route_pe, 1)
            link(v.tensor_copy(wn[:, :], U[:, 0:E1]))
            v.sem_inc(wn_raw, 1)
            with link.loop(NPAIR, 0) as i:
                for p in range(2):
                    ln_wait("aff", i, p)
                    normalise("aff", i, p)
                for p in range(2):
                    n = i * 2 + p
                    v.wait_ge(hU.filled, hU.at("aff", n))
                    v.sem_inc(hNT.freed, 1)
                    link.release(v.tensor_copy(num[:, bass.ts(n, GB), :].rearrange("p b e -> p (b e)"), U[:, 0:GB * E1]),
                                 num_ready, n + 1, hU.freed)
            v.wait_ge(wn_ready, 1)
            v.wait_ge(xnorm_ready, 1)
            be = [128, B, E1]
            link(v.tensor_tensor(a1[:, :, :], xnorm[:, :].unsqueeze(2).broadcast_to(be),
                                 wn[:, :].unsqueeze(1).broadcast_to(be), ALU.mult))
            link(v.tensor_scalar(a1[:, :, :], a1[:, :, :], 1e-9, None, ALU.add))
            link(v.reciprocal(a1[:, :, :], a1[:, :, :]))
            link(v.tensor_tensor(aff[:, :, :], num[:, :, :], a1[:, :, :], ALU.mult))
            v.tensor_reduce(asum[:, :], aff[:, :, :].rearrange("p b e -> p (b e)"), AX.X, ALU.add).then_inc(asum_ready, 1)
            link(v.tensor_reduce(own[:, :], aff[:, :, :], AX.X, ALU.max))
            own_b = own[:, :].unsqueeze(2).broadcast_to(be)
            link(v.tensor_tensor(oh[:, :, :], aff[:, :, :], own_b, ALU.is_equal))
            link(v.tensor_tensor(oh[:, :, :], oh[:, :, :], rev[:, :].unsqueeze(1).broadcast_to(be), ALU.mult))
            link(v.tensor_reduce(mx[:, :], oh[:, :, :], AX.X, ALU.max))
            link(v.tensor_tensor(oh[:, :, :], oh[:, :, :], mx[:, :].unsqueeze(2).broadcast_to(be), ALU.is_equal))
            v.sem_inc(aff_ready, 1)
            v.wait_ge(hT.filled, hT.at("route", 0))
            link(v.tensor_copy(affT[:, :], T[:, 0:S]))
            v.sem_inc(hT.freed, 1)
            v.wait_ge(hT.filled, hT.at("route", 1))
            link(v.tensor_copy(ohT[:, :], T[:, 0:S]))
            v.sem_inc(hT.freed, 1)
            link(v.tensor_tensor(aff_rows, affT[:, :].unsqueeze(1).broadcast_to([128, B, S]),
                                 batch_rows[:, :].unsqueeze(2).broadcast_to([128, B, S]), ALU.mult))
            v.sem_inc(affrows_ready, 1)
            v.wait_ge(cap_ready, 1)
            link(v.tensor_scalar(capv[:, :], capv[:, :], float(CAP_S), float(MIN_CAP), ALU.mult, ALU.max))
            link(v.tensor_scalar(capv[:, :], capv[:, :], float(CAP_S), None, ALU.min))
            for c in range(NBLK):
                if c % 2 == 0:
                    v.wait_ge(hB.filled, hB.at("route", c // 2))
                G = Bk[c // 2][:, c % 2, :].rearrange("p (b s) -> p b s", b=GB)
                g1 = f[:, 0, :].rearrange("p (b s) -> p b s", b=GB)
                g2 = f[:, 1, :].rearrange("p (b s) -> p b s", b=GB)
                own_c = own[:, c * GB:(c + 1) * GB].unsqueeze(2).broadcast_to([128, GB, S])
                link(v.tensor_tensor(g1, G, own_c, ALU.is_gt))
                link(v.tensor_tensor(g2, G, own_c, ALU.is_equal))
                if c % 2 == 1:
                    v.sem_inc(hB.freed, 1)
                link(v.tensor_tensor(g2, g2, earlier[:, :].unsqueeze(1).broadcast_to([128, GB, S]), ALU.mult))
                link(v.tensor_tensor(g1, g1, g2, ALU.add))
                link(v.tensor_reduce(rank[:, c * GB:(c + 1) * GB], g1, AX.X, ALU.add))
            link(v.tensor_scalar(rank[:, :], rank[:, :], 1.0, capv[:, 0:1], ALU.add, ALU.is_le))
            link(v.tensor_tensor(a1[:, :, :].rearrange("p b e -> p (b e)").rearrange("p (e b) -> p e b", e=E1),
                                 oh[:, :, :].rearrange("p b e -> p e b"),
                                 rank[:, :].unsqueeze(1).broadcast_to([128, E1, B]), ALU.mult))
            v.sem_inc(disp_ready, 1)
            v.wait_ge(hT.filled, hT.at("route", 2))
            link(v.tensor_copy(dT[:, :], T[:, 0:S]))
            v.sem_inc(dT_ready, 1)
            v.sem_inc(hT.freed, 1)
            v.wait_ge(route_pe, 3)
            link(v.tensor_copy(b2s[:, :], U[:, 0:D]))

            v.wait_ge(disp_loaded, 16 * E1)
            with link.loop(NPAIR, 2) as i:
                for p in range(2):
                    n = i * 2 + p
                    for e in range(E1):
                        k = i * 16 + (8 * p + e)
                        v.wait_ge(hNT.freed, hNT.at("moe1", k))
                        m_e = stack[:, e // 2, (e % 2) * B * S:(e % 2 + 1) * B * S]
                        link.release(v.tensor_tensor(nT[:, e % 2, :],
                                                     attnT[:, bass.ts(n, GB), :].rearrange("p b t -> p (b t)"),
                                                     m_e[:, bass.ts(n, BT)], ALU.mult),
                                     hNT.filled, hNT.at("moe1", k))
                    x_b = blk(x_tok, n)
                    v.wait_ge(hA.filled, hA.at("moe1", n))
                    v.sem_inc(hWA.freed, 1)
                    v.sem_inc(hWB.freed, 1)
                    link(v.tensor_tensor(x_b, x_b, A[p].rearrange("p (b d) -> p b d", b=GB), ALU.add))
                    v.sem_inc(hA.freed, 1)
                    v.tensor_tensor(x_b, x_b, b2s[:, :].unsqueeze(1).broadcast_to([128, GB, D]), ALU.add)\
                     .then_inc(x_done, 1)

        @block.tensor
        def _(pe):
            mm, tr = nc.tensor.matmul, nc.tensor.transpose
            pe.wait_ge(consts_ready, 2)
            pe.wait_ge(w_loaded, W_LOADS)

            def all_free(stage, *all_rings):
                for r in all_rings:
                    pe.wait_ge(r.freed, r.at(stage, r.depth - 1))

            def transposes(stage, k, src):
                pe.wait_ge(hT.freed, hT.at(stage, k))
                for j in range(GB):
                    last = tr(T[:, j * S:(j + 1) * S], src(j), ident[:, :])
                last.then_inc(hT.filled, 1)

            def normalised(stage, i, k, p):
                pe.wait_ge(hXN.filled, hXN.at(stage, i * 2 + p))
                transposes(stage, k, lambda j: xn_tm[:, p, j, :])

            def back(stage, i, k, p):
                pe.wait_ge(hOT.filled, hOT.at(stage, i * 2 + p))
                transposes(stage, k, lambda j: oT[:, p, j * S:(j + 1) * S])

            def tokens_out(bank, p, wt, n_out, last_sem):
                for j in range(GB):
                    last = mm(bank[:, j * n_out:(j + 1) * n_out], nT[:, p, j * S:(j + 1) * S], wt, start=True, stop=True)
                last.then_inc(last_sem, 1)

            with pe.Fori(0, NPAIR) as i:
                for p in range(2):
                    normalised("ctx", i, i * 2 + p, p)
                for p in range(2):
                    n = i * 2 + p
                    pe.wait_ge(hNT.filled, hNT.at("ctx", n))
                    pe.wait_ge(hB.freed, hB.at("ctx", n))
                    mm(Bk[p][:, 0, :], w["wk0"][:, :], nT[:, p, :], start=True, stop=True)
                    mm(Bk[p][:, 1, :], w["wk0s"][:, :], nT[:, p, :], start=True, stop=True).then_inc(hB.filled, 1)
                    pe.wait_ge(hA.freed, hA.at("ctx", n * 2 + 1))
                    tokens_out(A[0], p, w["wv0"][:, :], D, hA.filled)
                    tokens_out(A[1], p, w["wv2"][:, :], D, hA.filled)
                    pe.wait_ge(hU.freed, hU.at("ctx", n))
                    mm(U, w["wk2"][:, :], nT[:, p, :], start=True, stop=True).then_inc(hU.filled, 1)

            all_free("sio", hA, hB)
            with pe.Fori(0, NPAIR) as i:
                for p in range(2):
                    normalised("sio", i, i * 4 + p, p)
                for p in range(2):
                    n = i * 2 + p
                    pe.wait_ge(hNT.filled, hNT.at("sio", n))
                    pe.wait_ge(hB.freed, hB.at("sio", n))
                    mm(Bk[p][:, 0, :], w["wz"][:, :], nT[:, p, :], start=True, stop=True)
                    mm(Bk[p][:, 1, :], w["wdt"][:, :], nT[:, p, :], start=True, stop=True).then_inc(hB.filled, 1)
                    pe.wait_ge(hA.freed, hA.at("sio", n))
                    mm(A[p], w["wya"][:, :], nT[:, p, :], start=True, stop=True).then_inc(hA.filled, 1)
                for p in range(2):
                    n = i * 2 + p
                    pe.wait_ge(hF45.filled, hF45.at("sio", n))
                    pe.wait_ge(hU.freed, hU.at("sio", n))
                    mm(U, w["wy"][:, :], f[:, 4 + p, :], start=True, stop=True).then_inc(hU.filled, 1)
                for p in range(2):
                    back("sio", i, i * 4 + (2 + p), p)

            all_free("ffn", hA, hB)
            with pe.Fori(0, NPAIR) as i:
                for p in range(2):
                    normalised("ffn", i, i * 4 + p, p)
                for p in range(2):
                    pe.wait_ge(hNT.filled, hNT.at("ffn", i * 2 + p))
                    for c in range(5):
                        if c < 4:
                            k = 4 * p + c
                            pe.wait_ge(hB.freed, hB.at("ffn", i * 8 + k))
                            fs = slice(c * 128, (c + 1) * 128)
                            mm(Bk[k % 2][:, 0, :], w["wfc"][:, fs], nT[:, p, :], start=True, stop=True)
                            mm(Bk[k % 2][:, 1, :], w["wfa"][:, fs], nT[:, p, :], start=True, stop=True)\
                              .then_inc(hB.filled, 1)
                        if c > 0:
                            k = 4 * p + c - 1
                            pe.wait_ge(hWB.filled, hWB.at("ffn", i * 8 + k))
                            if c == 1:
                                pe.wait_ge(hA.freed, hA.at("ffn", i * 2 + p))
                            mm(A[p], w["wout"][:, c - 1, :], wb[:, k % 2, 0:BT], start=(c == 1), stop=(c == 4))\
                              .then_inc(hWB.freed if c < 4 else hA.filled, 1)
                for p in range(2):
                    back("ffn", i, i * 4 + (2 + p), p)

            def query_stage(a):
                stage = "qp%d" % a
                all_free(stage, hB)
                with pe.Fori(0, NPAIR) as i:
                    for p in range(2):
                        normalised(stage, i, i * (4 if a == 1 else 2) + p, p)
                    for p in range(2):
                        n = i * 2 + p
                        pe.wait_ge(hNT.filled, hNT.at(stage, n))
                        pe.wait_ge(hB.freed, hB.at(stage, n))
                        names = (("wq0", "wq0s"), ("wq1", "wk1"), ("wq2",))[a]
                        for q, name in enumerate(names):
                            last = mm(Bk[p][:, q, :], w[name][:, :], nT[:, p, :], start=True, stop=True)
                        last.then_inc(hB.filled, 1)
                        if a == 1:
                            pe.wait_ge(hA.freed, hA.at(stage, n))
                            tokens_out(A[p], p, w["wv1"][:, :], D, hA.filled)
                    if a == 1:
                        pe.wait_ge(hU.freed, hU.at(stage, i))
                        for b in range(8):
                            if b % 4 == 0:
                                pe.wait_ge(hF45.filled, hF45.at(stage, i * 2 + b // 4))
                            last = mm(U[:, 0:S], head_cols[:, (7 - b) * H:(15 - b) * H],
                                      f[:, 4 + b // 4, (b % 4) * S:(b % 4 + 1) * S], start=(b == 0), stop=(b == 7))
                        last.then_inc(hU.filled, 1)
                        pe.wait_ge(sel_ready, i + 1)
                        pe.wait_ge(hT.freed, hT.at(stage, i * 4 + 2))
                        tr(T[:, 0:S], sel[:, :], ident[:, :]).then_inc(hT.filled, 1)
                        pe.wait_ge(hT.freed, hT.at(stage, i * 4 + 3))
                        pe.sem_inc(hT.filled, 1)
                        pe.sem_inc(hT.freed, 1)

            def attention(a):
                stage = "ac%d" % a

                LOAD = 16 * (NPART + 3)

                def scores(n, u, s, m):
                    j, g4 = u // 4, u % 4
                    if u == 0:
                        pe.wait_ge(stack_loaded[s], m * LOAD + (len(range(s, NSTEP, 3)) * a + 1) * LOAD)
                    pe.wait_ge(hA.freed, hA.at(stage, n * 8 + u))
                    bank = A[u % 2]
                    if a == 1:
                        mm(bank, identb[:, :], causal[:, :].unsqueeze(1).broadcast_to([128, 4, S]), start=True, stop=False,
                           skip_group_check=True)
                    if a == 2:
                        mm(bank, identb[:, :], fullmask[:, bass.ds(n * 2 + j, 1), :].broadcast_to([128, 4, S]),
                           start=True, stop=False, skip_group_check=True)
                    for q in range(4):
                        h = g4 * 4 + q
                        last = mm(bank[:, q * S:(q + 1) * S], qst[s][:, h, j * S:(j + 1) * S],
                                  kst[s][:, h, j * S:(j + 1) * S], start=(a == 0), stop=True, skip_group_check=(a != 0))
                    last.then_inc(hA.filled, 1)

                def scores_T(n, u, s):
                    j, hh = u // 2, u % 2
                    if u == 0:
                        pe.wait_ge(m_stored, n * 32 + 32 * (NSTEP * a + 1))
                    pe.wait_ge(hB.freed, hB.at(stage, n * 4 + u))
                    for half in range(2):
                        bank = Bk[u % 2][:, half, :]
                        if a == 1:
                            mm(bank, causal[:, :], identb[:, :].unsqueeze(1).broadcast_to([128, 4, S]), start=True,
                               stop=False, skip_group_check=True)
                        if a == 2:
                            mm(bank, fullmask[:, bass.ds(n * 2 + j, 1), :].rearrange("p o k -> p (o k)"),
                               identb[:, :].unsqueeze(1).broadcast_to([128, 4, S]), start=True,
                               stop=False, skip_group_check=True)
                        for q in range(4):
                            h = hh * 8 + half * 4 + q
                            last = mm(bank[:, q * S:(q + 1) * S], kst[s][:, h, j * S:(j + 1) * S],
                                      qst[s][:, h, j * S:(j + 1) * S], start=(a == 0), stop=True,
                                      skip_group_check=(a != 0))
                    last.then_inc(hB.filled, 1)

                def values_sum(n, u):
                    j, hh = u // 2, u % 2
                    pe.wait_ge(hWA.filled, hWA.at(stage, n * 4 + u))
                    if hh == 0:
                        pe.wait_ge(hVB.filled, hVB.at(stage, n * 2 + j))
                        pe.wait_ge(hU.freed, hU.at(stage, n * 2 + j))
                    for q in range(8):
                        h = hh * 8 + q
                        rows, cols = slice(h % 4 * 32, h % 4 * 32 + 32), slice(h // 4 * S, (h // 4 + 1) * S)
                        last = mm(U[rows, cols], v_batch[j][:, h * VC:h * VC + 32], wa[:, u % 2, q * S:(q + 1) * S],
                                  start=True, stop=True)
                    last.then_inc(hU.filled if hh else hWA.freed, 1)

                def m_rows(n, k):
                    pe.wait_ge(mp_ready, n + (NSTEP * a + 1))
                    pe.wait_ge(hT.freed, hT.at(stage, k))
                    pe.sem_inc(pe_settled, 1)
                    tr(T.bitcast(bf16)[0:64, 0:S], mp[:, :, :, :].rearrange("p l h j -> p (l h j)"), identb[:, :])\
                      .then_inc(hT.filled, 1)

                def products_T(n, j, k):
                    pe.wait_ge(hOW.filled, hOW.at(stage, n * 2 + j))
                    transposes(stage, k, lambda c: o_wide[:, c * S:(c + 1) * S])

                def out_rows(n, j, k):
                    pe.wait_ge(hO.filled, hO.at(stage, n * 2 + j))
                    pe.wait_ge(hT.freed, hT.at(stage, k))
                    tr(T[:, 0:S], o_tok[:, j].rearrange("p h d -> p (h d)"), ident[:, :]).then_inc(hT.filled, 1)

                def step(n, before, p, m, do_a=True):
                    for op, u in STEP:
                        if op == "A" and do_a:
                            scores(n + 1, u, (p + 1) % 3, m + (p + 1) // 3)
                        elif op == "B":
                            scores_T(n, u, p)
                        elif op == "V":
                            values_sum(n, u)
                        elif op == "v" and before is not None:
                            values_sum(before, u)
                        elif op == "M" and do_a:
                            m_rows(n + 1, n * 5 + 3)
                        elif op == "X":
                            products_T(n, u, n * 5 + 1)
                        elif op == "x" and before is not None:
                            products_T(before, u, before * 5 + 4)
                        elif op == "O":
                            out_rows(n, u, n * 5 + 2)
                        elif op == "o" and before is not None:
                            out_rows(before, u, before * 5 + 5)

                pe.wait_ge(masks_ready, 1)
                all_free(stage, hA, hB)
                for u in range(8):
                    scores(0, u, 0, 0)
                m_rows(0, 0)
                step(0, None, 0, 0)
                with pe.Fori(0, (NSTEP - 2) // 3) as i:
                    for p in range(3):
                        step(i * 3 + (p + 1), i * 3 + p, (p + 1) % 3, i + (p + 1) // 3)
                step(NSTEP - 1, NSTEP - 2, (NSTEP - 1) % 3, (NSTEP - 1) // 3, do_a=False)
                values_sum(NSTEP - 1, 3)
                products_T(NSTEP - 1, 1, 5 * NSTEP - 2)
                out_rows(NSTEP - 1, 1, 5 * NSTEP - 1)

            def output_stage(a):
                stage = "po%d" % a
                all_free(stage, hB)
                with pe.Fori(0, NPAIR) as i:
                    for p in range(2):
                        n = i * 2 + p
                        pe.wait_ge(attnT_done, n * GB + (B * a + GB))
                        pe.wait_ge(hB.freed, hB.at(stage, n))
                        mm(Bk[p][:, 0, :], w["wo%d" % a][:, :],
                           attnT[:, bass.ts(n, GB), :].rearrange("p b t -> p (b t)"), start=True, stop=True)\
                          .then_inc(hB.filled, 1)
                    for p in range(2):
                        back(stage, i, i * 2 + p, p)

            query_stage(0)
            attention(0)
            output_stage(0)

            with pe.Fori(0, NPAIR) as i:
                for p in range(2):
                    normalised("moe0", i, i * 2 + p, p)
                for p in range(2):
                    n = i * 2 + p
                    pe.wait_ge(hNT.filled, hNT.at("moe0", n))
                    pe.wait_ge(hU.freed, hU.at("moe0", n))
                    tokens_out(U, p, w["router"][:, :], E0, hU.filled)
                for p in range(2):
                    for e in range(E0 + 2):
                        if e < E0 + 1:
                            k = i * 18 + (9 * p + e)
                            pe.wait_ge(hB.freed, hB.at("moe0", k * 2 + 1))
                            for q, name in enumerate(("gate", "up")):
                                for c in range(2):
                                    last = mm(Bk[q][:, c, :], w[name][:, e, c * 128:(c + 1) * 128], nT[:, p, :],
                                              start=True, stop=True)
                                last.then_inc(hB.filled, 1)
                        if e > 0:
                            k, s = i * 18 + (9 * p + e - 1), (p + e - 1) % 2
                            pe.wait_ge(hWB.filled, hWB.at("moe0", k))
                            pe.wait_ge(hA.freed, hA.at("moe0", k))
                            for j in range(GB):
                                for c in range(2):
                                    last = mm(A[s][:, j * D:(j + 1) * D],
                                              wb[:, s, c * BT + j * S:c * BT + (j + 1) * S],
                                              w["down"][:, e - 1, c, :], start=(c == 0), stop=(c == 1))
                            last.then_inc(hA.filled, 1)

            query_stage(1)
            attention(1)
            output_stage(1)
            query_stage(2)
            attention(2)
            output_stage(2)

            pe.wait_ge(waff_sq, 1)
            pe.wait_ge(hU.freed, hU.at("aff", 0))
            mm(U[:, 0:E1], ones[:, :], a1[:, 0, :], start=True, stop=True).then_inc(route_pe, 1)
            pe.wait_ge(wn_raw, 1)
            with pe.Fori(0, NPAIR) as i:
                for p in range(2):
                    pe.wait_ge(ssq_done, i * 8 + (B + 4 * p + 4))
                    normalised("aff", i, i * 2 + p, p)
                for p in range(2):
                    n = i * 2 + p
                    pe.wait_ge(hNT.filled, hNT.at("aff", n))
                    pe.wait_ge(hU.freed, hU.at("aff", n))
                    tokens_out(U, p, w["waff"][:, :], E1, hU.filled)
            pe.wait_ge(asum_ready, 1)
            pe.wait_ge(hU.freed, hU.at("route", 0))
            mm(U[:, 0:1], ones[:, :], asum[:, :], start=True, stop=True).then_inc(route_pe, 1)
            pe.wait_ge(aff_ready, 1)
            for k, src in enumerate((aff, oh)):
                pe.wait_ge(hT.freed, hT.at("route", k))
                tr(T[:, 0:S], src[:, :, :].rearrange("p b e -> p (b e)"), ident[:, :]).then_inc(hT.filled, 1)
            pe.wait_ge(affrows_ready, 1)
            for c in range(NBLK):
                if c % 2 == 0:
                    pe.wait_ge(hB.freed, hB.at("route", c // 2))
                last = mm(Bk[c // 2][:, c % 2, :], ohT[:, :], aff_rows[:, c * GB:(c + 1) * GB, :], start=True, stop=True)
                if c % 2:
                    last.then_inc(hB.filled, 1)
            pe.wait_ge(cap_ready, 1)
            mm(U[:, 0:D], ones[0:E1, :], w["b2r"][:, :], start=True, stop=True).then_inc(route_pe, 1)
            pe.wait_ge(disp_ready, 1)
            pe.wait_ge(hT.freed, hT.at("route", 2))
            tr(T[:, 0:S], a1[:, :, :].rearrange("p b e -> p (b e)"), ident[:, :]).then_inc(hT.filled, 1)

            with pe.Fori(0, NPAIR) as i:
                for p in range(2):
                    n = i * 2 + p
                    for e in range(E1 + 1):
                        if e < E1:
                            k = i * 16 + (8 * p + e)
                            pe.wait_ge(hNT.filled, hNT.at("moe1", k))
                            for q in range(2):
                                pe.wait_ge(hB.freed, hB.at("moe1", k * 2 + q))
                                for c in range(2):
                                    f0 = (2 * q + c) * 128
                                    last = mm(Bk[q][:, c, :], w["w1"][:, e, f0:f0 + 128], nT[:, e % 2, :],
                                              start=True, stop=True)
                                last.then_inc(hB.filled, 1)
                        if e > 0:
                            k, s = i * 16 + (8 * p + e - 1), (e - 1) % 2
                            pe.wait_ge(hWA.filled, hWA.at("moe1", k))
                            pe.wait_ge(hWB.filled, hWB.at("moe1", k))
                            if e == 1:
                                pe.wait_ge(hA.freed, hA.at("moe1", n))
                            for c in range(4):
                                src = (wa, wb)[c // 2]
                                for j in range(GB):
                                    c0 = (c % 2) * BT + j * S
                                    first = e == 1 and c == 0 and j == 0
                                    last = mm(A[p][:, j * D:(j + 1) * D], src[:, s, c0:c0 + S],
                                              w["w2"][:, e - 1, c, :], start=first, stop=(e == E1 and c == 3),
                                              skip_group_check=True)
                                if c == 1 and e < E1:
                                    last.then_inc(hWA.freed, 1)
                            last.then_inc(hWB.freed if e < E1 else hA.filled, 1)


STEP = [("A", 0), ("A", 1), ("v", 3), ("k", 1), ("B", 0), ("A", 2), ("A", 3), ("x", 1), ("n", 1), ("B", 1), ("V", 0),
        ("o", 1), ("A", 4), ("A", 5), ("B", 2), ("V", 1), ("K", 0), ("A", 6), ("A", 7), ("P", 0), ("X", 0), ("N", 0),
        ("B", 3), ("V", 2), ("O", 0), ("M", 0), ("E", 0)]


def kernel(**inputs):
    import numpy as np
    import concourse.bacc as bacc
    from concourse import mybir as mb
    from concourse.bass_utils import run_bass_kernel_spmd as run

    z = {k: np.asarray(v) for k, v in inputs.items()}
    feat = np.arange(D).reshape(H, DH).T.reshape(-1)
    partner = (np.arange(D).reshape(H, DH // 2, 2)[:, :, ::-1]).reshape(H, DH).T.reshape(-1)

    theta = (np.float32(1.0) / np.power(np.float32(10000.0), np.arange(0, DH, 2, dtype=np.float32) / np.float32(DH)))
    ang = np.arange(S, dtype=np.float32)[:, None] * theta.astype(np.float32)[None, :]
    cos = np.repeat(np.cos(ang).astype(np.float32).T, 2, axis=0)
    sin = np.repeat(np.sin(ang).astype(np.float32).T, 2, axis=0)
    sign = np.where(np.arange(DH) % 2 == 0, np.float32(-1), np.float32(1))[:, None]
    cos = np.repeat(cos, H, axis=0)
    sin = np.repeat(sin * sign, H, axis=0)

    a = {"x": z["x"], "ctx": z["ctx_1024"], "maskk": z["mask_Bx1xS2_if1"], "maskf": z["mask_Bx1xSxS2_if1"],
         "cos": cos, "sin": sin}
    L0 = lambda n: z["L0_attn_" + n]
    a.update(wz=L0("w_ln_z").T, wdt=L0("w_dt").T, wya=L0("w_yact").T, wy=L0("w_y").T, wfc=L0("w_fc").T,
             wfa=L0("w_fcact").T, wout=L0("w_out").T.reshape(4, 128, D).transpose(1, 0, 2))
    X0, A1, X1 = (lambda n: z["L0_xattn_" + n]), (lambda n: z["L1_attn_" + n]), (lambda n: z["L1_xattn_" + n])
    a.update(wq0=X0("Wq")[:, feat], wq0s=X0("Wq")[:, partner], wk0=X0("Wk")[:, feat], wk0s=X0("Wk")[:, partner],
             wv0=X0("Wv"), wo0=X0("Wo"), wq1=A1("Wq")[:, feat], wk1=A1("Wk")[:, feat], wv1=A1("Wv"), wo1=A1("Wo"),
             wq2=X1("Wq").T[:, feat], wk2=X1("Wk").T[:, feat], wv2=X1("Wv").T, wo2=X1("Wo").T)
    M0, M1 = (lambda n: z["L0_ffn_" + n]), (lambda n: z["L1_ffn_" + n])
    a.update(gate=np.concatenate([M0("shared_gate").T[None], M0("gate_w")]).transpose(1, 0, 2),
             up=np.concatenate([M0("shared_up").T[None], M0("up_w")]).transpose(1, 0, 2),
             down=np.concatenate([M0("shared_down").T[None], M0("down_w")]).reshape(E0 + 1, 2, 128, D)
             .transpose(2, 0, 1, 3),
             router=M0("router_w").T, waff=M1("waff").T, w1=M1("W1").transpose(1, 0, 2),
             w2=M1("W2").reshape(E1, 4, 128, D).transpose(2, 0, 1, 3),
             b1c=M1("b1").reshape(E1, 4, 128).transpose(2, 0, 1), b2r=M1("b2"))
    a.update(bv0=X0("bv"), bv1=A1("bv"), rbias=M0("routing_bias"), thr=M1("affinity_threshold").reshape(1))
    vec = {"b_z": L0("b_ln_z"), "b_dt": L0("b_dt"), "b_y": L0("b_y"), "b_ya": L0("b_yact"), "h0": L0("h0"),
           "g_sio": L0("g_sio"), "g_ffn": L0("g_ffn"), "b_out": L0("b_out"), "bq0": X0("bq")[feat],
           "bq0s": X0("bq")[partner], "bk0": X0("bk")[feat], "bk0s": X0("bk")[partner], "bo0": X0("bo"),
           "bq1": A1("bq")[feat], "bk1": A1("bk")[feat], "bo1": A1("bo"), "bo2": X1("bo")}
    for c in range(4):
        vec["b_fc%d" % c] = L0("b_fc")[c * 128:(c + 1) * 128]
        vec["b_fa%d" % c] = L0("b_fcact")[c * 128:(c + 1) * 128]
    a["cols"] = np.stack([vec[n] for n in COLS], axis=1)

    nc = bacc.Bacc("TRN2", target_bir_lowering=False, num_devices=1)
    arrays, aps = {}, {}
    for name, v in a.items():
        v = np.ascontiguousarray(v)
        arrays["in_" + name] = v
        aps[name] = nc.dram_tensor("in_" + name, v.shape, mb.dt.from_np(v.dtype), kind="ExternalInput").ap()
    aps["out"] = nc.dram_tensor("out_x", (B, S, D), mb.dt.float32, kind="ExternalOutput").ap()
    program(nc, aps)
    return run(nc, [arrays], core_ids=[0]).results[0]["out_x"]
```

```python
import concourse.bass as bass
from concourse import mybir
from contextlib import ExitStack, contextmanager

B, S, D, H = 16, 128, 128, 16
DH = D // H
NBLK = 4
GB = B // NBLK
BT = GB * S
NPAIR = NBLK // 2
NSTEP = 8
SB = B // NSTEP
ST = SB * S
FF0, I0, E0, TOPK = 512, 256, 8, 2
FF1, E1 = 512, 8
CAP_S, MIN_CAP = 256, 4
NTOP = 24
NPART = 3
ROW_M = NPART * NPART * DH
ROW_MASK = ROW_M + 2
NEG = -1.0e30
NT = B + E1
SCALE = float(DH) ** -0.5
LN_EPS, RMS_EPS = 1e-5, 1e-6
VC = DH + 1

STAGES = ["ctx", "sio", "ffn", "qp0", "ac0", "po0", "moe0", "qp1", "ac1", "po1", "qp2", "ac2", "po2",
          "aff", "route", "moe1"]

COLS = ["b_z", "b_dt", "b_y", "b_ya", "h0", "g_sio", "g_ffn", "b_out", "bq0", "bq0s", "bk0", "bk0s", "bo0",
        "bq1", "bk1", "bo1", "bo2"] + [f"b_fc{c}" for c in range(4)] + [f"b_fa{c}" for c in range(4)]


class Handoff:

    def __init__(self, sem, name, depth, uses, unit=1):
        self.filled, self.freed, self.depth = sem(name + "_filled"), sem(name + "_freed"), depth
        self.base, n, self.unit = {}, 0, unit
        for s in STAGES:
            self.base[s] = n
            n += uses.get(s, 0)

    def at(self, stage, k):
        return self.base[stage] + k + 1

    def free(self, stage, k):
        return k * self.unit + (self.base[stage] + 1) * self.unit

    def freed_at(self, stage, k):
        return self.base[stage] + k + 1 + self.depth

    def slot(self, stage, k):
        return (self.base[stage] + k) % self.depth


class Chain:

    def __init__(self, eng, sem, settled=None):
        self.eng, self.sem, self.base, self.k, self.settled = eng, sem, 0, 0, settled

    def settle(self):
        self.eng.sem_inc(self.settled, 1)

    def release(self, ins, filled, value, *freed):
        ins.then_inc(filled, 1)
        self.eng.wait_ge(filled, value)
        for r in freed:
            self.eng.sem_inc(r, 1)

    def __call__(self, ins, settle=False):
        ins.then_inc(self.sem, 1)
        self.k += 1
        self.eng.wait_ge(self.sem, self.base + self.k)
        if settle:
            self.settle()

    @contextmanager
    def loop(self, count, per):
        start = self.base + self.k
        with self.eng.Fori(0, count) as i:
            self.base, self.k = i * per + start, 0
            yield i
            assert self.k == per, (self.k, per)
        self.base, self.k = start + count * per, 0


def program(nc, t):
    f32, bf16, i32 = mybir.dt.float32, mybir.dt.bfloat16, mybir.dt.int32
    ALU, ACT, AX = mybir.AluOpType, mybir.ActivationFunctionType, mybir.AxisListType

    with ExitStack() as ctx:
        def sb(name, shape, dt=f32):
            return ctx.enter_context(nc.sbuf_tensor(name, shape, dt))

        def sem(name):
            return ctx.enter_context(nc.semaphore(name))

        q_scr = nc.dram_tensor("q_scr", (3, NSTEP, NPART, D, ST), bf16, kind="Internal").ap()
        k_scr = nc.dram_tensor("k_scr", (3, NSTEP, NPART, D, ST), bf16, kind="Internal").ap()
        keymask_scr = nc.dram_tensor("keymask_scr", (B, S), bf16, kind="Internal").ap()
        xs_scr = nc.dram_tensor("xs_scr", ((NT + B) * S, D), f32, kind="Internal").ap()
        ys_scr = nc.dram_tensor("ys_scr", ((NT + B) * S, D), f32, kind="Internal").ap()

        x_tok = sb("x_tok", [128, B, D])
        y_tok = sb("y_tok", [128, B, D])
        w = {n: sb("w_" + n, list(t[n].shape)) for n in
             ("wz", "wdt", "wya", "wy", "wfc", "wfa", "wout", "wq0", "wq0s", "wk0", "wk0s", "wv0", "wo0",
              "wq1", "wk1", "wv1", "wo1", "wq2", "wk2", "wv2", "wo2", "gate", "up", "down", "router", "waff",
              "w1", "w2", "b1c", "b2r", "cols", "cos", "sin")}
        bv0 = sb("bv0", [128, D]); bv1 = sb("bv1", [128, D]); rbias = sb("rbias", [128, E0]); thr = sb("thr", [128, 1])
        col = {n: w["cols"][:, i:i + 1] for i, n in enumerate(COLS)}
        negbdt = sb("negbdt", [128, 1])

        ident = sb("ident", [128, 128]); identb = sb("identb", [128, 128], bf16)
        causal = sb("causal", [128, 128], bf16)
        fullmask = sb("fullmask", [128, B, S], bf16)
        earlier = sb("earlier", [128, S])
        lower_e = sb("lower_e", [128, E0, E0])
        batch_rows = sb("batch_rows", [128, B])
        head_cols = sb("head_cols", [128, 15 * H])
        rev = sb("rev", [128, E1])
        ones = sb("ones", [128, 128])
        halves = sb("halves", [128, 2, 4 * B])
        eps_tile = sb("eps_tile", [128, GB]); inv_d = sb("inv_d", [128, GB])
        keymask = sb("keymask", [B, S], bf16)

        bn = sb("bn", [128, GB, 6]); mv_b = sb("mv_b", [128, GB, 2]); mv = sb("mv", [128, B, 2]); rstd = sb("rstd", [128, B])
        rr = sb("rr", [128, B]); r2 = sb("r2", [128, B]); ssq = sb("ssq", [128, B])
        ps_a = sb("ps_a", [128, GB]); ps_b = sb("ps_b", [128, GB])
        xn_tm = sb("xn_tm", [128, 2, GB, D]); nT = sb("nT", [128, 2, BT])
        wa = sb("wa", [128, 2, 2 * BT]); wb = sb("wb", [128, 2, 2 * BT])
        f = sb("f", [128, 6, BT])
        parts = sb("parts", [128, 2, NPART, BT], bf16)
        oT = sb("oT", [128, 2, BT])
        stack = sb("stack", [128, 4, H * ST], bf16)
        qflat = [stack[:, 0, :], stack[:, 1, :], wb[:, :, :].rearrange("p a n -> p (a n)").bitcast(bf16)]
        kflat = [stack[:, 2, :], stack[:, 3, :], f[:, 0:4, :].rearrange("p a n -> p (a n)").bitcast(bf16)]
        qst = [x.rearrange("p (h t) -> p h t", h=H) for x in qflat]
        kst = [x.rearrange("p (h t) -> p h t", h=H) for x in kflat]
        v0x = sb("v0x", [128, B, H, VC]); v2x = sb("v2x", [128, B, H, VC])
        vx = [v0x, v0x, v2x]
        attnT = y_tok
        negm = sb("negm", [128, H, SB]); mp = sb("mp", [128, 2, H, SB], bf16); mT = sb("mT", [64, S], bf16)
        rec = sb("rec", [128, H]); o_tok = sb("o_tok", [128, 2, H, DH])
        qn = sb("qn", [128, S]); top8 = sb("top8", [128, 8]); selT = sb("selT", [128, B, H])
        sel = sb("sel", [128, S])
        rl = sb("rl", [128, GB, E0]); pr = sb("pr", [128, GB, E0]); rk = sb("rk", [128, GB, E0])
        cmp1 = sb("cmp1", [128, GB * E0, E0]); cmp2 = sb("cmp2", [128, GB * E0, E0])
        junk = [c.rearrange("p a b -> p (a b)")[:, k * D:(k + 1) * D] for c in (cmp1[:, :, :], cmp2[:, :, :]) for k in (0, 1)]
        wsum = sb("wsum", [128, GB]); wr = sb("wr", [128, 2, GB, E0])
        num = sb("num", [128, B, E1]); aff = sb("aff", [128, B, E1]); oh = sb("oh", [128, B, E1])
        a1 = sb("a1", [128, B, E1]); wn = sb("wn", [128, E1]); own = sb("own", [128, B]); mx = sb("mx", [128, B])
        xnorm = sb("xnorm", [128, B]); asum = sb("asum", [128, 1]); capv = sb("capv", [128, 1])
        negthr = sb("negthr", [128, 1]); rank = sb("rank", [128, B])
        affT = sel; ohT = sb("ohT", [128, S])
        b2s = qn
        step128 = sb("step128", [128, B])
        tile_no = sb("tile_no", [128, NT])
        out_row = sb("out_row", [128, B])
        rt = selT[:, :, :].rearrange("p b h -> p (b h)")
        tot_e, tiles_e, end_e, start_e, base_e = (rt[:, k * E1:(k + 1) * E1] for k in range(5))
        pos, pos_i = rt[:, 48:64], rt[:, 64:80].bitcast(i32)
        te = rt[:, 80:80 + NT + 6]
        pair, pair_i = rt[:, 112:112 + NT + 3], rt[:, 144:144 + NT + 3].bitcast(i32)
        tot_s, cum_s, excl_s, off_s = (f[:, 2, k * S:(k + 1) * S] for k in range(4))
        gb = rl[:, :, :].rearrange("p b e -> p (b e)")
        low = stack[:, 0:2, :].rearrange("p a n -> p (a n)").bitcast(f32)
        high = stack[:, 2:4, :].rearrange("p a n -> p (a n)").bitcast(f32)
        b1_bc = low.rearrange("p (e n) -> p e n", e=E1)
        idle_e = high[:, 0:E1 * D].rearrange("p (e d) -> p e d", e=E1)
        xs = high[:, E1 * D:].rearrange("p (t d) -> p t d", t=NT)
        ys = f[:, :, :].rearrange("p k n -> p (k n)").rearrange("p (t d) -> p t d", t=NT)
        mask_i = wa[:, :, :].rearrange("p a n -> p (a n)").bitcast(i32).rearrange("p (b s) -> p b s", b=B)
        km_all = y_tok[:, :, :].rearrange("p b d -> p (b d)").bitcast(i32)
        km_i = wb[0:B, 0, 0:S].bitcast(i32)
        aff_rows = wa[:, :, :].rearrange("p a n -> p (a n)").rearrange("p (b s) -> p b s", b=B)
        v_batch = [f[:, 4, j * 256:j * 256 + (H - 1) * VC + 32] for j in range(2)]
        o_wide = f[:, 5, :]

        ps = ctx.enter_context(nc.psum_tensor("ps", [128, 8, 512], f32))
        T, U = ps[:, 0, :], ps[:, 1, :]
        A = [ps[:, 2, :], ps[:, 3, :]]
        Bk = [ps[:, 4:6, :], ps[:, 6:8, :]]
        BF = [b.rearrange("p a n -> p (a n)") for b in Bk]

        hT = Handoff(sem, "bankT", 1, dict(moe1=NT, ctx=4, sio=8, ffn=8, qp0=4, ac0=40, po0=4, moe0=4, qp1=8, ac1=40,
                                            po1=4, qp2=4, ac2=40, po2=4, aff=4, route=2))
        hU = Handoff(sem, "bankU", 1, dict(ctx=4, sio=4, ac0=16, moe0=4, qp1=2, ac1=16, ac2=16, aff=4, route=3))
        hA = Handoff(sem, "bankA", 2, dict(ctx=8, sio=4, ffn=4, ac0=64, moe0=36, qp1=4, ac1=64, ac2=64, moe1=NT))
        hB = Handoff(sem, "bankB", 2, dict(ctx=4, sio=4, ffn=16, qp0=4, ac0=32, po0=4, moe0=72, qp1=4, ac1=32,
                                           po1=4, qp2=4, ac2=32, po2=4, route=2))
        hXN = Handoff(sem, "xn_tm", 2, dict(ctx=4, sio=4, ffn=4, qp0=4, moe0=4, qp1=4, qp2=4, aff=4, moe1=NT))
        hNT = Handoff(sem, "nT", 2, dict(ctx=4, sio=4, ffn=4, qp0=4, moe0=4, qp1=4, qp2=4, aff=4, moe1=NT))
        hWA = Handoff(sem, "wa", 2, dict(sio=4, ffn=16, ac0=32, moe0=36, ac1=32, ac2=32, moe1=NT))
        hWB = Handoff(sem, "wb", 2, dict(sio=4, ffn=16, moe0=36, moe1=NT))
        hOT = Handoff(sem, "oT", 2, dict(sio=4, ffn=4, po0=4, po1=4, po2=4))
        half = dict(ctx=4, qp0=2, qp1=4, qp2=2)
        hP = [Handoff(sem, "parts%d" % s, 1, half, unit=32) for s in range(2)]
        hO = Handoff(sem, "o_tok", 2, dict(ac0=16, ac1=16, ac2=16))
        hFV = [Handoff(sem, "to_split%d" % s, 1, half) for s in range(2)]
        hF45 = Handoff(sem, "f45", 2, dict(sio=4, qp1=4))
        hVB = Handoff(sem, "v_batch", 2, dict(ac0=16, ac1=16, ac2=16))
        hOW = Handoff(sem, "o_wide", 1, dict(ac0=16, ac1=16, ac2=16))
        hG = Handoff(sem, "gelu", 2, dict(moe1=NT))
        hHT = Handoff(sem, "hidden_T", 2, dict(moe1=NT))
        hDN = Handoff(sem, "down", 2, dict(moe1=NT))
        rings = (hG, hHT, hDN, hVB, hOW, hT, hU, hA, hB, hXN, hNT, hWA, hWB, hOT, hO, hF45, *hP, *hFV)

        consts_ready = sem("consts_ready"); x_loaded = sem("x_loaded"); w_loaded = [sem("w_loaded%d" % k) for k in range(4)]
        masks_loaded = sem("masks_loaded"); km_loaded = sem("km_loaded"); ctx_loaded = [sem("ctx_loaded0"), sem("ctx_loaded1")]; stack_init = sem("stack_init")
        const_rows = sem("const_rows"); keymask_ready = sem("keymask_ready"); masks_ready = sem("masks_ready")
        dve_chain = sem("dve_chain"); pool_chain = sem("pool_chain"); act_chain = sem("act_chain")
        pool_settled = sem("pool_settled"); dve_settled = sem("dve_settled"); pe_settled = sem("pe_settled")
        stats_done = sem("stats_done"); rstd_done = sem("rstd_done")
        x1_done = sem("x1_done"); ssq_done = sem("ssq_done"); r2_done = sem("r2_done")
        stack_loaded = [sem("stack_loaded%d" % k) for k in range(3)]; slot2_filled = sem("slot2_filled")
        stack_freed = sem("stack_freed"); m_ready = sem("m_ready"); mp_ready = sem("mp_ready"); m_stored = sem("m_stored")
        attnT_done = sem("attnT_done"); v0_ready = sem("v0_ready"); v2_ready = sem("v2_ready")
        h_ready = sem("h_ready")
        absq_ready = sem("absq_ready"); sel_ready = sem("sel_ready"); selT_ready = sem("selT_ready")
        logits_ready = sem("logits_ready"); probs_ready = sem("probs_ready")
        scaled_ready = sem("scaled_ready"); scaled_used = sem("scaled_used")
        sq_done = sem("sq_done"); num_ready = sem("num_ready"); route_pe = sem("route_pe")
        waff_sq = sem("waff_sq"); wn_ready = sem("wn_ready"); wn_raw = sem("wn_raw"); xnorm_ready = sem("xnorm_ready")
        asum_ready = sem("asum_ready"); cap_ready = sem("cap_ready"); aff_ready = sem("aff_ready")
        affT_ready = sem("affT_ready"); affrows_ready = sem("affrows_ready"); disp_ready = sem("disp_ready")
        zero_ready = sem("zero_ready"); zero_stored = sem("zero_stored"); b1_loaded = sem("b1_loaded")
        gb_ready = sem("gb_ready"); idle_filled = sem("idle_filled"); idle_ready = sem("idle_ready")
        xhat_ready = sem("xhat_ready"); pos_ready = sem("pos_ready"); te_ready = sem("te_ready")
        xs_scattered = sem("xs_scattered"); xs_loaded = [sem("xs_loaded0"), sem("xs_loaded1")]
        ys_raw = sem("ys_raw"); ys_ready = sem("ys_ready"); ys_stored = sem("ys_stored"); gathered = [sem("gathered%d" % k) for k in range(NBLK)]
        x_done = sem("x_done"); out_stored = sem("out_stored")

        def blk(tile, b, n=GB):
            return tile[:, bass.ts(b, n), :]

        def in_tiles(x, behind):
            return not isinstance(x, int) or 0 <= x - behind < NT

        def expert_tiles(eng, step):
            for x in range(4):
                step(x, x % 2)
            with eng.Fori(0, (NT - 4) // 2) as i:
                for p in range(2):
                    step(i * 2 + (4 + p), p)
            for x in range(NT, NT + 3):
                step(x, x % 2)

        def tile_of(a, tile):
            return a[:, tile, :] if isinstance(tile, int) else a[:, bass.ds(tile, 1), :].rearrange("p o n -> p (o n)")

        def experts_of(eng, x):
            src = pair_i[0:1, x:x + 1] if isinstance(x, int) else pair_i[0:1, bass.ds(x, 1)]
            both = eng.value_load(src, min_val=0, max_val=E1 * E1 - 1)
            return both & (E1 - 1), (both >> (E1.bit_length() - 1)) & (E1 - 1)

        STAT = {s: 4 * k for k, s in enumerate(["sio", "qp0", "moe0", "qp1", "qp2", "aff"])}
        groups = [["cols", "wk0", "wk0s", "wv0", "wv2", "wk2", "cos", "sin"], ["wz", "wdt", "wya", "wy"],
                  ["wfc", "wfa", "wout"]]
        groups.append([n for n in w if not any(n in g for g in groups)])
        spread = [[(bv0, "bv0"), (thr, "thr")], [], [], [(bv1, "bv1"), (rbias, "rbias")]]
        W_LOADS = [16 * (len(a) + len(b)) for a, b in zip(groups, spread)]

        def load_weights(eng, k):
            for n in groups[k]:
                eng.dma_start(w[n][...], t[n]).then_inc(w_loaded[k], 16)
            for dst, n in spread[k]:
                eng.dma_start(dst[:, :], t[n].partition_broadcast(128)).then_inc(w_loaded[k], 16)

        def split(eng, link, stage, s, u, rope, keys=None):
            v, r, part = f[:, 2 * s, :], f[:, 2 * s + 1, :], parts[:, s]
            eng.wait_ge(hFV[s].filled, hFV[s].at(stage, u))
            link.settle()
            if rope:
                link(eng.tensor_tensor(v, v, r, ALU.add), settle=True)
            if keys is not None:
                link(eng.scalar_tensor_tensor(out=v, in0=keys, scalar=0.0, in1=v, op0=ALU.not_equal, op1=ALU.mult),
                     settle=True)
            eng.wait_ge(hP[s].freed, hP[s].free(stage, u))
            link.settle()
            link(eng.tensor_copy(part[:, 0, :], v), settle=True)
            link(eng.tensor_tensor(r, v, part[:, 0, :], ALU.subtract), settle=True)
            link(eng.tensor_copy(part[:, 1, :], r), settle=True)
            link.release(eng.tensor_tensor(part[:, 2, :], r, part[:, 1, :], ALU.subtract),
                         hP[s].filled, hP[s].at(stage, u), hFV[s].freed)

        block = ctx.enter_context(nc.Block())

        @block.sync
        def _(sp):
            for p in range(2):
                sp.wait_ge(hXN.freed, hXN.at("ctx", p))
                sp.dma_start(xn_tm[:, p], t["ctx"][p * GB:(p + 1) * GB].rearrange("b t d -> t b d"))\
                  .then_inc(ctx_loaded[p], 16)
            for b in range(NBLK):
                sp.dma_start(x_tok[:, b * GB:(b + 1) * GB, :],
                             t["x"][b * GB:(b + 1) * GB].rearrange("b t d -> t b d")).then_inc(x_loaded, 16)
            for p in range(2):
                sp.wait_ge(ctx_loaded[p], 16)
                sp.sem_inc(hXN.filled, 1)
            for p in range(2):
                sp.wait_ge(hXN.freed, hXN.at("ctx", 2 + p))
                sp.dma_start(xn_tm[:, p], t["ctx"][(2 + p) * GB:(3 + p) * GB].rearrange("b t d -> t b d"))\
                  .then_inc(ctx_loaded[p], 16)
                sp.wait_ge(ctx_loaded[p], 32)
                sp.sem_inc(hXN.filled, 1)

            def scratch_stage(stage, tensors):
                per = len(tensors)
                with sp.Fori(0, NPAIR) as i:
                    for p in range(2):
                        for q, dst in enumerate(tensors):
                            s, u = (per * p + q) % 2, i * per + (per * p + q) // 2
                            sp.wait_ge(hP[s].filled, hP[s].at(stage, u))
                            for j in range(2):
                                sp.dma_start(dst[bass.ds(i * 4 + (2 * p + j), 1)].rearrange("o c p t -> p (o c) t"),
                                             parts[:, s, :, j * ST:(j + 1) * ST]).then_inc(hP[s].freed, 16)

            def load_stack(a, n, slot):
                loaded = stack_loaded[slot]
                sp.wait_ge(stack_freed, n + (NSTEP * a + 1))
                sp.dma_start(qflat[slot][ROW_M:ROW_M + 2], qflat[slot][ROW_MASK + 1:ROW_MASK + 3]).then_inc(loaded, 16)
                for i in range(NPART):
                    src = q_scr[a, bass.ds(n, 1), i].rearrange("o (d h) t -> o d (h t)", d=DH)
                    sp.dma_start(qflat[slot][i * 24:i * 24 + 24], src.broadcast_to([NPART, DH, H * ST]))\
                      .then_inc(loaded, 16)
                src = k_scr[a, bass.ds(n, 1)].rearrange("o c (d h) t -> o (c d) (h t)", d=DH)
                sp.dma_start(kflat[slot][0:ROW_M], src.broadcast_to([NPART, NPART * DH, H * ST])).then_inc(loaded, 16)
                if a == 0:
                    src = keymask_scr.rearrange("(n b) s -> n (b s)", b=SB)[bass.ds(n, 1)]
                    sp.dma_start(kst[slot][ROW_MASK:ROW_MASK + 1], src.unsqueeze(1).broadcast_to([1, H, ST]))\
                      .then_inc(loaded, 16)
                else:
                    sp.dma_start(kflat[slot][ROW_MASK:ROW_MASK + 1], qflat[slot][ROW_MASK + 1:ROW_MASK + 2])\
                      .then_inc(loaded, 16)

            def store_m(a, n, slot):
                sp.wait_ge(m_ready, n + (NSTEP * a + 1))
                for k in range(2):
                    sp.dma_start(qflat[slot][ROW_M + k:ROW_M + k + 1], mT[k * H * SB:(k + 1) * H * SB, :])\
                      .then_inc(m_stored, 16)

            def attention_loads(a):
                for h in hP:
                    sp.wait_ge(h.freed, h.free("ac%d" % a, 0))
                load_stack(a, 0, 0)
                load_stack(a, 1, 1)
                sp.wait_ge(slot2_filled, 2 * a + 2)
                sp.dma_start(qflat[2][ROW_MASK:ROW_MASK + 1], kflat[2][ROW_MASK + 1:ROW_MASK + 2]).then_inc(const_rows, 16)
                sp.wait_ge(const_rows, 16 * (4 + a))
                store_m(a, 0, 0)
                with sp.Fori(0, NSTEP // 3) as i:
                    for p in range(3):
                        load_stack(a, i * 3 + (p + 2), (p + 2) % 3)
                        store_m(a, i * 3 + (p + 1), (p + 1) % 3)
                store_m(a, NSTEP - 1, (NSTEP - 1) % 3)

            scratch_stage("ctx", [k_scr[0], k_scr[2]])
            load_weights(sp, 3)
            sp.wait_ge(zero_ready, 2)
            for dst, row, n in ((xs_scr, 0, NT), (ys_scr, NT, B)):
                sp.dma_start(dst[row * S:(row + n) * S].rearrange("(r p) d -> p r d", p=S),
                             sel[:, :].unsqueeze(1).broadcast_to([128, n, D])).then_inc(zero_stored, 16)
            sp.wait_ge(stack_init, 2)
            for s in (0, 1):
                sp.dma_start(qst[s][ROW_MASK:ROW_MASK + 1], kst[s][ROW_MASK:ROW_MASK + 1]).then_inc(const_rows, 16)
            sp.wait_ge(keymask_ready, 1)
            sp.dma_start(keymask_scr, keymask[:, :]).then_inc(const_rows, 16)
            sp.wait_ge(const_rows, 48)
            scratch_stage("qp0", [q_scr[0]])
            attention_loads(0)
            scratch_stage("qp1", [q_scr[1], k_scr[1]])
            attention_loads(1)
            scratch_stage("qp2", [q_scr[2]])
            attention_loads(2)
            sp.wait_ge(stack_freed, 3 * NSTEP + 3)
            sp.dma_start(low, t["b1"].rearrange("e n -> (e n)").partition_broadcast(128)).then_inc(b1_loaded, 16)
            sp.wait_ge(xs_scattered, 16 * B)
            for k, (lo, hi) in enumerate(((0, 4), (4, NT))):
                sp.dma_start(xs[:, lo:hi, :], xs_scr[lo * S:hi * S].rearrange("(r p) d -> p r d", p=S))\
                  .then_inc(xs_loaded[k], 16)
            with sp.Fori(0, NT // 2) as i:
                sp.wait_ge(ys_ready, i * 2 + 2)
                sp.dma_start(ys_scr[bass.ts(i, 2 * S)].rearrange("(r p) d -> p r d", p=S), ys[:, bass.ts(i, 2), :])\
                  .then_inc(ys_stored, 16)
            with sp.Fori(0, NBLK) as b:
                sp.wait_ge(x_done, b + 1)
                sp.dma_start(t["out"][bass.ts(b, GB)].rearrange("b t d -> t b d"), blk(x_tok, b)).then_inc(out_stored, 16)
            sp.wait_ge(out_stored, 16 * NBLK)

        @block.gpsimd
        def _(g):
            chain = Chain(g, pool_chain, pool_settled)

            def link(ins):
                chain(ins, settle=True)

            for r in rings:
                g.sem_inc(r.freed, r.depth * r.unit)
            g.sem_inc(stack_freed, 3)
            g.sem_inc(scaled_used, 2)
            g.memset(ident[:, :], 0.0)
            g.memset(v0x[:, :, :, :], 1.0)
            g.memset(v2x[:, :, :, :], 1.0).then_inc(zero_ready, 1)
            g.wait_ge(zero_ready, 1)
            link(g.affine_select(out=ident[:, :], in_=ident[:, :], compare_op=ALU.not_equal, fill=1.0, base=0,
                                 pattern=[[-1, 128]], channel_multiplier=1))
            g.memset(halves[:, 0, :], -0.5)
            g.memset(halves[:, 1, :], 0.5)
            g.memset(eps_tile[:, :], LN_EPS)
            g.memset(inv_d[:, :], 1.0 / D)
            g.memset(sel[:, :], 0.0).then_inc(zero_ready, 1)
            g.wait_ge(zero_ready, 2)
            g.wait_ge(w_loaded[0], W_LOADS[0])
            link(g.tensor_scalar(negbdt[:, :], col["b_dt"], -1.0, None, ALU.mult))
            link(g.tensor_scalar(negthr[:, :], thr[:, :], -1.0, None, ALU.mult))
            g.sem_inc(consts_ready, 1)

            def stats(s):
                with chain.loop(NBLK, 2) as b:
                    g.wait_ge(stats_done, b + (STAT[s] + 1))
                    chain.settle()
                    link(g.tensor_tensor(ps_a[:, :], mv[:, bass.ts(b, GB), 1], eps_tile[:, :], ALU.add))
                    link(g.tensor_tensor(rstd[:, bass.ts(b, GB)], ps_a[:, :], halves[:, 0, 0:GB], ALU.pow))
                    g.sem_inc(rstd_done, 1)

            def split_stage(stage, per, rope=False):
                with chain.loop(NPAIR, per * (4 if rope else 3)) as i:
                    for p in range(per):
                        split(g, chain, stage, 1, i * per + p, rope)

            def attention(a):
                stage = "ac%d" % a
                g.wait_ge(hFV[0].freed, hFV[0].at(stage, 0))
                g.memset(qflat[2], 0.0).then_inc(slot2_filled, 1)
                g.memset(kflat[2], 1.0).then_inc(slot2_filled, 1)
                g.wait_ge(hF45.freed, hF45.at(stage, 1))
                link(g.memset(f[:, 4:6, :], 0.0))
                g.wait_ge(v0_ready, NBLK if a == 0 else 2 * NBLK)
                g.wait_ge(v2_ready, NBLK)
                with chain.loop(NSTEP, 0) as n:
                    for j in range(2):
                        k = n * 2 + j
                        g.wait_ge(hVB.freed, hVB.at(stage, k))
                        chain.settle()
                        g.tensor_copy(v_batch[j][:, 0:H * VC],
                                      vx[a][:, bass.ds(k, 1), :, :].rearrange("p o h c -> p (o h c)"))\
                         .then_inc(hVB.filled, 1)

            with chain.loop(NBLK, 7) as b:
                q4 = bass.ts(b, GB)
                g.wait_ge(stats_done, b + 1)
                chain.settle()
                link(g.tensor_tensor(ps_a[:, :], mv[:, q4, 1], eps_tile[:, :], ALU.add))
                link(g.tensor_tensor(rstd[:, q4], ps_a[:, :], halves[:, 0, 0:GB], ALU.pow))
                link(g.tensor_tensor(ps_a[:, :], rstd[:, q4], rstd[:, q4], ALU.mult))
                link(g.tensor_tensor(ps_a[:, :], ps_a[:, :], mv[:, q4, 1], ALU.mult))
                link(g.tensor_scalar(ps_a[:, :], ps_a[:, :], RMS_EPS, None, ALU.add))
                link(g.tensor_tensor(ps_b[:, :], ps_a[:, :], halves[:, 0, 0:GB], ALU.pow))
                link(g.tensor_tensor(rr[:, q4], ps_b[:, :], rstd[:, q4], ALU.mult))
                g.sem_inc(rstd_done, 1)

            split_stage("ctx", 2)

            g.memset(ones[:, :], 1.0)
            g.memset(head_cols[:, :], 0.0)
            g.memset(batch_rows[:, :], 1.0)
            g.memset(lower_e[:, :, :], 1.0)
            g.memset(earlier[:, :], 1.0)
            g.memset(causal[:, :], 0.0)
            g.iota(rev[:, :], [[-1, E1]], base=E1, channel_multiplier=0, allow_small_or_imprecise_dtypes=True)
            g.iota(step128[:, :], [[S, B]], base=0, channel_multiplier=0, allow_small_or_imprecise_dtypes=True)
            g.iota(tile_no[:, :], [[1, NT]], base=0, channel_multiplier=0, allow_small_or_imprecise_dtypes=True)
            g.iota(out_row[:, :], [[S, B]], base=NT * S, channel_multiplier=1, allow_small_or_imprecise_dtypes=True)
            g.memset(stack[:, 0:2, :], 0.0).then_inc(stack_init, 1)
            g.memset(stack[:, 2:4, :], 1.0).then_inc(stack_init, 1)
            g.wait_ge(stack_init, 2)
            link(g.tensor_copy(identb[:, :], ident[:, :]))
            link(g.affine_select(out=causal[:, :], in_=causal[:, :], compare_op=ALU.is_ge, fill=NEG, base=0,
                                 pattern=[[-1, 128]], channel_multiplier=1))
            link(g.affine_select(out=earlier[:, :], in_=earlier[:, :], compare_op=ALU.is_gt, fill=0.0, base=0,
                                 pattern=[[-1, 128]], channel_multiplier=1))
            link(g.affine_select(out=lower_e[:, :, :], in_=lower_e[:, :, :], compare_op=ALU.is_gt, fill=0.0, base=0,
                                 pattern=[[1, E0], [-1, E0]], channel_multiplier=0))
            link(g.affine_select(out=batch_rows[:, :], in_=batch_rows[:, :], compare_op=ALU.is_ge, fill=0.0, base=0,
                                 pattern=[[-E1, B]], channel_multiplier=1))
            link(g.affine_select(out=batch_rows[:, :], in_=batch_rows[:, :], compare_op=ALU.is_ge, fill=0.0,
                                 base=E1 - 1, pattern=[[E1, B]], channel_multiplier=-1))
            for d in range(DH):
                link(g.affine_select(out=head_cols[:, 7 * H:8 * H], in_=head_cols[:, 7 * H:8 * H],
                                     compare_op=ALU.not_equal, fill=1.0, base=-H * d, pattern=[[-1, H]],
                                     channel_multiplier=1))
            g.sem_inc(consts_ready, 1)

            with chain.loop(NBLK, 4) as b:
                q4 = bass.ts(b, GB)
                g.wait_ge(x1_done, b + 1)
                chain.settle()
                link(g.tensor_tensor(blk(x_tok, b), blk(x_tok, b), blk(y_tok, b), ALU.add))
                g.wait_ge(ssq_done, b * GB + GB)
                chain.settle()
                link(g.tensor_tensor(ps_b[:, :], ssq[:, q4], inv_d[:, :], ALU.mult))
                link(g.tensor_scalar(ps_a[:, :], ps_b[:, :], RMS_EPS, None, ALU.add))
                link(g.tensor_tensor(r2[:, q4], ps_a[:, :], halves[:, 0, 0:GB], ALU.pow))
                g.sem_inc(r2_done, 1)
            stats("qp0")
            split_stage("qp0", 1, True)
            attention(0)
            stats("moe0")
            with chain.loop(NBLK, E0) as b:
                for e in range(E0):
                    g.wait_ge(scaled_ready, b * E0 + (e + 1))
                    chain.settle()
                    link(g.tensor_tensor(blk(x_tok, b), blk(x_tok, b),
                                         f[:, e % 2, :].rearrange("p (b d) -> p b d", b=GB), ALU.add))
                    g.sem_inc(scaled_used, 1)
            stats("qp1")
            split_stage("qp1", 2)
            attention(1)
            stats("qp2")
            split_stage("qp2", 1)
            attention(2)
            stats("aff")
            g.wait_ge(wn_raw, 1)
            g.tensor_tensor(wn[:, :], wn[:, :], halves[:, 1, 0:E1], ALU.pow).then_inc(wn_ready, 1)
            g.wait_ge(ssq_done, 2 * B)
            g.tensor_tensor(xnorm[:, :], ssq[:, :], halves[:, 1, 0:B], ALU.pow).then_inc(xnorm_ready, 1)
            g.wait_ge(pos_ready, 1)
            g.wait_ge(xhat_ready, NBLK)
            g.wait_ge(zero_stored, 32)
            for b in range(B):
                g.indirect_dma_start(xs_scr, bass.IndirectOffsetOnAxis(ap=pos_i[:, b:b + 1], axis=0), y_tok[:, b, :],
                                     None).then_inc(xs_scattered, 16)
            g.wait_ge(te_ready, 1)

            def tile_in(x, p):
                g.wait_ge(hXN.freed, hXN.at("moe1", x))
                chain.settle()
                g.tensor_copy(xn_tm[:, p, 0, :], tile_of(xs, x)).then_inc(hXN.filled, 1)

            def tile_out(x):
                _, e = experts_of(g, x + 3)
                g.wait_ge(ys_raw, x + 1)
                chain.settle()
                y = tile_of(ys, x)
                g.tensor_tensor(y, y, idle_e[:, bass.ds(e, 1), :].rearrange("p o d -> p (o d)"), ALU.subtract)\
                 .then_inc(ys_ready, 1)

            AHEAD = 6
            for x in range(AHEAD):
                if x % 4 == 0:
                    g.wait_ge(xs_loaded[x // 4], 16)
                tile_in(x, x % 2)
            with g.Fori(0, (NT - AHEAD) // 2) as i:
                for p in range(2):
                    tile_in(i * 2 + (AHEAD + p), p)
                    tile_out(i * 2 + p)
            for x in range(NT - AHEAD, NT):
                tile_out(x)
            g.wait_ge(ys_stored, 16 * (NT // 2))
            for b in range(B):
                g.indirect_dma_start(y_tok[:, b, :], None, ys_scr,
                                     bass.IndirectOffsetOnAxis(ap=pos_i[:, b:b + 1], axis=0))\
                 .then_inc(gathered[b // GB], 16)

        @block.scalar
        def _(act):
            link = Chain(act, act_chain)
            load_weights(act, 0)
            load_weights(act, 1)
            act.dma_start(km_all, t["maskk"].rearrange("b o k -> (b o k)").partition_broadcast(128))\
               .then_inc(km_loaded, 16)
            load_weights(act, 2)
            act.dma_start(mask_i, t["maskf"].rearrange("b o q k -> q (b o) k")).then_inc(masks_loaded, 16)
            act.dma_start(km_i, t["maskk"].rearrange("b o k -> (b o) k")).then_inc(masks_loaded, 16)
            act.wait_ge(consts_ready, 1)
            act.wait_ge(w_loaded[0], W_LOADS[0])

            def transposed(stage, i, k, p, scale=None, xn_freed=True):
                act.wait_ge(hT.filled, hT.at(stage, k))
                if xn_freed:
                    act.sem_inc(hXN.freed, 1)
                act.wait_ge(hNT.freed, hNT.at(stage, i * 2 + p))
                ins = (act.activation(nT[:, p, :], T, ACT.Copy) if scale is None
                       else act.activation(nT[:, p, :], T, ACT.Identity, scale=scale))
                link.release(ins, hNT.filled, hNT.at(stage, i * 2 + p), hT.freed)

            with link.loop(NPAIR, 0) as i:
                for p in range(2):
                    transposed("ctx", i, i * 2 + p, p)
                for p in range(2):
                    act.wait_ge(hA.filled, hA.at("ctx", i * 4 + 2 * p + 1))
                    link.release(act.activation(v2x[:, bass.ts(i * 2 + p, GB), :, 0:DH],
                                                A[1].rearrange("p (b h d) -> p b h d", b=GB, h=H), ACT.Copy),
                                 v2_ready, i * 2 + (p + 1), hA.freed)
                    act.wait_ge(hU.filled, hU.at("ctx", i * 2 + p))
                    act.sem_inc(hNT.freed, 1)
                    act.wait_ge(hFV[1].freed, hFV[1].at("ctx", i * 2 + p))
                    link.release(act.activation(f[:, 2, :], U, ACT.Copy), hFV[1].filled, hFV[1].at("ctx", i * 2 + p),
                                 hU.freed)

            act.wait_ge(masks_ready, 1)
            with link.loop(NPAIR, 0) as i:
                for p in range(2):
                    transposed("sio", i, i * 4 + p, p, scale=col["g_sio"])
                for p in range(2):
                    n = i * 2 + p
                    act.wait_ge(hB.filled, hB.at("sio", n))
                    act.wait_ge(hWA.freed, hWA.at("sio", n))
                    act.wait_ge(hWB.freed, hWB.at("sio", n))
                    act.activation(wa[:, p, 0:BT], Bk[p][:, 0, :], ACT.Sigmoid, bias=col["b_z"])
                    act.activation(wa[:, p, BT:], Bk[p][:, 1, :], ACT.Sigmoid, bias=col["b_dt"])
                    act.activation(wb[:, p, 0:BT], Bk[p][:, 1, :], ACT.Sigmoid, bias=negbdt[:, :], scale=-1.0)\
                       .then_inc(hB.freed, 1)
                    act.wait_ge(hA.filled, hA.at("sio", n))
                    act.sem_inc(hNT.freed, 1)
                    link.release(act.activation(wb[:, p, BT:], A[p], ACT.Silu, bias=col["b_ya"]),
                                 hWB.filled, hWB.at("sio", n), hWA.filled, hA.freed)
                for p in range(2):
                    act.wait_ge(x1_done, i * 2 + (p + 1))
                    for j in range(GB):
                        tok = bass.ds(i * 8 + (4 * p + j), 1)
                        act.activation(junk[j], y_tok[:, tok, :].rearrange("p o d -> p (o d)"), ACT.Square,
                                       accum_out=ssq[:, tok]).then_inc(ssq_done, 1)
                    act.wait_ge(ssq_done, i * 8 + (4 * p + 4))

            with link.loop(NPAIR, 0) as i:
                for p in range(2):
                    transposed("ffn", i, i * 4 + p, p, scale=col["g_ffn"])
                for p in range(2):
                    for c in range(4):
                        k = 4 * p + c
                        act.wait_ge(hB.filled, hB.at("ffn", i * 8 + k))
                        if c == 3:
                            act.sem_inc(hNT.freed, 1)
                        act.wait_ge(hWA.freed, hWA.at("ffn", i * 8 + k))
                        act.activation(wa[:, k % 2, 0:BT], Bk[k % 2][:, 1, :], ACT.Silu, bias=col["b_fa%d" % c])\
                           .then_inc(hWA.filled, 1)
                    act.wait_ge(hA.filled, hA.at("ffn", i * 2 + p))
                    act.sem_inc(hWB.freed, 1)
                    act.wait_ge(hOT.freed, hOT.at("ffn", i * 2 + p))
                    link.release(act.activation(oT[:, p, :], A[p], ACT.Identity, bias=col["b_out"]),
                                 hOT.filled, hOT.at("ffn", i * 2 + p), hA.freed)

            def query_stage(a):
                stage = "qp%d" % a
                with link.loop(NPAIR, 0) as i:
                    for p in range(2):
                        transposed(stage, i, i * (4 if a == 1 else 2) + p, p)
                    for p in range(2):
                        n = i * 2 + p
                        if a == 0:
                            continue
                        act.wait_ge(hB.filled, hB.at(stage, n))
                        if a == 1:
                            for q, bias in enumerate(("bq1", "bk1")):
                                act.wait_ge(hFV[q].freed, hFV[q].at(stage, n))
                                act.activation(f[:, 2 * q, :], Bk[p][:, q, :], ACT.Identity, bias=col[bias])\
                                   .then_inc(hFV[q].filled, 1)
                            act.wait_ge(hF45.freed, hF45.at(stage, n))
                            link.release(act.activation(f[:, 4 + p, :], Bk[p][:, 0, :], ACT.Abs, bias=col["bq1"]),
                                         hF45.filled, hF45.at(stage, n), hB.freed)
                        else:
                            act.sem_inc(hNT.freed, 1)
                            act.wait_ge(hFV[p].freed, hFV[p].at(stage, i))
                            link.release(act.activation(f[:, 2 * p, :], Bk[p][:, 0, :], ACT.Copy),
                                         hFV[p].filled, hFV[p].at(stage, i), hB.freed)

            def attention(a):
                stage = "ac%d" % a

                def exps(n, u):
                    act.wait_ge(hB.filled, hB.at(stage, n * 4 + u))
                    if u == 3:
                        act.sem_inc(stack_freed, 1)
                    act.wait_ge(hWA.freed, hWA.at(stage, n * 4 + u))
                    link.release(act.activation(wa[:, u % 2, :], BF[u % 2], ACT.Exp, scale=SCALE),
                                 hWA.filled, hWA.at(stage, n * 4 + u), hB.freed)

                def products_out(n, j):
                    k = n * 2 + j
                    act.wait_ge(hU.filled, hU.at(stage, k))
                    act.sem_inc(hWA.freed, 1)
                    act.sem_inc(hVB.freed, 1)
                    act.wait_ge(hOW.freed, hOW.at(stage, k))
                    link.release(act.activation(o_wide, U, ACT.Copy), hOW.filled, hOW.at(stage, k), hU.freed)

                def store_o(n, j, k):
                    act.wait_ge(hT.filled, hT.at(stage, k))
                    act.sem_inc(hO.freed, 1)
                    link.release(act.activation(attnT[:, bass.ds(n * 2 + j, 1), :].rearrange("p o t -> p (o t)"),
                                                T[:, 0:S], ACT.Copy),
                                 attnT_done, n * 2 + (B * a + j + 1), hT.freed)

                def step(n, before):
                    for op, u in STEP:
                        if op == "B":
                            exps(n, u)
                        elif op == "K":
                            products_out(n, u)
                        elif op == "k" and before is not None:
                            products_out(before, u)
                        elif op == "o" and before is not None:
                            store_o(before, u, before * 5 + (3 + 2 * u))

                step(0, None)
                with link.loop((NSTEP - 2) // 3, 0) as i:
                    for p in range(3):
                        step(i * 3 + (p + 1), i * 3 + p)
                step(NSTEP - 1, NSTEP - 2)
                store_o(NSTEP - 1, 0, 5 * NSTEP - 3)
                products_out(NSTEP - 1, 1)
                store_o(NSTEP - 1, 1, 5 * NSTEP - 1)

            def output_stage(a):
                stage = "po%d" % a
                with link.loop(NPAIR, 0) as i:
                    for p in range(2):
                        n = i * 2 + p
                        act.wait_ge(hB.filled, hB.at(stage, n))
                        act.wait_ge(hOT.freed, hOT.at(stage, n))
                        link.release(act.activation(oT[:, p, :], Bk[p][:, 0, :], ACT.Identity, bias=col["bo%d" % a]),
                                     hOT.filled, hOT.at(stage, n), hB.freed)

            query_stage(0)
            attention(0)
            output_stage(0)

            with link.loop(NPAIR, 0) as i:
                for p in range(2):
                    transposed("moe0", i, i * 2 + p, p)
                for p in range(2):
                    act.wait_ge(logits_ready, i * 2 + (p + 1))
                    act.activation(pr[:, :, :], rl[:, :, :], ACT.Sigmoid).then_inc(probs_ready, 1)
                for p in range(2):
                    for e in range(E0 + 1):
                        k = i * 18 + (9 * p + e)
                        s = (p + e) % 2
                        act.wait_ge(hB.filled, hB.at("moe0", k * 2))
                        act.wait_ge(hWA.freed, hWA.at("moe0", k))
                        link.release(act.activation(wa[:, s, :], BF[0], ACT.Silu),
                                     hWA.filled, hWA.at("moe0", k), hB.freed)

            query_stage(1)
            attention(1)
            output_stage(1)
            query_stage(2)
            attention(2)
            output_stage(2)

            act.activation(a1[:, 0, :], w["waff"][:, :], ACT.Square).then_inc(waff_sq, 1)
            with link.loop(NPAIR, 0) as i:
                for p in range(2):
                    act.wait_ge(hXN.filled, hXN.at("aff", i * 2 + p))
                    act.wait_ge(ssq_done, i * 8 + (B + 4 * p))
                    for j in range(GB):
                        tok = bass.ds(i * 8 + (4 * p + j), 1)
                        act.activation(junk[j], xn_tm[:, p, j, :], ACT.Square,
                                       accum_out=ssq[:, tok]).then_inc(ssq_done, 1)
                    act.wait_ge(ssq_done, i * 8 + (B + 4 * p + 4))
                    act.wait_ge(hT.filled, hT.at("aff", i * 2 + p))
                    act.activation(y_tok[:, bass.ts(i * 2 + p, GB), :], xn_tm[:, p], ACT.Copy).then_inc(xhat_ready, 1)
                    act.wait_ge(xhat_ready, i * 2 + (p + 1))
                    act.sem_inc(hXN.freed, 1)
                    act.wait_ge(hNT.freed, hNT.at("aff", i * 2 + p))
                    link.release(act.activation(nT[:, p, :], T, ACT.Copy),
                                 hNT.filled, hNT.at("aff", i * 2 + p), hT.freed)
            act.wait_ge(route_pe, 2)
            act.activation(capv[:, :], U[:, 0:1], ACT.Sigmoid, bias=negthr[:, :], scale=1.0 / (B * S * E1))\
               .then_inc(cap_ready, 1)

            act.activation(gb, w["b1c"][:, :, :].rearrange("p e c -> p (e c)"), ACT.Gelu).then_inc(gb_ready, 1)

            def step(x, p):
                if in_tiles(x, 0):
                    act.wait_ge(hT.filled, hT.at("moe1", x))
                    act.sem_inc(hXN.freed, 1)
                    act.wait_ge(hNT.freed, hNT.at("moe1", x))
                    link.release(act.activation(nT[:, p, 0:S], T[:, 0:S], ACT.Copy),
                                 hNT.filled, hNT.at("moe1", x), hT.freed)
                if in_tiles(x, 1):
                    act.wait_ge(hWA.filled, hWA.at("moe1", x - 1))
                    act.wait_ge(hG.freed, hG.at("moe1", x - 1))
                    link.release(act.activation(wa[:, 1 - p, BT:], wa[:, 1 - p, 0:BT], ACT.Gelu),
                                 hG.filled, hG.at("moe1", x - 1), hWA.freed)
                if in_tiles(x, 3):
                    act.wait_ge(hDN.filled, hDN.at("moe1", x - 3))
                    act.sem_inc(hWB.freed, 1)
                    link.release(act.activation(tile_of(ys, x - 3), Bk[1 - p][:, 1, 0:D], ACT.Copy),
                                 ys_raw, x - 3 + 1, hDN.freed)

            expert_tiles(act, step)

        @block.vector
        def _(v):
            link = Chain(v, dve_chain, dve_settled)

            def statistics(b):
                link.settle()
                for j in range(GB):
                    last = v.bn_stats(bn[:, j, :], x_tok[:, bass.ds(b * GB + j, 1), :].rearrange("p o d -> p (o d)"))
                link(last, settle=True)
                for j in range(GB):
                    last = v.bn_aggr(mv_b[:, j, :], bn[:, j, :])
                link(last)
                v.tensor_copy(mv[:, bass.ts(b, GB), :], mv_b[:, :, :]).then_inc(stats_done, 1)

            def normalise(stage, i, p, r=rstd, src=x_tok, sub=True):
                v.wait_ge(hXN.freed, hXN.at(stage, i * 2 + p))
                for j in range(GB):
                    tok = bass.ds(i * 8 + (4 * p + j), 1)
                    x_j = src[:, tok, :].rearrange("p o d -> p (o d)")
                    if sub:
                        last = v.tensor_scalar(xn_tm[:, p, j, :], x_j, mv[:, tok, 0], r[:, tok], ALU.subtract, ALU.mult)
                    else:
                        last = v.tensor_scalar(xn_tm[:, p, j, :], x_j, r[:, tok], None, ALU.mult)
                last.then_inc(hXN.filled, 1)

            def ln_wait(stage, i, p):
                v.wait_ge(rstd_done, i * 2 + (STAT[stage] + p + 1))

            v.wait_ge(x_loaded, 16 * NBLK)
            with link.loop(NBLK, 2) as b:
                statistics(b)
            v.wait_ge(w_loaded[0], W_LOADS[0])
            v.wait_ge(consts_ready, 1)

            def rope(stage, i, p, s, u, b0, b1):
                v.wait_ge(hB.filled, hB.at(stage, i * 2 + p))
                v.wait_ge(hFV[s].freed, hFV[s].at(stage, u))
                for q, (bias, tab) in enumerate(((b0, "cos"), (b1, "sin"))):
                    last = v.scalar_tensor_tensor(
                        out=f[:, 2 * s + q, :].rearrange("p (b t) -> p b t", b=GB),
                        in0=Bk[p][:, q, :].rearrange("p (b t) -> p b t", b=GB), scalar=col[bias],
                        in1=w[tab][:, :].unsqueeze(1).broadcast_to([128, GB, S]), op0=ALU.add, op1=ALU.mult)
                link.release(last, hFV[s].filled, hFV[s].at(stage, u), hB.freed)

            def values(stage, i, p, k, bias, ready):
                v.wait_ge(hA.filled, hA.at(stage, k))
                s = 0 if stage == "ctx" else p
                link.release(v.tensor_tensor(v0x[:, bass.ts(i * 2 + p, GB), :, 0:DH],
                                             A[s].rearrange("p (b h d) -> p b h d", b=GB, h=H),
                                             bias[:, :].rearrange("p (h d) -> p h d", h=H).unsqueeze(1)
                                             .broadcast_to([128, GB, H, DH]), ALU.add),
                             v0_ready, ready, hA.freed)

            v.wait_ge(km_loaded, 16)
            with link.loop(NPAIR, 2 * 5) as i:
                for p in range(2):
                    rope("ctx", i, p, 0, i * 2 + p, "bk0", "bk0s")
                    values("ctx", i, p, i * 4 + 2 * p, bv0, i * 2 + (p + 1))
                    split(v, link, "ctx", 0, i * 2 + p, True, keys=km_all[:, bass.ts(i * 2 + p, BT)])

            v.wait_ge(masks_loaded, 32)
            v.tensor_scalar(keymask[:, :], km_i, 0.0, NEG, ALU.is_equal, ALU.mult).then_inc(keymask_ready, 1)
            link(v.tensor_scalar(fullmask[:, :, :], mask_i, 0.0, NEG, ALU.is_equal, ALU.mult))
            v.sem_inc(masks_ready, 1)

            with link.loop(NPAIR, 2) as i:
                for p in range(2):
                    ln_wait("sio", i, p)
                    for j in range(GB):
                        tok = bass.ds(i * 8 + (4 * p + j), 1)
                        v.tensor_scalar(y_tok[:, tok, :].rearrange("p o d -> p (o d)"),
                                        x_tok[:, tok, :].rearrange("p o d -> p (o d)"), mv[:, tok, 0], rstd[:, tok],
                                        ALU.subtract, ALU.mult)
                    normalise("sio", i, p, r=rr)
                for p in range(2):
                    n = i * 2 + p
                    v.wait_ge(hWB.filled, hWB.at("sio", n))
                    v.wait_ge(hWA.filled, hWA.at("sio", n))
                    link(v.tensor_tensor(f[:, p, :], wa[:, p, 0:BT], wa[:, p, BT:], ALU.mult))
                    v.wait_ge(hF45.freed, hF45.at("sio", n))
                    for j in range(GB):
                        c = slice(j * S, (j + 1) * S)
                        last = v.tensor_tensor_scan(f[:, 4 + p, c], wb[:, p, c], f[:, p, c], col["h0"],
                                                    ALU.mult, ALU.add)
                    link.release(last, hF45.filled, hF45.at("sio", n), hWA.freed)
                for p in range(2):
                    n = i * 2 + p
                    v.wait_ge(hU.filled, hU.at("sio", n))
                    v.sem_inc(hF45.freed, 1)
                    v.wait_ge(hOT.freed, hOT.at("sio", n))
                    link.release(v.scalar_tensor_tensor(out=oT[:, p, :], in0=U, scalar=col["b_y"], in1=wb[:, p, BT:],
                                                        op0=ALU.add, op1=ALU.mult),
                                 hOT.filled, hOT.at("sio", n), hU.freed, hWB.freed)
                for p in range(2):
                    n = i * 2 + p
                    v.wait_ge(hT.filled, hT.at("sio", i * 4 + (2 + p)))
                    v.sem_inc(hOT.freed, 1)
                    y_b = y_tok[:, bass.ts(n, GB), :].rearrange("p b d -> p (b d)")
                    link.release(v.tensor_tensor(y_b, y_b, T, ALU.add), x1_done, n + 1, hT.freed)

            def add_output(stage, n, k):
                v.wait_ge(hT.filled, hT.at(stage, k))
                v.sem_inc(hOT.freed, 1)
                x_b = x_tok[:, bass.ts(n, GB), :].rearrange("p b d -> p (b d)")
                link.release(v.tensor_tensor(x_b, x_b, T, ALU.add), hT.freed, hT.freed_at(stage, k))
                statistics(n)

            with link.loop(NPAIR, 4) as i:
                for p in range(2):
                    v.wait_ge(r2_done, i * 2 + (p + 1))
                    normalise("ffn", i, p, r=r2, src=y_tok, sub=False)
                for p in range(2):
                    for c in range(4):
                        k = 4 * p + c
                        v.wait_ge(hWA.filled, hWA.at("ffn", i * 8 + k))
                        v.wait_ge(hWB.freed, hWB.at("ffn", i * 8 + k))
                        link.release(v.scalar_tensor_tensor(out=wb[:, k % 2, 0:BT], in0=Bk[k % 2][:, 0, :],
                                                            scalar=col["b_fc%d" % c], in1=wa[:, k % 2, 0:BT],
                                                            op0=ALU.add, op1=ALU.mult),
                                     hWB.filled, hWB.at("ffn", i * 8 + k), hB.freed, hWA.freed)
                for p in range(2):
                    add_output("ffn", i * 2 + p, i * 4 + (2 + p))

            def query_stage(a):
                stage = "qp%d" % a
                with link.loop(NPAIR, (4, 2 * 3 + SELECT_LINKS, 3)[a]) as i:
                    for p in range(2):
                        ln_wait(stage, i, p)
                        normalise(stage, i, p)
                    for p in range(2):
                        if a == 0:
                            rope(stage, i, p, p, i, "bq0", "bq0s")
                            v.sem_inc(hNT.freed, 1)
                            if p == 0:
                                split(v, link, stage, 0, i, True)
                        if a == 1:
                            values(stage, i, p, i * 2 + p, bv1, i * 2 + (NBLK + p + 1))
                            v.sem_inc(hNT.freed, 1)
                            split(v, link, stage, 0, i * 2 + p, False)
                        if a == 2 and p == 0:
                            split(v, link, stage, 0, i, False)
                    if a == 1:
                        v.wait_ge(hU.filled, hU.at(stage, i))
                        v.sem_inc(hF45.freed, 2)
                        v.wait_ge(zero_stored, 32)
                        link(v.tensor_copy(qn[:, :], U[:, 0:S]), settle=True)
                        v.sem_inc(hU.freed, 1)
                        for _ in range(NTOP // 8):
                            link(v.max(top8[:, :], qn[:, :]), settle=True)
                            link(v.match_replace(qn[:, :], top8[:, :], qn[:, :], -1.0), settle=True)
                        link(v.tensor_scalar(sel[:, :], qn[:, :], 0.0, None, ALU.is_lt))
                        v.sem_inc(sel_ready, 1)
                        v.wait_ge(hT.filled, hT.at(stage, i * 4 + 2))
                        link(v.tensor_copy(selT[:, bass.ts(i, 8), :].rearrange("p b h -> p (b h)"), T[:, 0:S]))
                        v.sem_inc(hT.freed, 1)

            def attention(a):
                stage = "ac%d" % a

                def maxima(n, u):
                    j, g4 = u // 4, u % 4
                    v.wait_ge(hA.filled, hA.at(stage, n * 8 + u))
                    v.tensor_reduce(negm[:, g4 * 4:g4 * 4 + 4, j], A[u % 2].rearrange("p (h k) -> p h k", h=4),
                                    AX.X, ALU.max, negate=True).then_inc(hA.freed, 1)

                def m_parts(n):
                    v.wait_ge(hA.freed, hA.freed_at(stage, n * 8 + 7))
                    link(v.tensor_copy(mp[:, 0], negm[:, :, :]))
                    v.tensor_tensor(mp[:, 1], negm[:, :, :], mp[:, 0], ALU.subtract).then_inc(mp_ready, 1)

                def m_store(n, k):
                    v.wait_ge(hT.filled, hT.at(stage, k))
                    link.release(v.tensor_copy(mT[:, :], T.bitcast(bf16)[0:64, 0:S]),
                                 m_ready, n + (NSTEP * a + 1), hT.freed)

                def normalise_heads(n, j, kt):
                    k = n * 2 + j
                    v.wait_ge(hT.filled, hT.at(stage, kt))
                    v.sem_inc(hOW.freed, 1)
                    o = T.rearrange("p (h w) -> p h w", h=H)
                    link(v.reciprocal(rec[:, :].unsqueeze(2), o[:, :, DH:VC]))
                    if a == 1:
                        link(v.tensor_tensor(rec[:, :], rec[:, :],
                                             selT[:, bass.ds(k, 1), :].rearrange("p o h -> p (o h)"), ALU.mult))
                    v.wait_ge(hO.freed, hO.at(stage, k))
                    link.release(v.tensor_tensor(o_tok[:, j], o[:, :, 0:DH],
                                                 rec[:, :].unsqueeze(2).broadcast_to([128, H, DH]), ALU.mult),
                                 hO.filled, hO.at(stage, k), hT.freed)

                def step(n, before, do_a=True):
                    for op, u in STEP:
                        if op == "A" and do_a:
                            maxima(n + 1, u)
                        elif op == "P" and do_a:
                            m_parts(n + 1)
                        elif op == "E" and do_a:
                            m_store(n + 1, n * 5 + 2)
                        elif op == "N":
                            normalise_heads(n, u, n * 5 + 1)
                        elif op == "n" and before is not None:
                            normalise_heads(before, u, before * 5 + 4)

                nl = 2 if a == 1 else 1
                for u in range(8):
                    maxima(0, u)
                m_parts(0)
                m_store(0, 0)
                step(0, None)
                with link.loop((NSTEP - 2) // 3, 3 * (1 + 2 * nl)) as i:
                    for p in range(3):
                        step(i * 3 + (p + 1), i * 3 + p)
                step(NSTEP - 1, NSTEP - 2, do_a=False)
                normalise_heads(NSTEP - 1, 1, 5 * NSTEP - 2)

            def output_stage(a):
                stage = "po%d" % a
                with link.loop(NPAIR, 4) as i:
                    for p in range(2):
                        add_output(stage, i * 2 + p, i * 2 + p)

            SELECT_LINKS = 1 + 2 * (NTOP // 8) + 1 + 1
            v.wait_ge(w_loaded[3], W_LOADS[3])
            v.wait_ge(consts_ready, 2)
            query_stage(0)
            attention(0)
            output_stage(0)

            for h in hFV:
                v.wait_ge(h.freed, h.at("moe0", 0))
            with link.loop(NPAIR, 2 * 10 + 2 + 4) as i:
                for p in range(2):
                    ln_wait("moe0", i, p)
                    normalise("moe0", i, p)
                for p in range(2):
                    n = i * 2 + p
                    v.wait_ge(hU.filled, hU.at("moe0", n))
                    link.release(v.tensor_tensor(rl[:, :, :], U[:, 0:GB * E0].rearrange("p (b e) -> p b e", b=GB),
                                                 rbias[:, :].unsqueeze(1).broadcast_to([128, GB, E0]), ALU.add),
                                 logits_ready, n + 1, hU.freed)
                    v.wait_ge(probs_ready, n + 1)
                    p_j = pr[:, :, :].unsqueeze(2).broadcast_to([128, GB, E0, E0])
                    p_e = pr[:, :, :].unsqueeze(3).broadcast_to([128, GB, E0, E0])
                    c1 = cmp1[:, :, :].rearrange("p (b e) j -> p b e j", b=GB)
                    c2 = cmp2[:, :, :].rearrange("p (b e) j -> p b e j", b=GB)
                    link(v.tensor_tensor(c1, p_j, p_e, ALU.is_gt))
                    link(v.tensor_tensor(c2, p_j, p_e, ALU.is_equal))
                    link(v.tensor_tensor(c2, c2, lower_e[:, :, :].unsqueeze(1).broadcast_to([128, GB, E0, E0]), ALU.mult))
                    link(v.tensor_tensor(c1, c1, c2, ALU.add))
                    rk2 = rk[:, :, :].rearrange("p b e -> p (b e)")
                    link(v.tensor_reduce(rk2, cmp1[:, :, :], AX.X, ALU.add))
                    link(v.tensor_scalar(rk2, rk2, float(TOPK) - 0.5, None, ALU.is_lt))
                    link(v.tensor_tensor(rk[:, :, :], rk[:, :, :], pr[:, :, :], ALU.mult))
                    link(v.tensor_reduce(wsum[:, :], rk[:, :, :], AX.X, ALU.add))
                    link(v.reciprocal(wsum[:, :], wsum[:, :]))
                    link(v.tensor_tensor(wr[:, p], rk[:, :, :], wsum[:, :].unsqueeze(2).broadcast_to([128, GB, E0]),
                                         ALU.mult))
                for p in range(2):
                    n = i * 2 + p
                    x_b = x_tok[:, bass.ts(n, GB), :].rearrange("p b d -> p (b d)")
                    for e in range(E0 + 2):
                        if e < E0 + 1:
                            k, s = i * 18 + (9 * p + e), (p + e) % 2
                            v.wait_ge(hWA.filled, hWA.at("moe0", k))
                            v.wait_ge(hB.filled, hB.at("moe0", k * 2 + 1))
                            if e == E0:
                                v.sem_inc(hNT.freed, 1)
                            v.wait_ge(hWB.freed, hWB.at("moe0", k))
                            link.release(v.tensor_tensor(wb[:, s, :], wa[:, s, :], BF[1], ALU.mult),
                                         hWB.filled, hWB.at("moe0", k), hB.freed, hWA.freed)
                        if e > 0:
                            k, s = i * 18 + (9 * p + e - 1), (p + e - 1) % 2
                            v.wait_ge(hA.filled, hA.at("moe0", k))
                            v.sem_inc(hWB.freed, 1)
                            if e == 1:
                                link(v.tensor_tensor(x_b, x_b, A[s], ALU.add))
                                v.sem_inc(hA.freed, 1)
                            else:
                                m = e - 2
                                v.wait_ge(scaled_used, n * E0 + (m + 1))
                                link.release(v.tensor_tensor(f[:, m % 2, :].rearrange("p (b d) -> p b d", b=GB),
                                                             A[s].rearrange("p (b d) -> p b d", b=GB),
                                                             wr[:, p, :, m:m + 1].broadcast_to([128, GB, D]), ALU.mult),
                                             scaled_ready, n * E0 + (m + 1), hA.freed)
                    v.wait_ge(scaled_used, n * E0 + (E0 + 2))
                    statistics(n)

            query_stage(1)
            attention(1)
            output_stage(1)
            query_stage(2)
            attention(2)
            output_stage(2)

            for h in hFV:
                v.wait_ge(h.freed, h.at("aff", 0))
            v.wait_ge(route_pe, 1)
            link(v.tensor_copy(wn[:, :], U[:, 0:E1]))
            v.sem_inc(wn_raw, 1)
            with link.loop(NPAIR, 0) as i:
                for p in range(2):
                    ln_wait("aff", i, p)
                    normalise("aff", i, p)
                for p in range(2):
                    n = i * 2 + p
                    v.wait_ge(hU.filled, hU.at("aff", n))
                    v.sem_inc(hNT.freed, 1)
                    link.release(v.tensor_copy(num[:, bass.ts(n, GB), :].rearrange("p b e -> p (b e)"), U[:, 0:GB * E1]),
                                 num_ready, n + 1, hU.freed)
            v.wait_ge(wn_ready, 1)
            v.wait_ge(xnorm_ready, 1)
            be = [128, B, E1]
            link(v.tensor_tensor(a1[:, :, :], xnorm[:, :].unsqueeze(2).broadcast_to(be),
                                 wn[:, :].unsqueeze(1).broadcast_to(be), ALU.mult))
            link(v.tensor_scalar(a1[:, :, :], a1[:, :, :], 1e-9, None, ALU.add))
            link(v.reciprocal(a1[:, :, :], a1[:, :, :]))
            link(v.tensor_tensor(aff[:, :, :], num[:, :, :], a1[:, :, :], ALU.mult))
            v.tensor_reduce(asum[:, :], aff[:, :, :].rearrange("p b e -> p (b e)"), AX.X, ALU.add).then_inc(asum_ready, 1)
            link(v.tensor_reduce(own[:, :], aff[:, :, :], AX.X, ALU.max))
            own_b = own[:, :].unsqueeze(2).broadcast_to(be)
            link(v.tensor_tensor(oh[:, :, :], aff[:, :, :], own_b, ALU.is_equal))
            link(v.tensor_tensor(oh[:, :, :], oh[:, :, :], rev[:, :].unsqueeze(1).broadcast_to(be), ALU.mult))
            link(v.tensor_reduce(mx[:, :], oh[:, :, :], AX.X, ALU.max))
            link(v.tensor_tensor(oh[:, :, :], oh[:, :, :], mx[:, :].unsqueeze(2).broadcast_to(be), ALU.is_equal))
            v.sem_inc(aff_ready, 1)
            v.wait_ge(hT.filled, hT.at("route", 0))
            link(v.tensor_copy(affT[:, :], T[:, 0:S]))
            v.sem_inc(hT.freed, 1)
            v.wait_ge(hT.filled, hT.at("route", 1))
            link(v.tensor_copy(ohT[:, :], T[:, 0:S]))
            v.sem_inc(hT.freed, 1)
            link(v.tensor_tensor(aff_rows, affT[:, :].unsqueeze(1).broadcast_to([128, B, S]),
                                 batch_rows[:, :].unsqueeze(2).broadcast_to([128, B, S]), ALU.mult))
            v.sem_inc(affrows_ready, 1)
            v.wait_ge(cap_ready, 1)
            link(v.tensor_scalar(capv[:, :], capv[:, :], float(CAP_S), float(MIN_CAP), ALU.mult, ALU.max))
            link(v.tensor_scalar(capv[:, :], capv[:, :], float(CAP_S), None, ALU.min))
            for c in range(NBLK):
                if c % 2 == 0:
                    v.wait_ge(hB.filled, hB.at("route", c // 2))
                G = Bk[c // 2][:, c % 2, :].rearrange("p (b s) -> p b s", b=GB)
                g1 = f[:, 0, :].rearrange("p (b s) -> p b s", b=GB)
                g2 = f[:, 1, :].rearrange("p (b s) -> p b s", b=GB)
                own_c = own[:, c * GB:(c + 1) * GB].unsqueeze(2).broadcast_to([128, GB, S])
                link(v.tensor_tensor(g1, G, own_c, ALU.is_gt))
                link(v.tensor_tensor(g2, G, own_c, ALU.is_equal))
                if c % 2 == 1:
                    v.sem_inc(hB.freed, 1)
                link(v.tensor_tensor(g2, g2, earlier[:, :].unsqueeze(1).broadcast_to([128, GB, S]), ALU.mult))
                link(v.tensor_tensor(g1, g1, g2, ALU.add))
                link(v.tensor_reduce(rank[:, c * GB:(c + 1) * GB], g1, AX.X, ALU.add))
            link(v.tensor_scalar(rank[:, :], rank[:, :], 1.0, capv[:, 0:1], ALU.add, ALU.is_le))
            link(v.tensor_tensor(a1[:, :, :].rearrange("p b e -> p (b e)").rearrange("p (e b) -> p e b", e=E1),
                                 oh[:, :, :].rearrange("p b e -> p e b"),
                                 rank[:, :].unsqueeze(1).broadcast_to([128, E1, B]), ALU.mult))
            v.sem_inc(disp_ready, 1)
            v.wait_ge(idle_filled, 1)
            link(v.tensor_copy(idle_e, ps[:, 2:4, :].rearrange("p a n -> p (a n)").rearrange("p (e d) -> p e d", e=E1)))
            v.sem_inc(idle_ready, 1)
            link(v.tensor_reduce(b2s[:, :], idle_e.rearrange("p e d -> p d e"), AX.X, ALU.add))
            v.wait_ge(route_pe, 4)
            link(v.tensor_tensor(b2s[:, :], b2s[:, :], U[:, 2 * S:2 * S + D], ALU.add))
            link(v.tensor_copy(tot_s, U[:, S:2 * S]))
            link(v.tensor_tensor_scan(cum_s, ones[:, :], tot_s, 0.0, ALU.mult, ALU.add))
            link(v.tensor_tensor(excl_s, cum_s, tot_s, ALU.subtract))
            link(v.tensor_tensor(off_s, U[:, 0:S], excl_s, ALU.add))
            eb = lambda x: x.rearrange("p (e b) -> p e b", e=E1)
            first = eb(excl_s)[:, :, 0]
            link(v.tensor_tensor(tot_e, eb(cum_s)[:, :, B - 1], first, ALU.subtract))
            over = eb(f[:, 3, 0:S])
            link(v.tensor_tensor(over, tot_e.unsqueeze(2).broadcast_to([128, E1, B]),
                                 step128[:, :].unsqueeze(1).broadcast_to([128, E1, B]), ALU.is_gt))
            link(v.tensor_reduce(tiles_e, over, AX.X, ALU.add))
            link(v.tensor_tensor_scan(end_e, ones[:, 0:E1], tiles_e, 0.0, ALU.mult, ALU.add))
            link(v.tensor_tensor(start_e, end_e, tiles_e, ALU.subtract))
            link(v.scalar_tensor_tensor(out=base_e, in0=start_e, scalar=float(S), in1=first, op0=ALU.mult,
                                        op1=ALU.subtract))
            link(v.tensor_tensor(eb(off_s), eb(off_s), base_e.unsqueeze(2).broadcast_to([128, E1, B]), ALU.add))
            link(v.tensor_tensor(off_s, off_s, a1[:, :, :].rearrange("p b e -> p (b e)"), ALU.mult))
            link(v.tensor_reduce(pos, off_s.rearrange("p (e b) -> p b e", e=E1), AX.X, ALU.add))
            link(v.tensor_scalar(mx[:, :], rank[:, :], -1.0, 1.0, ALU.mult, ALU.add))
            link(v.tensor_tensor(mx[:, :], mx[:, :], out_row[:, :], ALU.mult))
            link(v.tensor_tensor(pos, pos, mx[:, :], ALU.add))
            link(v.tensor_copy(pos_i, pos))
            v.sem_inc(pos_ready, 1)
            ended = f[:, 3, S:S + NT * E1].rearrange("p (t e) -> p t e", t=NT)
            link(v.tensor_tensor(ended, tile_no[:, :].unsqueeze(2).broadcast_to([128, NT, E1]),
                                 end_e.unsqueeze(1).broadcast_to([128, NT, E1]), ALU.is_ge))
            link(v.memset(te, 0.0))
            link(v.tensor_reduce(te[:, 3:3 + NT], ended, AX.X, ALU.add))
            link(v.tensor_scalar(te, te, float(E1 - 1), None, ALU.min))
            link(v.scalar_tensor_tensor(out=pair, in0=te[:, 0:NT + 3], scalar=float(E1), in1=te[:, 2:NT + 5],
                                        op0=ALU.mult, op1=ALU.add))
            link(v.tensor_copy(pair_i, pair))
            v.sem_inc(te_ready, 1)
            for n in range(NBLK):
                x_b = x_tok[:, n * GB:(n + 1) * GB, :]
                link(v.tensor_tensor(x_b, x_b, b2s[:, :].unsqueeze(1).broadcast_to([128, GB, D]), ALU.add))

            v.wait_ge(b1_loaded, 16)

            def step(x, p):
                if in_tiles(x, 1):
                    e, _ = experts_of(v, x)
                    v.wait_ge(hA.filled, hA.at("moe1", x - 1))
                    v.sem_inc(hNT.freed, 1)
                    v.wait_ge(hWA.freed, hWA.at("moe1", x - 1))
                    link.release(v.tensor_tensor(wa[:, 1 - p, 0:BT], A[1 - p],
                                                 b1_bc[:, bass.ds(e, 1), :].rearrange("p o n -> p (o n)"), ALU.add),
                                 hWA.filled, hWA.at("moe1", x - 1), hA.freed)
                if in_tiles(x, 2):
                    v.wait_ge(hHT.filled, hHT.at("moe1", x - 2))
                    v.sem_inc(hG.freed, 1)
                    v.wait_ge(hWB.freed, hWB.at("moe1", x - 2))
                    link.release(v.tensor_copy(wb[:, p, 0:BT], Bk[p][:, 0, :]), hWB.filled, hWB.at("moe1", x - 2),
                                 hHT.freed)
            expert_tiles(v, step)
            for n in range(NBLK):
                v.wait_ge(gathered[n], 16 * GB)
                x_b = x_tok[:, n * GB:(n + 1) * GB, :]
                v.tensor_tensor(x_b, x_b, y_tok[:, n * GB:(n + 1) * GB, :], ALU.add).then_inc(x_done, 1)

        @block.tensor
        def _(pe):
            mm, tr = nc.tensor.matmul, nc.tensor.transpose
            pe.wait_ge(consts_ready, 1)
            pe.wait_ge(w_loaded[0], W_LOADS[0])

            def all_free(stage, *all_rings):
                for r in all_rings:
                    pe.wait_ge(r.freed, r.at(stage, r.depth - 1))

            def transposes(stage, k, src):
                pe.wait_ge(hT.freed, hT.at(stage, k))
                for j in range(GB):
                    last = tr(T[:, j * S:(j + 1) * S], src(j), ident[:, :])
                last.then_inc(hT.filled, 1)

            def normalised(stage, i, k, p):
                pe.wait_ge(hXN.filled, hXN.at(stage, i * 2 + p))
                transposes(stage, k, lambda j: xn_tm[:, p, j, :])

            def back(stage, i, k, p):
                pe.wait_ge(hOT.filled, hOT.at(stage, i * 2 + p))
                transposes(stage, k, lambda j: oT[:, p, j * S:(j + 1) * S])

            def tokens_out(bank, p, wt, n_out, last_sem):
                for j in range(GB):
                    last = mm(bank[:, j * n_out:(j + 1) * n_out], nT[:, p, j * S:(j + 1) * S], wt, start=True, stop=True)
                last.then_inc(last_sem, 1)

            with pe.Fori(0, NPAIR) as i:
                for p in range(2):
                    normalised("ctx", i, i * 2 + p, p)
                for p in range(2):
                    n = i * 2 + p
                    pe.wait_ge(hNT.filled, hNT.at("ctx", n))
                    pe.wait_ge(hB.freed, hB.at("ctx", n))
                    mm(Bk[p][:, 0, :], w["wk0"][:, :], nT[:, p, :], start=True, stop=True)
                    mm(Bk[p][:, 1, :], w["wk0s"][:, :], nT[:, p, :], start=True, stop=True).then_inc(hB.filled, 1)
                    pe.wait_ge(hA.freed, hA.at("ctx", n * 2 + 1))
                    tokens_out(A[0], p, w["wv0"][:, :], D, hA.filled)
                    tokens_out(A[1], p, w["wv2"][:, :], D, hA.filled)
                    pe.wait_ge(hU.freed, hU.at("ctx", n))
                    mm(U, w["wk2"][:, :], nT[:, p, :], start=True, stop=True).then_inc(hU.filled, 1)

            pe.wait_ge(w_loaded[1], W_LOADS[1])
            all_free("sio", hA, hB)
            with pe.Fori(0, NPAIR) as i:
                for p in range(2):
                    normalised("sio", i, i * 4 + p, p)
                for p in range(2):
                    n = i * 2 + p
                    pe.wait_ge(hNT.filled, hNT.at("sio", n))
                    pe.wait_ge(hB.freed, hB.at("sio", n))
                    mm(Bk[p][:, 0, :], w["wz"][:, :], nT[:, p, :], start=True, stop=True)
                    mm(Bk[p][:, 1, :], w["wdt"][:, :], nT[:, p, :], start=True, stop=True).then_inc(hB.filled, 1)
                    pe.wait_ge(hA.freed, hA.at("sio", n))
                    mm(A[p], w["wya"][:, :], nT[:, p, :], start=True, stop=True).then_inc(hA.filled, 1)
                for p in range(2):
                    n = i * 2 + p
                    pe.wait_ge(hF45.filled, hF45.at("sio", n))
                    pe.wait_ge(hU.freed, hU.at("sio", n))
                    mm(U, w["wy"][:, :], f[:, 4 + p, :], start=True, stop=True).then_inc(hU.filled, 1)
                for p in range(2):
                    back("sio", i, i * 4 + (2 + p), p)

            pe.wait_ge(w_loaded[2], W_LOADS[2])
            all_free("ffn", hA, hB)
            with pe.Fori(0, NPAIR) as i:
                for p in range(2):
                    normalised("ffn", i, i * 4 + p, p)
                for p in range(2):
                    pe.wait_ge(hNT.filled, hNT.at("ffn", i * 2 + p))
                    for c in range(5):
                        if c < 4:
                            k = 4 * p + c
                            pe.wait_ge(hB.freed, hB.at("ffn", i * 8 + k))
                            fs = slice(c * 128, (c + 1) * 128)
                            mm(Bk[k % 2][:, 0, :], w["wfc"][:, fs], nT[:, p, :], start=True, stop=True)
                            mm(Bk[k % 2][:, 1, :], w["wfa"][:, fs], nT[:, p, :], start=True, stop=True)\
                              .then_inc(hB.filled, 1)
                        if c > 0:
                            k = 4 * p + c - 1
                            pe.wait_ge(hWB.filled, hWB.at("ffn", i * 8 + k))
                            if c == 1:
                                pe.wait_ge(hA.freed, hA.at("ffn", i * 2 + p))
                            mm(A[p], w["wout"][:, c - 1, :], wb[:, k % 2, 0:BT], start=(c == 1), stop=(c == 4))\
                              .then_inc(hWB.freed if c < 4 else hA.filled, 1)
                for p in range(2):
                    back("ffn", i, i * 4 + (2 + p), p)

            def query_stage(a):
                stage = "qp%d" % a
                all_free(stage, hB)
                with pe.Fori(0, NPAIR) as i:
                    for p in range(2):
                        normalised(stage, i, i * (4 if a == 1 else 2) + p, p)
                    for p in range(2):
                        n = i * 2 + p
                        pe.wait_ge(hNT.filled, hNT.at(stage, n))
                        pe.wait_ge(hB.freed, hB.at(stage, n))
                        names = (("wq0", "wq0s"), ("wq1", "wk1"), ("wq2",))[a]
                        for q, name in enumerate(names):
                            last = mm(Bk[p][:, q, :], w[name][:, :], nT[:, p, :], start=True, stop=True)
                        last.then_inc(hB.filled, 1)
                        if a == 1:
                            pe.wait_ge(hA.freed, hA.at(stage, n))
                            tokens_out(A[p], p, w["wv1"][:, :], D, hA.filled)
                    if a == 1:
                        pe.wait_ge(hU.freed, hU.at(stage, i))
                        for b in range(8):
                            if b % 4 == 0:
                                pe.wait_ge(hF45.filled, hF45.at(stage, i * 2 + b // 4))
                            last = mm(U[:, 0:S], head_cols[:, (7 - b) * H:(15 - b) * H],
                                      f[:, 4 + b // 4, (b % 4) * S:(b % 4 + 1) * S], start=(b == 0), stop=(b == 7))
                        last.then_inc(hU.filled, 1)
                        pe.wait_ge(sel_ready, i + 1)
                        pe.wait_ge(hT.freed, hT.at(stage, i * 4 + 2))
                        tr(T[:, 0:S], sel[:, :], ident[:, :]).then_inc(hT.filled, 1)
                        pe.wait_ge(hT.freed, hT.at(stage, i * 4 + 3))
                        pe.sem_inc(hT.filled, 1)
                        pe.sem_inc(hT.freed, 1)

            def attention(a):
                stage = "ac%d" % a

                LOAD = 16 * (NPART + 3)

                def scores(n, u, s, m):
                    j, g4 = u // 4, u % 4
                    if u == 0:
                        pe.wait_ge(stack_loaded[s], m * LOAD + (len(range(s, NSTEP, 3)) * a + 1) * LOAD)
                    pe.wait_ge(hA.freed, hA.at(stage, n * 8 + u))
                    bank = A[u % 2]
                    if a == 1:
                        mm(bank, identb[:, :], causal[:, :].unsqueeze(1).broadcast_to([128, 4, S]), start=True, stop=False,
                           skip_group_check=True)
                    if a == 2:
                        mm(bank, identb[:, :], fullmask[:, bass.ds(n * 2 + j, 1), :].broadcast_to([128, 4, S]),
                           start=True, stop=False, skip_group_check=True)
                    for q in range(4):
                        h = g4 * 4 + q
                        last = mm(bank[:, q * S:(q + 1) * S], qst[s][:, h, j * S:(j + 1) * S],
                                  kst[s][:, h, j * S:(j + 1) * S], start=(a == 0), stop=True, skip_group_check=(a != 0))
                    last.then_inc(hA.filled, 1)

                def scores_T(n, u, s):
                    j, hh = u // 2, u % 2
                    if u == 0:
                        pe.wait_ge(m_stored, n * 32 + 32 * (NSTEP * a + 1))
                    pe.wait_ge(hB.freed, hB.at(stage, n * 4 + u))
                    for half in range(2):
                        bank = Bk[u % 2][:, half, :]
                        if a == 1:
                            mm(bank, causal[:, :], identb[:, :].unsqueeze(1).broadcast_to([128, 4, S]), start=True,
                               stop=False, skip_group_check=True)
                        if a == 2:
                            mm(bank, fullmask[:, bass.ds(n * 2 + j, 1), :].rearrange("p o k -> p (o k)"),
                               identb[:, :].unsqueeze(1).broadcast_to([128, 4, S]), start=True,
                               stop=False, skip_group_check=True)
                        for q in range(4):
                            h = hh * 8 + half * 4 + q
                            last = mm(bank[:, q * S:(q + 1) * S], kst[s][:, h, j * S:(j + 1) * S],
                                      qst[s][:, h, j * S:(j + 1) * S], start=(a == 0), stop=True,
                                      skip_group_check=(a != 0))
                    last.then_inc(hB.filled, 1)

                def values_sum(n, u):
                    j, hh = u // 2, u % 2
                    pe.wait_ge(hWA.filled, hWA.at(stage, n * 4 + u))
                    if hh == 0:
                        pe.wait_ge(hVB.filled, hVB.at(stage, n * 2 + j))
                        pe.wait_ge(hU.freed, hU.at(stage, n * 2 + j))
                    for q in range(8):
                        h = hh * 8 + q
                        rows, cols = slice(h % 4 * 32, h % 4 * 32 + 32), slice(h // 4 * S, (h // 4 + 1) * S)
                        last = mm(U[rows, cols], v_batch[j][:, h * VC:h * VC + 32], wa[:, u % 2, q * S:(q + 1) * S],
                                  start=True, stop=True)
                    last.then_inc(hU.filled if hh else hWA.freed, 1)

                def m_rows(n, k):
                    pe.wait_ge(mp_ready, n + (NSTEP * a + 1))
                    pe.wait_ge(hT.freed, hT.at(stage, k))
                    pe.sem_inc(pe_settled, 1)
                    tr(T.bitcast(bf16)[0:64, 0:S], mp[:, :, :, :].rearrange("p l h j -> p (l h j)"), identb[:, :])\
                      .then_inc(hT.filled, 1)

                def products_T(n, j, k):
                    pe.wait_ge(hOW.filled, hOW.at(stage, n * 2 + j))
                    transposes(stage, k, lambda c: o_wide[:, c * S:(c + 1) * S])

                def out_rows(n, j, k):
                    pe.wait_ge(hO.filled, hO.at(stage, n * 2 + j))
                    pe.wait_ge(hT.freed, hT.at(stage, k))
                    tr(T[:, 0:S], o_tok[:, j].rearrange("p h d -> p (h d)"), ident[:, :]).then_inc(hT.filled, 1)

                def step(n, before, p, m, do_a=True):
                    for op, u in STEP:
                        if op == "A" and do_a:
                            scores(n + 1, u, (p + 1) % 3, m + (p + 1) // 3)
                        elif op == "B":
                            scores_T(n, u, p)
                        elif op == "V":
                            values_sum(n, u)
                        elif op == "v" and before is not None:
                            values_sum(before, u)
                        elif op == "M" and do_a:
                            m_rows(n + 1, n * 5 + 2)
                        elif op == "X":
                            products_T(n, u, n * 5 + 1)
                        elif op == "x" and before is not None:
                            products_T(before, u, before * 5 + 4)
                        elif op == "o" and before is not None:
                            out_rows(before, u, before * 5 + (3 + 2 * u))

                pe.wait_ge(masks_ready, 1)
                all_free(stage, hA, hB)
                for u in range(8):
                    scores(0, u, 0, 0)
                m_rows(0, 0)
                step(0, None, 0, 0)
                with pe.Fori(0, (NSTEP - 2) // 3) as i:
                    for p in range(3):
                        step(i * 3 + (p + 1), i * 3 + p, (p + 1) % 3, i + (p + 1) // 3)
                step(NSTEP - 1, NSTEP - 2, (NSTEP - 1) % 3, (NSTEP - 1) // 3, do_a=False)
                out_rows(NSTEP - 1, 0, 5 * NSTEP - 3)
                values_sum(NSTEP - 1, 3)
                products_T(NSTEP - 1, 1, 5 * NSTEP - 2)
                out_rows(NSTEP - 1, 1, 5 * NSTEP - 1)

            def output_stage(a):
                stage = "po%d" % a
                all_free(stage, hB)
                with pe.Fori(0, NPAIR) as i:
                    for p in range(2):
                        n = i * 2 + p
                        pe.wait_ge(attnT_done, n * GB + (B * a + GB))
                        pe.wait_ge(hB.freed, hB.at(stage, n))
                        mm(Bk[p][:, 0, :], w["wo%d" % a][:, :],
                           attnT[:, bass.ts(n, GB), :].rearrange("p b t -> p (b t)"), start=True, stop=True)\
                          .then_inc(hB.filled, 1)
                    for p in range(2):
                        back(stage, i, i * 2 + p, p)

            pe.wait_ge(w_loaded[3], W_LOADS[3])
            pe.wait_ge(consts_ready, 2)
            query_stage(0)
            attention(0)
            output_stage(0)

            with pe.Fori(0, NPAIR) as i:
                for p in range(2):
                    normalised("moe0", i, i * 2 + p, p)
                for p in range(2):
                    n = i * 2 + p
                    pe.wait_ge(hNT.filled, hNT.at("moe0", n))
                    pe.wait_ge(hU.freed, hU.at("moe0", n))
                    tokens_out(U, p, w["router"][:, :], E0, hU.filled)
                for p in range(2):
                    for e in range(E0 + 2):
                        if e < E0 + 1:
                            k = i * 18 + (9 * p + e)
                            pe.wait_ge(hB.freed, hB.at("moe0", k * 2 + 1))
                            for q, name in enumerate(("gate", "up")):
                                for c in range(2):
                                    last = mm(Bk[q][:, c, :], w[name][:, e, c * 128:(c + 1) * 128], nT[:, p, :],
                                              start=True, stop=True)
                                last.then_inc(hB.filled, 1)
                        if e > 0:
                            k, s = i * 18 + (9 * p + e - 1), (p + e - 1) % 2
                            pe.wait_ge(hWB.filled, hWB.at("moe0", k))
                            pe.wait_ge(hA.freed, hA.at("moe0", k))
                            for j in range(GB):
                                for c in range(2):
                                    last = mm(A[s][:, j * D:(j + 1) * D],
                                              wb[:, s, c * BT + j * S:c * BT + (j + 1) * S],
                                              w["down"][:, e - 1, c, :], start=(c == 0), stop=(c == 1))
                            last.then_inc(hA.filled, 1)

            query_stage(1)
            attention(1)
            output_stage(1)
            query_stage(2)
            attention(2)
            output_stage(2)

            pe.wait_ge(waff_sq, 1)
            pe.wait_ge(hU.freed, hU.at("aff", 0))
            mm(U[:, 0:E1], ones[:, :], a1[:, 0, :], start=True, stop=True).then_inc(route_pe, 1)
            pe.wait_ge(wn_raw, 1)
            with pe.Fori(0, NPAIR) as i:
                for p in range(2):
                    pe.wait_ge(ssq_done, i * 8 + (B + 4 * p + 4))
                    normalised("aff", i, i * 2 + p, p)
                for p in range(2):
                    n = i * 2 + p
                    pe.wait_ge(hNT.filled, hNT.at("aff", n))
                    pe.wait_ge(hU.freed, hU.at("aff", n))
                    tokens_out(U, p, w["waff"][:, :], E1, hU.filled)
            pe.wait_ge(asum_ready, 1)
            pe.wait_ge(hU.freed, hU.at("route", 0))
            mm(U[:, 0:1], ones[:, :], asum[:, :], start=True, stop=True).then_inc(route_pe, 1)
            pe.wait_ge(aff_ready, 1)
            for k, src in enumerate((aff, oh)):
                pe.wait_ge(hT.freed, hT.at("route", k))
                tr(T[:, 0:S], src[:, :, :].rearrange("p b e -> p (b e)"), ident[:, :]).then_inc(hT.filled, 1)
            pe.wait_ge(affrows_ready, 1)
            for c in range(NBLK):
                if c % 2 == 0:
                    pe.wait_ge(hB.freed, hB.at("route", c // 2))
                last = mm(Bk[c // 2][:, c % 2, :], ohT[:, :], aff_rows[:, c * GB:(c + 1) * GB, :], start=True, stop=True)
                if c % 2:
                    last.then_inc(hB.filled, 1)
            pe.wait_ge(cap_ready, 1)
            mm(U[:, 2 * S:2 * S + D], ones[0:E1, :], w["b2r"][:, :], start=True, stop=True).then_inc(route_pe, 1)
            pe.wait_ge(gb_ready, 1)
            pe.wait_ge(hA.freed, hA.at("moe1", 1))
            for e in range(E1):
                for c in range(4):
                    last = mm(ps[:, 2 + e // 4, (e % 4) * D:(e % 4 + 1) * D],
                              gb[:, e * 4 + c:e * 4 + c + 1].broadcast_to([128, 128]), w["w2"][:, e, c, :],
                              start=(c == 0), stop=(c == 3))
            last.then_inc(idle_filled, 1)
            pe.wait_ge(disp_ready, 1)
            disp = a1[:, :, :].rearrange("p b e -> p (b e)")
            mm(U[:, 0:S], earlier[:, :], disp, start=True, stop=True)
            mm(U[:, S:2 * S], ones[:, :], disp, start=True, stop=True).then_inc(route_pe, 1)

            pe.wait_ge(idle_ready, 1)
            pe.wait_ge(te_ready, 1)
            all_free("route", hB)
            pe.wait_ge(hB.freed, hB.base["route"] + 2 + 2)

            def step(x, p):
                if in_tiles(x, 0):
                    pe.wait_ge(hXN.filled, hXN.at("moe1", x))
                    pe.wait_ge(hT.freed, hT.at("moe1", x))
                    tr(T[:, 0:S], xn_tm[:, p, 0, :], ident[:, :]).then_inc(hT.filled, 1)
                e1, e3 = experts_of(pe, x)
                if in_tiles(x, 1):
                    pe.wait_ge(hNT.filled, hNT.at("moe1", x - 1))
                    pe.wait_ge(hA.freed, hA.at("moe1", x - 1))
                    mm(A[1 - p], nT[:, 1 - p, 0:S], w["w1"][:, bass.ds(e1, 1), :].rearrange("p o n -> p (o n)"),
                       start=True, stop=True).then_inc(hA.filled, 1)
                if in_tiles(x, 2):
                    pe.wait_ge(hG.filled, hG.at("moe1", x - 2))
                    pe.wait_ge(hHT.freed, hHT.at("moe1", x - 2))
                    for c in range(4):
                        last = tr(Bk[p][:, 0, c * S:(c + 1) * S], wa[:, p, BT + c * S:BT + (c + 1) * S], ident[:, :])
                    last.then_inc(hHT.filled, 1)
                if in_tiles(x, 3):
                    pe.wait_ge(hWB.filled, hWB.at("moe1", x - 3))
                    pe.wait_ge(hDN.freed, hDN.at("moe1", x - 3))
                    for c in range(4):
                        last = mm(Bk[1 - p][:, 1, 0:D], wb[:, 1 - p, c * S:(c + 1) * S],
                                  w["w2"][:, bass.ds(e3, 1), c, :].rearrange("p o d -> p (o d)"), start=(c == 0),
                                  stop=(c == 3))
                    last.then_inc(hDN.filled, 1)

            expert_tiles(pe, step)


STEP = [("A", 0), ("A", 1), ("o", 0), ("v", 3), ("k", 1), ("A", 2), ("A", 3), ("B", 0), ("x", 1), ("n", 1), ("B", 1),
        ("V", 0), ("o", 1), ("A", 4), ("A", 5), ("B", 2), ("V", 1), ("K", 0), ("A", 6), ("A", 7), ("P", 0), ("B", 3),
        ("X", 0), ("N", 0), ("V", 2), ("M", 0), ("E", 0)]


def kernel(**inputs):
    import numpy as np
    import concourse.bacc as bacc
    from concourse import mybir as mb
    from concourse.bass_utils import run_bass_kernel_spmd as run

    z = {k: np.asarray(v) for k, v in inputs.items()}
    feat = np.arange(D).reshape(H, DH).T.reshape(-1)
    partner = (np.arange(D).reshape(H, DH // 2, 2)[:, :, ::-1]).reshape(H, DH).T.reshape(-1)

    theta = (np.float32(1.0) / np.power(np.float32(10000.0), np.arange(0, DH, 2, dtype=np.float32) / np.float32(DH)))
    ang = np.arange(S, dtype=np.float32)[:, None] * theta.astype(np.float32)[None, :]
    cos = np.repeat(np.cos(ang).astype(np.float32).T, 2, axis=0)
    sin = np.repeat(np.sin(ang).astype(np.float32).T, 2, axis=0)
    sign = np.where(np.arange(DH) % 2 == 0, np.float32(-1), np.float32(1))[:, None]
    cos = np.repeat(cos, H, axis=0)
    sin = np.repeat(sin * sign, H, axis=0)

    a = {"x": z["x"], "ctx": z["ctx_1024"], "maskk": z["mask_Bx1xS2_if1"], "maskf": z["mask_Bx1xSxS2_if1"],
         "cos": cos, "sin": sin}
    L0 = lambda n: z["L0_attn_" + n]
    a.update(wz=L0("w_ln_z").T, wdt=L0("w_dt").T, wya=L0("w_yact").T, wy=L0("w_y").T, wfc=L0("w_fc").T,
             wfa=L0("w_fcact").T, wout=L0("w_out").T.reshape(4, 128, D).transpose(1, 0, 2))
    X0, A1, X1 = (lambda n: z["L0_xattn_" + n]), (lambda n: z["L1_attn_" + n]), (lambda n: z["L1_xattn_" + n])
    a.update(wq0=X0("Wq")[:, feat], wq0s=X0("Wq")[:, partner], wk0=X0("Wk")[:, feat], wk0s=X0("Wk")[:, partner],
             wv0=X0("Wv"), wo0=X0("Wo"), wq1=A1("Wq")[:, feat], wk1=A1("Wk")[:, feat], wv1=A1("Wv"), wo1=A1("Wo"),
             wq2=X1("Wq").T[:, feat], wk2=X1("Wk").T[:, feat], wv2=X1("Wv").T, wo2=X1("Wo").T)
    M0, M1 = (lambda n: z["L0_ffn_" + n]), (lambda n: z["L1_ffn_" + n])
    a.update(gate=np.concatenate([M0("shared_gate").T[None], M0("gate_w")]).transpose(1, 0, 2),
             up=np.concatenate([M0("shared_up").T[None], M0("up_w")]).transpose(1, 0, 2),
             down=np.concatenate([M0("shared_down").T[None], M0("down_w")]).reshape(E0 + 1, 2, 128, D)
             .transpose(2, 0, 1, 3),
             router=M0("router_w").T, waff=M1("waff").T, b1=M1("b1"), w1=M1("W1").transpose(1, 0, 2),
             w2=M1("W2").reshape(E1, 4, 128, D).transpose(2, 0, 1, 3),
             b1c=M1("b1").reshape(E1, 4, 128).transpose(2, 0, 1), b2r=M1("b2"))
    a.update(bv0=X0("bv"), bv1=A1("bv"), rbias=M0("routing_bias"), thr=M1("affinity_threshold").reshape(1))
    vec = {"b_z": L0("b_ln_z"), "b_dt": L0("b_dt"), "b_y": L0("b_y"), "b_ya": L0("b_yact"), "h0": L0("h0"),
           "g_sio": L0("g_sio"), "g_ffn": L0("g_ffn"), "b_out": L0("b_out"), "bq0": X0("bq")[feat],
           "bq0s": X0("bq")[partner], "bk0": X0("bk")[feat], "bk0s": X0("bk")[partner], "bo0": X0("bo"),
           "bq1": A1("bq")[feat], "bk1": A1("bk")[feat], "bo1": A1("bo"), "bo2": X1("bo")}
    for c in range(4):
        vec["b_fc%d" % c] = L0("b_fc")[c * 128:(c + 1) * 128]
        vec["b_fa%d" % c] = L0("b_fcact")[c * 128:(c + 1) * 128]
    a["cols"] = np.stack([vec[n] for n in COLS], axis=1)

    nc = bacc.Bacc("TRN2", target_bir_lowering=False, num_devices=1)
    arrays, aps = {}, {}
    for name, v in a.items():
        v = np.ascontiguousarray(v)
        arrays["in_" + name] = v
        aps[name] = nc.dram_tensor("in_" + name, v.shape, mb.dt.from_np(v.dtype), kind="ExternalInput").ap()
    aps["out"] = nc.dram_tensor("out_x", (B, S, D), mb.dt.float32, kind="ExternalOutput").ap()
    program(nc, aps)
    return run(nc, [arrays], core_ids=[0]).results[0]["out_x"]
```
